# Optimizing a Trainium2 kernel written in Bass

```python
import numpy as np
import jax
import jax.numpy as jnp

def _softmax(x, axis=-1):
    return jax.nn.softmax(x, axis=axis)

def _gelu(x):
    return jax.nn.gelu(x, approximate=True)

def _silu(x):
    return jax.nn.silu(x)

def _sigmoid(x):
    return jax.nn.sigmoid(x)

def _layernorm(x, axis=-1, eps=1e-05):
    m = jnp.mean(x, axis=axis, keepdims=True)
    v = jnp.var(x, axis=axis, keepdims=True)
    return (x - m) / jnp.sqrt(v + eps)

def _scatter_add(tgt, idx, src, axis=0):
    return tgt.at[idx].add(src)

def _segment_sum(src, seg, n):
    return jax.ops.segment_sum(src, seg, n)
kernel_name = 'mk_vit_tower_d1_tok_img256_r4_ecae91'

def setup_inputs(seed: int=0):
    np.random.seed(seed)
    _w = jnp.asarray

    def _rec_inputs():
        import jax
        import jax.numpy as jnp
        _rk = jax.random.key(seed)
        x = -0.000928989 + 1.00043 * jax.random.normal(jax.random.fold_in(_rk, 1), (32, 64, 64, 1), jnp.float32)
        return x
    x = _rec_inputs()

    def _L0_tok_setup():
        import jax, jax.numpy as jnp
        import numpy as np
        L = 4
        M1 = 12
        M2 = 12
        BN_EPS = 1e-05

        def _fourier_layer(v, W1, W2):
            B, C, Sx, Sy = v.shape
            x_ft = jnp.fft.rfft2(v)
            out1 = jnp.einsum('bixy,ioxy->boxy', x_ft[:, :, :M1, :M2], W1)
            out2 = jnp.einsum('bixy,ioxy->boxy', x_ft[:, :, -M1:, :M2], W2)
            out_ft = jnp.zeros((B, C, Sx, Sy // 2 + 1), jnp.complex64)
            out_ft = out_ft.at[:, :, :M1, :M2].set(out1)
            out_ft = out_ft.at[:, :, Sx - M1:, :M2].set(out2)
            return jnp.fft.irfft2(out_ft, s=(Sx, Sy))
        key = jax.random.key(seed)
        ks = jax.random.split(key, 10)
        B, S, d_a, d_v, d_u = (16, 64, 3, 32, 1)
        return {'x': jax.random.normal(ks[0], (B, S, S, 1), jnp.float32), 'p_w': jax.random.normal(ks[1], (d_a, d_v), jnp.float32) * 0.3, 'p_b': jax.random.normal(ks[2], (d_v,), jnp.float32) * 0.1, 'fw1': jax.random.normal(ks[3], (L, d_v, d_v, M1, M2, 2), jnp.float32) * (1.0 / d_v), 'fw2': jax.random.normal(ks[4], (L, d_v, d_v, M1, M2, 2), jnp.float32) * (1.0 / d_v), 'w_w': jax.random.normal(ks[5], (L, d_v, d_v), jnp.float32) * (1.0 / np.sqrt(d_v)), 'w_b': jax.random.normal(ks[6], (L, d_v), jnp.float32) * 0.1, 'bn_g': jnp.ones((L, d_v), jnp.float32), 'bn_b': jnp.zeros((L, d_v), jnp.float32), 'q_w': jax.random.normal(ks[7], (d_v, d_u), jnp.float32) * 0.3, 'q_b': jax.random.normal(ks[8], (d_u,), jnp.float32) * 0.1}
    _L0_tok_all = _L0_tok_setup()
    _L0_tok_in = {k: v for k, v in _L0_tok_all.items() if k in ('p_w', 'p_b', 'fw1', 'fw2', 'w_w', 'w_b', 'bn_g', 'bn_b', 'q_w', 'q_b')}
    del _L0_tok_all

    def _L0_attn_setup():
        import jax, jax.numpy as jnp
        import numpy as np
        MIDC = 64
        HEADS = 16
        HEADC = MIDC // HEADS
        EPS = 1e-05

        def _layernorm(x, w, b):
            mean = jnp.mean(x, axis=-1, keepdims=True)
            std = jnp.std(x, axis=-1, keepdims=True, ddof=1)
            return w * (x - mean) / (std + EPS) + b
        key = jax.random.key(seed)
        ks = jax.random.split(key, 3)
        B, HW = (8, 4096)
        x = jax.random.normal(ks[0], (B, HW, MIDC), dtype=jnp.float32)
        W_qkv = jax.random.normal(ks[1], (3 * MIDC, MIDC), dtype=jnp.float32) * 0.02
        b_qkv = jnp.zeros((3 * MIDC,), dtype=jnp.float32)
        kln_w = jnp.ones((HEADS, 1, HEADC), dtype=jnp.float32)
        kln_b = jnp.zeros((HEADS, 1, HEADC), dtype=jnp.float32)
        vln_w = jnp.ones((HEADS, 1, HEADC), dtype=jnp.float32)
        vln_b = jnp.zeros((HEADS, 1, HEADC), dtype=jnp.float32)
        W_proj = jax.random.normal(ks[2], (MIDC, MIDC), dtype=jnp.float32) * 0.02
        b_proj = jnp.zeros((MIDC,), dtype=jnp.float32)
        return {'x': x, 'W_qkv': W_qkv, 'b_qkv': b_qkv, 'kln_w': kln_w, 'kln_b': kln_b, 'vln_w': vln_w, 'vln_b': vln_b, 'W_proj': W_proj, 'b_proj': b_proj}
    _L0_attn_all = _L0_attn_setup()
    _L0_attn_in = {k: v for k, v in _L0_attn_all.items() if k in ('W_qkv', 'b_qkv', 'kln_w', 'kln_b', 'vln_w', 'vln_b', 'W_proj', 'b_proj')}
    del _L0_attn_all

    def _L0_ffn_setup():
        import jax, jax.numpy as jnp
        import numpy as np
        D_IN, D_HID, D_OUT = (64, 128, 64)
        N_EXPERTS, TOP_K = (64, 2)
        B, S = (8, 1024)
        key = jax.random.key(seed)
        ks = jax.random.split(key, 8)
        scale_in = 1.0 / np.sqrt(D_IN)
        scale_hid = 1.0 / np.sqrt(D_HID)
        return {'x': jax.random.normal(ks[0], (B, S, D_IN), dtype=jnp.float32), 'Wr': jax.random.uniform(ks[1], (D_IN, N_EXPERTS), jnp.float32, -scale_in, scale_in), 'br': jax.random.uniform(ks[2], (N_EXPERTS,), jnp.float32, -scale_in, scale_in), 'W1': jax.random.uniform(ks[3], (N_EXPERTS, D_IN, D_HID), jnp.float32, -scale_in, scale_in), 'b1': jax.random.uniform(ks[4], (N_EXPERTS, D_HID), jnp.float32, -scale_in, scale_in), 'W2': jax.random.uniform(ks[5], (N_EXPERTS, D_HID, D_OUT), jnp.float32, -scale_hid, scale_hid), 'b2': jax.random.uniform(ks[6], (N_EXPERTS, D_OUT), jnp.float32, -scale_hid, scale_hid)}
    _L0_ffn_all = _L0_ffn_setup()
    _L0_ffn_in = {k: v for k, v in _L0_ffn_all.items() if k in ('Wr', 'br', 'W1', 'b1', 'W2', 'b2')}
    del _L0_ffn_all
    return {'x': x, 'L0_tok_p_w': _L0_tok_in['p_w'], 'L0_tok_p_b': _L0_tok_in['p_b'], 'L0_tok_fw1': _L0_tok_in['fw1'], 'L0_tok_fw2': _L0_tok_in['fw2'], 'L0_tok_w_w': _L0_tok_in['w_w'], 'L0_tok_w_b': _L0_tok_in['w_b'], 'L0_tok_bn_g': _L0_tok_in['bn_g'], 'L0_tok_bn_b': _L0_tok_in['bn_b'], 'L0_tok_q_w': _L0_tok_in['q_w'], 'L0_tok_q_b': _L0_tok_in['q_b'], 'L0_attn_W_qkv': _L0_attn_in['W_qkv'], 'L0_attn_b_qkv': _L0_attn_in['b_qkv'], 'L0_attn_kln_w': _L0_attn_in['kln_w'], 'L0_attn_kln_b': _L0_attn_in['kln_b'], 'L0_attn_vln_w': _L0_attn_in['vln_w'], 'L0_attn_vln_b': _L0_attn_in['vln_b'], 'L0_attn_W_proj': _L0_attn_in['W_proj'], 'L0_attn_b_proj': _L0_attn_in['b_proj'], 'L0_ffn_Wr': _L0_ffn_in['Wr'], 'L0_ffn_br': _L0_ffn_in['br'], 'L0_ffn_W1': _L0_ffn_in['W1'], 'L0_ffn_b1': _L0_ffn_in['b1'], 'L0_ffn_W2': _L0_ffn_in['W2'], 'L0_ffn_b2': _L0_ffn_in['b2']}

def reference(x, L0_tok_p_w, L0_tok_p_b, L0_tok_fw1, L0_tok_fw2, L0_tok_w_w, L0_tok_w_b, L0_tok_bn_g, L0_tok_bn_b, L0_tok_q_w, L0_tok_q_b, L0_attn_W_qkv, L0_attn_b_qkv, L0_attn_kln_w, L0_attn_kln_b, L0_attn_vln_w, L0_attn_vln_b, L0_attn_W_proj, L0_attn_b_proj, L0_ffn_Wr, L0_ffn_br, L0_ffn_W1, L0_ffn_b1, L0_ffn_W2, L0_ffn_b2):
    import jax
    import jax.numpy as jnp

    def _L0_tok_ref(x, p_w, p_b, fw1, fw2, w_w, w_b, bn_g, bn_b, q_w, q_b):
        import jax, jax.numpy as jnp
        import numpy as np
        L = 4
        M1 = 12
        M2 = 12
        BN_EPS = 1e-05

        def _fourier_layer(v, W1, W2):
            B, C, Sx, Sy = v.shape
            x_ft = jnp.fft.rfft2(v)
            out1 = jnp.einsum('bixy,ioxy->boxy', x_ft[:, :, :M1, :M2], W1)
            out2 = jnp.einsum('bixy,ioxy->boxy', x_ft[:, :, -M1:, :M2], W2)
            out_ft = jnp.zeros((B, C, Sx, Sy // 2 + 1), jnp.complex64)
            out_ft = out_ft.at[:, :, :M1, :M2].set(out1)
            out_ft = out_ft.at[:, :, Sx - M1:, :M2].set(out2)
            return jnp.fft.irfft2(out_ft, s=(Sx, Sy))
        B, Sx, Sy, _ = x.shape
        gx = jnp.broadcast_to(jnp.linspace(0.0, 1.0, Sx, dtype=jnp.float32)[None, :, None, None], (B, Sx, Sy, 1))
        gy = jnp.broadcast_to(jnp.linspace(0.0, 1.0, Sy, dtype=jnp.float32)[None, None, :, None], (B, Sx, Sy, 1))
        h = jnp.concatenate([x, gx, gy], axis=-1)
        v = h @ p_w + p_b
        v = jnp.transpose(v, (0, 3, 1, 2))
        for i in range(L):
            W1 = fw1[i, ..., 0] + 1j * fw1[i, ..., 1]
            W2 = fw2[i, ..., 0] + 1j * fw2[i, ..., 1]
            x1 = _fourier_layer(v, W1, W2)
            x2 = jnp.einsum('bcxy,cd->bdxy', v, w_w[i]) + w_b[i][None, :, None, None]
            v = x1 + x2
            mean = jnp.mean(v, axis=(0, 2, 3), keepdims=True)
            var = jnp.var(v, axis=(0, 2, 3), keepdims=True)
            v = (v - mean) * jax.lax.rsqrt(var + BN_EPS)
            v = v * bn_g[i][None, :, None, None] + bn_b[i][None, :, None, None]
            if i < L - 1:
                v = jax.nn.relu(v)
        out = jnp.einsum('bcxy,cu->bxyu', v, q_w) + q_b
        return jnp.squeeze(out)

    def _L0_attn_ref(x, W_qkv, b_qkv, kln_w, kln_b, vln_w, vln_b, W_proj, b_proj):
        import jax, jax.numpy as jnp
        import numpy as np
        MIDC = 64
        HEADS = 16
        HEADC = MIDC // HEADS
        EPS = 1e-05

        def _layernorm(x, w, b):
            mean = jnp.mean(x, axis=-1, keepdims=True)
            std = jnp.std(x, axis=-1, keepdims=True, ddof=1)
            return w * (x - mean) / (std + EPS) + b
        B, HW, C = x.shape
        bias = x
        qkv = jnp.einsum('bnc,oc->bno', x, W_qkv) + b_qkv
        qkv = qkv.reshape(B, HW, HEADS, 3 * HEADC).transpose(0, 2, 1, 3)
        q, k, v = jnp.split(qkv, 3, axis=-1)
        k = _layernorm(k, kln_w, kln_b)
        v = _layernorm(v, vln_w, vln_b)
        kv = jnp.einsum('bhnd,bhne->bhde', k, v) / HW
        out = jnp.einsum('bhnd,bhde->bhne', q, kv)
        out = out.transpose(0, 2, 1, 3).reshape(B, HW, C)
        ret = out + bias
        proj = jnp.einsum('bnc,oc->bno', ret, W_proj) + b_proj
        return jax.nn.gelu(proj, approximate=False) + bias

    def _L0_ffn_ref(x, Wr, br, W1, b1, W2, b2):
        import jax, jax.numpy as jnp
        import numpy as np
        D_IN, D_HID, D_OUT = (64, 128, 64)
        N_EXPERTS, TOP_K = (64, 2)
        B, S = (8, 1024)
        Bx, Sx, D = x.shape
        xf = x.reshape(-1, D)
        T = xf.shape[0]
        E = Wr.shape[1]
        logits = xf @ Wr + br
        topk_logits, topk_idx = jax.lax.top_k(logits, TOP_K)
        gates = jax.nn.softmax(topk_logits, axis=1)
        combine = jnp.zeros((T, E), xf.dtype).at[jnp.arange(T)[:, None], topk_idx].add(gates)
        out = jnp.zeros((T, W2.shape[-1]), xf.dtype)
        for e in range(E):
            h = jax.nn.relu(xf @ W1[e] + b1[e])
            y = h @ W2[e] + b2[e]
            out = out + combine[:, e:e + 1] * y
        return out.reshape(Bx, Sx, -1)
    h = _L0_tok_ref(x, L0_tok_p_w, L0_tok_p_b, L0_tok_fw1, L0_tok_fw2, L0_tok_w_w, L0_tok_w_b, L0_tok_bn_g, L0_tok_bn_b, L0_tok_q_w, L0_tok_q_b)
    h = h + _L0_attn_ref(_layernorm(h, axis=-1), L0_attn_W_qkv, L0_attn_b_qkv, L0_attn_kln_w, L0_attn_kln_b, L0_attn_vln_w, L0_attn_vln_b, L0_attn_W_proj, L0_attn_b_proj)
    h = h + _L0_ffn_ref(_layernorm(h, axis=-1), L0_ffn_Wr, L0_ffn_br, L0_ffn_W1, L0_ffn_b1, L0_ffn_W2, L0_ffn_b2)
    return h

_drawn_inputs = setup_inputs


def setup_inputs(seed=0):
    import zlib

    import numpy as np

    out = dict(_drawn_inputs(seed))
    spreads = {'L0_tok_bn_g': (1.0, 0.2),
     'L0_tok_bn_b': (0.0, 0.1),
     'L0_attn_b_qkv': (0.0, 0.8),
     'L0_attn_kln_w': (1.0, 0.6),
     'L0_attn_kln_b': (0.0, 0.8),
     'L0_attn_vln_w': (1.0, 0.6),
     'L0_attn_vln_b': (0.0, 0.8),
     'L0_attn_b_proj': (0.0, 0.296)}
    factors = {'L0_tok_p_b': 8.0,
     'L0_tok_w_b': 8.0,
     'L0_attn_W_qkv': 8.0,
     'L0_ffn_b1': 6.891,
     'L0_ffn_b2': 3.848}
    for name, (base, spread) in spreads.items():
        noise = np.random.default_rng([zlib.crc32(name.encode()), seed]).standard_normal(out[name].shape)
        drawn = base * np.exp(spread * noise) if base else spread * noise
        out[name] = jnp.asarray(drawn.astype(out[name].dtype))
    for name, factor in factors.items():
        out[name] = (out[name] * factor).astype(out[name].dtype)
    return out
```

```python
import concourse.bass as bass
from concourse import mybir
from contextlib import ExitStack
import numpy as np

B, S, CH, LAYERS = 32, 64, 32, 4
QG, JN = 4, 8
KX, KY = 24, 12
KG = KX // QG
GM = KG * KY * 2
NPIX = S * S
CW = 512
NC = NPIX // CW
YF = KY * 2
XB = 4
MK = 6
MSTEPS = KG * KY // MK
EPS = 1e-5
PCOLS = 128 + 3


def constants():
    f = np.float64
    two_pi = 2 * np.pi / S
    y, ky = np.arange(S, dtype=f), np.arange(KY, dtype=f)
    kx = np.array(list(range(12)) + list(range(52, 64)), dtype=f)
    cy, sy = np.cos(two_pi * np.outer(y, ky)), np.sin(two_pi * np.outer(y, ky))
    cx, sx = np.cos(two_pi * np.outer(y, kx)), np.sin(two_pi * np.outer(y, kx))
    fy = np.zeros((2, S, 2, KY, 2), f)
    for a in range(2):
        fy[a, :, a, :, 0], fy[a, :, a, :, 1] = cy, -sy
    fx = np.zeros((2, S, KX, 2), f)
    fx[0, :, :, 0], fx[1, :, :, 0] = cx, sx
    fx[0, :, :, 1], fx[1, :, :, 1] = -sx, cx
    tx = np.zeros((KX, 2, 2, S, 2, 2), f)
    for a in range(2):
        tx[:, a, 0, :, a, 0], tx[:, a, 1, :, a, 0] = cx.T / S, -sx.T / S
        tx[:, a, 0, :, a, 1], tx[:, a, 1, :, a, 1] = sx.T / S, cx.T / S
    wk = np.where(ky == 0, 1.0, 2.0)[:, None] / S
    ty = np.zeros((XB, KY, 2, XB, S), f)
    for a in range(XB):
        ty[a, :, 0, a], ty[a, :, 1, a] = wk * cy.T, -wk * sy.T
    avg = np.kron(np.full((QG, QG), 1.0 / QG), np.eye(CH))
    lin = np.linspace(0.0, 1.0, S, dtype=np.float32)
    grid = np.stack([np.repeat(lin, S), np.tile(lin, S), np.ones(NPIX, np.float32)])
    mask = np.kron(np.eye(16), np.ones((4, 4))) / S
    iota = np.tile(np.arange(64), (128, 1))
    out = dict(fy=fy.reshape(128, 48), fx=fx.reshape(128, 48), tx=tx.reshape(96, 256), ty=ty.reshape(96, 256),
               ident=np.eye(128), avg=avg, grid=grid, mask=mask, iota=iota)
    return {k: np.ascontiguousarray(v.astype(np.float32)) for k, v in out.items()}


def vit_tower(nc, x, p_w, p_b, fw1, fw2, w_w, w_b, bn_g, bn_b, q_w, q_b, W_qkv, b_qkv, kln_w, kln_b, vln_w, vln_b,
              W_proj, b_proj, Wr, br, W1, b1, W2, b2, c_fy, c_fx, c_tx, c_ty, c_ident, c_avg, c_grid, c_mask, c_iota,
              out):
    fp32 = mybir.dt.float32
    ALU = mybir.AluOpType
    ACT = mybir.ActivationFunctionType
    ctx = ExitStack()
    with ctx:
        def sb(name, shape, dt=fp32):
            return ctx.enter_context(nc.sbuf_tensor(name, shape, dt))

        def sem(name):
            return ctx.enter_context(nc.semaphore(name))

        big = sb("big", [128, JN, NPIX])
        modes = sb("modes", [128, B * GM])
        wmode = sb("wmode", [128, CH, GM])
        work = sb("work", [128, 8832])
        xmode = modes[:, :].rearrange("p (b f) -> p b f", b=B)
        z1t = modes[0:96, 0:2048].rearrange("p (s n) -> p s n", s=4)
        vch = work[:, 0:2048].rearrange("p (s n) -> p s n", s=4)
        vt = work[:, 2048:4096].rearrange("p (s n) -> p s n", s=4)
        cy_ = work[:, 4096:5632]
        dx_ = work[:, 5632:7168]
        xj = work[:, 7168:7744]
        xin = work[0:7, 0:4096].rearrange("p (s n) -> p s n", s=2)
        ymode = work[:, 0:4608].rearrange("p (b f) -> p b f", b=B)
        wring = work[:, 4608:7680].rearrange("p (s m c) -> p s m c", s=2, c=128)
        xring = work[:, 7680:8832].rearrange("p (s m t b) -> p s m t b", s=2, m=MK, t=3)
        z1 = work[:, 4608:6144]
        yq = work[:, 6144:6720]
        yp = work[:, 7488:8064]
        yt = work[0:96, 6720:7488]
        ht = work[:, 2048:3072]

        flat = big[:, :, :].rearrange("p j n -> p (j n)")
        pos = [0]

        def tail(n, rows=128):
            pos[0] += n
            return flat[0:rows, pos[0] - n:pos[0]]

        TT = 16
        res = tail(1024)
        xn, xc, sq = tail(1024), tail(2048), tail(2048)
        red, red2, red3 = tail(512), tail(512), tail(512)
        kv = tail(2048)
        xt, rt = tail(2048, 65), tail(2048, 65)
        qt, kvm, ct = tail(2048, 64), tail(2048, 64), tail(2048, 64)
        gl, lg, comb, eq = tail(1024), tail(1024), tail(1024), tail(1024)
        mx, ixf, gate = tail(128), tail(128), tail(64)
        acc = tail(1024)
        hid = tail(4096).rearrange("p (s n) -> p s n", s=8)
        gated = tail(2048).rearrange("p (s n) -> p s n", s=4)
        assert pos[0] <= JN * NPIX
        wpos = [0]

        def tailw(n, rows):
            wpos[0] += n
            return modes[0:rows, wpos[0] - n:wpos[0]]

        wqkv, wproj, wroute = tailw(192, 65), tailw(64, 65), tailw(64, 65)
        b2all, mask, iota, lnwb = tailw(64, 64), tailw(64, 64), tailw(64, 128), tailw(256, 128)
        wflat = wmode[:, :, :].rearrange("p o f -> p (o f)")
        w1r = wflat[0:65, 0:512].rearrange("p (s e n) -> p s e n", s=2, e=2)
        w2r = wflat[:, 512:768].rearrange("p (s e n) -> p s e n", s=2, e=2)
        ixs = sb("ixs", [128, 128], mybir.dt.uint32)

        fy, fx = sb("fy", [128, 48]), sb("fx", [128, 48])
        tx, ty = sb("tx", [96, 256]), sb("ty", [96, 256])
        ident, avg = sb("ident", [128, 128]), sb("avg", [128, 128])
        lift = sb("lift", [7, 128])
        params = sb("params", [128, LAYERS, PCOLS])
        cur = sb("cur", [128, PCOLS])
        stats = sb("stats", [128, JN * NC, 6])
        bn = sb("bn", [128, 16])
        qcol = sb("qcol", [128, 4])
        qb = sb("qb", [128, 1])

        banks = [ctx.enter_context(nc.psum_tensor(f"bank{i}", [128, 512], fp32)) for i in range(8)]
        PA, PB, PC, PD = banks[0:2], banks[2:4], banks[4:6], banks[6:8]

        consts_in = sem("consts_in")
        zeroed = sem("zeroed")
        a_full, b_full, c_full, d_full = sem("a_full"), sem("b_full"), sem("c_full"), sem("d_full")
        a_free, b_free, c_free, d_free = sem("a_free"), sem("b_free"), sem("c_free"), sem("d_free")
        xin_in, xin_free = [sem("xin_in0"), sem("xin_in1")], sem("xin_free")
        v_ready, v_copied = sem("v_ready"), sem("v_copied")
        v_free = sem("v_free")
        x_sent = sem("x_sent")
        w_in, w_used = sem("w_in"), sem("w_used")
        cur_ready = sem("cur_ready")
        ring_clear = sem("ring_clear")
        exp_dve, exp_act, exp_pool = sem("exp_dve"), sem("exp_act"), sem("exp_pool")
        y_done = sem("y_done")
        yq_in, yp_ready = sem("yq_in"), sem("yp_ready")
        stat_done = sem("stat_done")
        bn_chain, bn_mm, bn_sq, bn_done = sem("bn_chain"), sem("bn_mm"), sem("bn_sq"), sem("bn_done")
        pool_past, dve_past = sem("pool_past"), sem("dve_past")
        out_sent = sem("out_sent")
        tail_in, ones_set, tail_chain = sem("tail_in"), sem("ones_set"), sem("tail_chain")
        h_full, xn_ready, xt_full, xt_ready = sem("h_full"), sem("xn_ready"), sem("xt_full"), sem("xt_ready")
        var_ready, std_ready = sem("var_ready"), sem("std_ready")
        kv_full, q_full, qt_ready, kv_taken, kv_ready = (sem("kv_full"), sem("q_full"), sem("qt_ready"),
                                                         sem("kv_taken"), sem("kv_ready"))
        kvm_full, kvm_ready, att_full, rt_ready = sem("kvm_full"), sem("kvm_ready"), sem("att_full"), sem("rt_ready")
        proj_full, gelu_ready, lg_full, lg_taken = sem("proj_full"), sem("gelu_ready"), sem("lg_full"), sem("lg_taken")
        dif_ready, exp_ready, comb_ready = sem("dif_ready"), sem("exp_ready"), sem("comb_ready")
        ct_full, ct_ready, bias_full, acc_ready = sem("ct_full"), sem("ct_ready"), sem("bias_full"), sem("acc_ready")
        e_in = [sem("e_in0"), sem("e_in1")]
        hid_full, hid_ready, hid_used = sem("hid_full"), sem("hid_ready"), sem("hid_used")
        y_taken, acc_done = sem("y_taken"), sem("acc_done")

        AF, AM, AI = 64, MSTEPS, 32
        BF, BI = 64, 32
        CF, CI = 32, 48
        DF, DI = 16, 48
        AL, BL, CL, DL = AF + AM + AI, BF + BI, CF + CI, DF + DI
        B0 = 64
        EXPERTS = 64
        NCONST = 16 * (6 + 4 * 4 + 3 * 4 + 4 + 3 + 4 + 1)
        V0H = 2 * JN

        block = ctx.enter_context(nc.Block())

        @block.sync
        def _(sp):
            for dst, src in ((fy, c_fy), (fx, c_fx), (tx, c_tx), (ty, c_ty), (ident, c_ident), (avg, c_avg)):
                sp.dma_start(dst[:, :], src).then_inc(consts_in, 16)
            sp.wait_ge(zeroed, 3)
            for q in range(QG):
                r = slice(q * CH, (q + 1) * CH)
                for l in range(LAYERS):
                    sp.dma_start(params[r, l, r], w_w[l]).then_inc(consts_in, 16)
                for n, src in enumerate((w_b, bn_g, bn_b)):
                    sp.dma_start(params[r, :, 128 + n:129 + n], src.rearrange("l (c o) -> c l o", o=1),
                                 allow_slow_non_contiguous=True).then_inc(consts_in, 16)
                sp.dma_start(lift[q:q + 1, r], p_w[0:1, :]).then_inc(consts_in, 16)
                sp.dma_start(qcol[r, q:q + 1], q_w).then_inc(consts_in, 16)
            for n, src in enumerate((p_w[1:2, :], p_w[2:3, :], p_b.rearrange("(a c) -> a c", a=1))):
                sp.dma_start(lift[4 + n:5 + n, :].rearrange("a (q c) -> a q c", q=QG),
                             src.rearrange("a (u c) -> a u c", u=1).broadcast_to([1, QG, CH])).then_inc(consts_in, 16)
            sp.dma_start(qb[:, :], q_b.rearrange("(a c) -> a c", a=1).broadcast_to([128, 1])).then_inc(consts_in, 16)

            xv = x.rearrange("(q j) (h r) y o -> j h q (r y o)", q=QG, h=2)
            gv = c_grid.rearrange("p (h n) -> h p n", h=2)
            with sp.Fori(0, JN) as j:
                for h in range(2):
                    sp.wait_ge(xin_free, j * 2 + h + 1)
                    sp.dma_start(xin[0:4, h, :], xv[j, h]).then_inc(xin_in[h], 16)
                    sp.dma_start(xin[4:7, h, :], gv[h]).then_inc(xin_in[h], 16)

            def load_weights(l):
                for g in range(QG):
                    fw = (fw1, fw2)[g // 2]
                    k0 = (g % 2) * GM
                    sp.dma_start(wmode[g * CH:(g + 1) * CH, :, :], fw[l, :, :, k0:k0 + GM]).then_inc(w_in, 16)

            def send_spectra(l):
                with sp.Fori(0, JN) as j:
                    sp.wait_ge(d_free, l * DL + j * 2 + 4)
                    for q in range(QG):
                        for g in range(QG):
                            sp.dma_start(xmode[g * CH:(g + 1) * CH, q * JN + j, :],
                                         xj[q * CH:(q + 1) * CH, g * GM:(g + 1) * GM]).then_inc(x_sent, 16)

            def fetch_mixed(l, j):
                for q in range(QG):
                    for g in range(QG):
                        sp.dma_start(yq[q * CH:(q + 1) * CH, g * GM:(g + 1) * GM],
                                     ymode[g * CH:(g + 1) * CH, q * JN + j, :]).then_inc(yq_in, 16)

            load_weights(0)
            send_spectra(0)

            def rest_of_layer(l):
                sp.wait_ge(a_free, l * AL + AF + AM + 2)
                fetch_mixed(l, 0)
                with sp.Fori(0, JN - 1) as j:
                    sp.wait_ge(yp_ready, l * JN + j + 1)
                    fetch_mixed(l, j + 1)

            with sp.Fori(0, LAYERS - 1) as l:
                rest_of_layer(l)
                sp.wait_ge(w_used, l * 3 + 3)
                load_weights(l + 1)
                send_spectra(l + 1)
            rest_of_layer(LAYERS - 1)
            sp.wait_ge(bn_done, LAYERS)
            for dst, src in ((wqkv[0:64, :], W_qkv), (wqkv[64:65, :], b_qkv.rearrange("(a n) -> a n", a=1)),
                             (wproj[0:64, :], W_proj), (wproj[64:65, :], b_proj.rearrange("(a n) -> a n", a=1)),
                             (wroute[0:64, :], Wr), (wroute[64:65, :], br.rearrange("(a n) -> a n", a=1)),
                             (b2all, b2), (mask, c_mask), (iota, c_iota)):
                sp.dma_start(dst, src).then_inc(tail_in, 16)
            for n, src in enumerate((kln_w, vln_w, kln_b, vln_b)):
                sp.dma_start(lnwb[:, n * 64:(n + 1) * 64],
                             src.rearrange("h (a o) d -> a (h o d)", a=1).broadcast_to([128, 64])).then_inc(tail_in, 16)
            with sp.Fori(0, EXPERTS // 4) as i:
                for s in range(2):
                    sp.wait_ge(hid_used, (i * 2 + s) * 8)
                    e = bass.ds(i * 4 + s * 2, 2)
                    sp.dma_start(w1r[0:64, s, :, :], W1[e, :, :].rearrange("e d h -> d e h")).then_inc(e_in[s], 16)
                    sp.dma_start(w1r[64:65, s, :, :], b1[e, :].rearrange("e (a h) -> a e h", a=1)).then_inc(e_in[s], 16)
                    sp.dma_start(w2r[:, s, :, :], W2[e, :, :].rearrange("e h d -> h e d")).then_inc(e_in[s], 16)
            sp.wait_ge(acc_done, 2 * EXPERTS + 4)
            for q in range(QG):
                sp.dma_start(out[q * JN:(q + 1) * JN].rearrange("j (xp x) y -> xp j (x y)", x=2),
                             acc[q * 32:(q + 1) * 32, :].rearrange("p (j n) -> p j n", j=JN)).then_inc(out_sent, 16)
            sp.wait_ge(out_sent, 64)

        @block.gpsimd
        def _(pool):
            pool.memset(params[:, :, :], 0.0).then_inc(zeroed, 1)
            pool.memset(lift[:, :], 0.0).then_inc(zeroed, 1)
            pool.memset(qcol[:, :], 0.0).then_inc(zeroed, 1)

            def mixing(l):
                pool.wait_ge(x_sent, (l * JN + JN) * 256)
                pool.sem_inc(pool_past, 1)
                pool.memset(work[:, 4608:7680], 0.0).then_inc(ring_clear, 1)
                pool.wait_ge(ring_clear, l + 1)
                pool.wait_ge(w_in, (l + 1) * 64)
                pool.sem_inc(pool_past, 1)
                with pool.Fori(0, KG) as k:
                    for h in range(2):
                        pool.wait_ge(a_full, l * AL + AF + k * 2 + h - 1)
                        pool.sem_inc(pool_past, 1)
                        for g in (2, 3):
                            r = slice(g * CH, (g + 1) * CH)
                            src = wmode[r, :, bass.ds(k * YF + h * 12, 12)].rearrange("p o m -> p m o")
                            pool.tensor_copy(wring[r, h, :, r], src).then_inc(exp_pool, 1)
                pool.wait_ge(exp_pool, (l * MSTEPS + MSTEPS) * 2)
                pool.sem_inc(w_used, 1)

            def regroup(l):
                with pool.Fori(0, JN) as j:
                    pool.wait_ge(yq_in, (l * JN + j + 1) * 256)
                    pool.wait_ge(d_full, l * DL + DF + j * 6 - 4)
                    pool.sem_inc(pool_past, 1)
                    pool.tensor_copy(yp.rearrange("p (y k f) -> p k y f", y=KY // 2, k=KX),
                                     yq.rearrange("p (k y f) -> p k y f", k=KX, y=KY // 2)).then_inc(yp_ready, 1)

            def keep_chunks(l):
                with pool.Fori(0, JN) as j:
                    for c in range(NC):
                        pool.wait_ge(v_ready, (l * JN + j) * NC + c + 1)
                        pool.sem_inc(pool_past, 1)
                        pool.tensor_copy(big[:, j, c * CW:(c + 1) * CW], vch[:, c % 4, :]).then_inc(v_copied, 1)

            with pool.Fori(0, LAYERS - 1) as l:
                mixing(l)
                regroup(l)
                keep_chunks(l + 1)
            mixing(LAYERS - 1)
            regroup(LAYERS - 1)
            pool.wait_ge(b_free, B0 + LAYERS * BL + JN * 2 + 2)
            pool.memset(xt[64:65, :], 1.0).then_inc(ones_set, 1)
            pool.memset(rt[64:65, :], 1.0).then_inc(ones_set, 1)
            pool.wait_ge(acc_ready, 1)
            with pool.Fori(0, EXPERTS // 2) as i:
                for e in range(2):
                    for half in range(2):
                        n = e * 2 + half
                        pool.wait_ge(y_taken, i * 4 + n + 5)
                        pool.wait_ge(acc_done, i * 4 + n + 3)
                        pool.sem_inc(pool_past, 1)
                        a = acc[:, half * 512:(half + 1) * 512]
                        pool.tensor_tensor(a, a, gated[:, n, :], ALU.add).then_inc(acc_done, 1)

        @block.scalar
        def _(act):
            act.wait_ge(consts_in, NCONST)

            def forward(l, first):
                def apply(j, c):
                    act.wait_ge(v_free, (l * JN + j) * NC + c + 1)
                    if not first:
                        act.wait_ge(v_copied, ((l - 1) * JN + j) * NC + c + 1)
                    src = big[:, j, c * CW:(c + 1) * CW]
                    if first:
                        act.activation(vch[:, c % 4, :], src, ACT.Copy).then_inc(v_ready, 1)
                    else:
                        act.activation(vch[:, c % 4, :], src, ACT.Relu, bias=bn[:, 9:10],
                                       scale=bn[:, 8:9]).then_inc(v_ready, 1)

                def cy_out(j, c):
                    act.wait_ge(b_full, B0 + l * BL + j * NC + c + 1)
                    act.activation(cy_.rearrange("p (f x) -> p f x", f=YF)[:, :, c * 8:(c + 1) * 8],
                                   PB[c % 2][:, 0:192].rearrange("p (x f) -> p f x", x=8), ACT.Copy).then_inc(b_free, 1)

                def x_out(j, h):
                    act.wait_ge(d_full, l * DL + j * 2 + h + 1)
                    dst = xj.rearrange("p (k y r) -> p y k r", k=KX, y=KY)[:, h * 6:h * 6 + 6]
                    act.activation(dst, PD[h][:, 0:288].rearrange("p (y k r) -> p y k r", y=6, k=KX),
                                   ACT.Copy).then_inc(d_free, 1)

                def group(j, last):
                    for c in range(NC):
                        if c < NC - 3:
                            apply(j, c + 3)
                        elif not last:
                            apply(j + 1, c - (NC - 3))
                        if c == 0:
                            act.wait_ge(c_free, l * CL + j * 4 + 2)
                        cy_out(j, c)
                    act.wait_ge(x_sent, (l * JN + j) * 256)
                    x_out(j, 0)
                    x_out(j, 1)

                for c in range(3):
                    apply(0, c)
                with act.Fori(0, JN - 1) as j:
                    group(j, False)
                group(JN - 1, True)

            def mixing(l):
                act.wait_ge(x_sent, (l * JN + JN) * 256)

                def xs(k, h):
                    act.wait_ge(a_full, l * AL + AF + k * 2 + h - 1)
                    src = xmode[:, :, bass.ds(k * YF + h * 12, 12)].rearrange("p b (m r) -> p m r b", r=2)
                    act.activation(xring[:, h, :, 0, :], src[:, :, 1, :], ACT.Copy, scale=-1.0).then_inc(exp_act, 1)
                    act.activation(xring[:, h, :, 1, :], src[:, :, 0, :], ACT.Copy).then_inc(exp_act, 1)
                    act.activation(xring[:, h, :, 2, :], src[:, :, 1, :], ACT.Copy).then_inc(exp_act, 1)

                def y_out(k, h):
                    act.wait_ge(a_full, l * AL + AF + k * 2 + h + 1)
                    dst = ymode[:, :, bass.ds(k * YF + h * 12, 12)].rearrange("p b m -> p m b")
                    act.activation(dst, PA[h][:, 0:384].rearrange("p (m b) -> p m b", b=B), ACT.Copy).then_inc(a_free, 1)

                xs(0, 0)
                with act.Fori(0, KG - 1) as k:
                    xs(k, 1)
                    y_out(k, 0)
                    xs(k + 1, 0)
                    y_out(k, 1)
                xs(KG - 1, 1)
                y_out(KG - 1, 0)
                y_out(KG - 1, 1)

            def inverse(l):
                def z1_out(j, p):
                    if p == 0:
                        act.wait_ge(d_full, l * DL + DF + j * 6)
                    act.wait_ge(c_full, l * CL + CF + j * 6 + p + 1)
                    dst = z1.rearrange("p (x f) -> p x f", f=YF)[:, :, p * 4:p * 4 + 4]
                    act.activation(dst, PC[p % 2][:, 0:256].rearrange("p (x f) -> p x f", f=4),
                                   ACT.Copy).then_inc(c_free, 1)

                def u_out(j, c):
                    full, free, P, base = ((a_full, a_free, PA, l * AL + AF + AM), (b_full, b_free, PB, B0 + l * BL + BF))[c % 2]
                    act.wait_ge(full, base + j * 4 + c // 2 + 1)
                    act.activation(big[:, j, c * CW:(c + 1) * CW], P[(c // 2) % 2][:, :], ACT.Identity,
                                   bias=cur[:, 128:129]).then_inc(free, 1)

                for p in range(6):
                    z1_out(0, p)

                def group(j, last):
                    for c in range(NC):
                        u_out(j, c)
                        if c >= 4 and c < 7 and not last:
                            z1_out(j + 1, 2 * (c - 4))
                            z1_out(j + 1, 2 * (c - 4) + 1)
                with act.Fori(0, JN - 1) as j:
                    group(j, False)
                group(JN - 1, True)

            def norm(l):
                act.wait_ge(bn_sq, 2 * l + 1)
                act.activation(bn[:, 5:6], bn[:, 4:5], ACT.Sqrt).then_inc(bn_sq, 1)

            with act.Fori(0, JN) as j:
                for c in range(NC):
                    act.wait_ge(b_full, j * NC + c + 1)
                    act.activation(big[:, j, c * CW:(c + 1) * CW], PB[c % 2][:, :], ACT.Copy).then_inc(b_free, 1)
            act.wait_ge(b_free, B0 + 2)
            forward(0, True)
            with act.Fori(0, LAYERS - 1) as l:
                mixing(l)
                act.wait_ge(cur_ready, l + 1)
                inverse(l)
                norm(l)
                act.wait_ge(bn_done, l + 1)
                forward(l + 1, False)
            mixing(LAYERS - 1)
            act.wait_ge(cur_ready, LAYERS)
            inverse(LAYERS - 1)
            norm(LAYERS - 1)
            act.wait_ge(bn_done, LAYERS)
            n0 = LAYERS * JN * NC
            with act.Fori(0, JN) as j:
                for c in range(NC):
                    act.wait_ge(v_free, j * NC + n0 + c + 1)
                    act.activation(vch[:, c % 4, :], big[:, j, c * CW:(c + 1) * CW], ACT.Identity, bias=bn[:, 9:10],
                                   scale=bn[:, 8:9]).then_inc(v_ready, 1)

            def deviation(n, scale, bias):
                act.wait_ge(var_ready, n)
                act.activation(red3[:, 0:bias], red2[:, 0:bias], ACT.Sqrt, scale=scale).then_inc(std_ready, 1)

            def xt_out(n):
                for b in range(4):
                    act.wait_ge(xt_full, n * 4 + b + 1)
                    act.activation(xt[0:64, b * 512:(b + 1) * 512], (PB + PC)[b][0:64, :], ACT.Copy).then_inc(xt_ready, 1)

            deviation(1, 1.0, TT)
            xt_out(0)
            for b in range(4):
                act.wait_ge(q_full, b + 1)
                act.activation(qt[:, b * 512:(b + 1) * 512], (PC + PD)[b][0:64, :], ACT.Copy).then_inc(qt_ready, 1)
            deviation(2, 1.0 / 3, 512)
            for b in range(2):
                act.wait_ge(proj_full, b + 1)
                act.activation(gl[:, b * 512:(b + 1) * 512], PA[b][:, :], ACT.Gelu).then_inc(gelu_ready, 1)
            deviation(3, 1.0, TT)
            xt_out(1)
            act.wait_ge(dif_ready, 1)
            act.activation(gate[:, 16:32], gate[:, 0:16], ACT.Exp).then_inc(exp_ready, 1)
            with act.Fori(0, EXPERTS // 2) as i:
                for n in range(8):
                    act.wait_ge(hid_used, i * 8 + n + 1)
                    act.wait_ge(hid_full, i * 8 + n + 1)
                    act.activation(hid[:, n, :], (PA + PB)[n % 4][:, :], ACT.Relu).then_inc(hid_ready, 1)

        @block.vector
        def _(dve):
            for s, n in ((a_free, 2), (b_free, 2), (c_free, 2), (d_free, 2), (v_free, 4), (xin_free, 2), (v_copied, 4),
                         (hid_used, 8), (hid_ready, 4), (y_taken, 4), (acc_done, 4)):
                dve.sem_inc(s, n)

            def forward(l):
                with dve.Fori(0, JN) as j:
                    for c in range(NC):
                        dve.wait_ge(a_full, l * AL + j * NC + c + 1)
                        dve.wait_ge(b_full, l * BL + j * NC + c + B0 - 3)
                        dve.tensor_copy(vt[:, c % 4, :], PA[c % 2][:, :]).then_inc(a_free, 1)
                    dve.wait_ge(d_full, l * DL + j * 2)
                    for n in range(4):
                        dve.wait_ge(c_full, l * CL + j * 4 + n + 1)
                        dve.tensor_copy(dx_[:, n * 384:(n + 1) * 384], PC[n % 2][:, 0:384]).then_inc(c_free, 1)

            def mixing(l):
                dve.wait_ge(ring_clear, l + 1)
                dve.wait_ge(w_in, (l + 1) * 64)
                dve.tensor_copy(cur[:, :], params[:, l, :]).then_inc(cur_ready, 1)
                with dve.Fori(0, KG) as k:
                    for h in range(2):
                        dve.wait_ge(a_full, l * AL + AF + k * 2 + h - 1)
                        for g in (0, 1):
                            r = slice(g * CH, (g + 1) * CH)
                            src = wmode[r, :, bass.ds(k * YF + h * 12, 12)].rearrange("p o m -> p m o")
                            dve.tensor_copy(wring[r, h, :, r], src).then_inc(exp_dve, 1)
                dve.wait_ge(exp_dve, (l * MSTEPS + MSTEPS) * 2)
                dve.sem_inc(w_used, 2)

            def inverse(l):
                def yt_out(j, n):
                    if n == 0:
                        dve.wait_ge(c_full, l * CL + CF + j * 6)
                    dve.wait_ge(d_full, l * DL + DF + j * 6 + n + 1)
                    dve.tensor_copy(yt[:, n * 384:(n + 1) * 384], PD[n][0:96, 0:384]).then_inc(d_free, 1)

                def z1t_out(j, s):
                    dve.wait_ge(d_full, l * DL + DF + j * 6 + 2 + s + 1)
                    dve.tensor_copy(z1t[:, s, :], PD[s % 2][0:96, :]).then_inc(d_free, 1)

                def take(j, c):
                    free, base = ((a_free, l * AL + AF + AM), (b_free, B0 + l * BL + BF))[c % 2]
                    dve.wait_ge(free, base + j * 4 + c // 2 + 3)
                    dve.bn_stats(stats[:, bass.ds(j * NC + c, 1), :],
                                 big[:, j, c * CW:(c + 1) * CW]).then_inc(stat_done, 1)

                yt_out(0, 0)
                yt_out(0, 1)

                def group(j, last):
                    z1t_out(j, 0)
                    z1t_out(j, 1)
                    take(j, 0)
                    z1t_out(j, 2)
                    take(j, 1)
                    z1t_out(j, 3)
                    take(j, 2)
                    if not last:
                        yt_out(j + 1, 0)
                    take(j, 3)
                    if not last:
                        yt_out(j + 1, 1)
                    for c in range(4, NC):
                        take(j, c)
                with dve.Fori(0, JN - 1) as j:
                    group(j, False)
                group(JN - 1, True)

            def norm(l):
                n = [0]

                def step(ins):
                    n[0] += 1
                    ins.then_inc(bn_chain, 1)
                    dve.wait_ge(bn_chain, l * 8 + n[0])
                dve.wait_ge(stat_done, (l + 1) * JN * NC)
                dve.sem_inc(dve_past, 1)
                dve.bn_aggr(bn[:, 0:2], stats[:, :, :]).then_inc(bn_mm, 1)
                dve.wait_ge(bn_mm, l * 4 + 2)
                step(dve.tensor_copy(bn[:, 2:3], PD[0][:, 0:1]))
                step(dve.tensor_tensor(bn[:, 3:4], bn[:, 0:1], bn[:, 2:3], ALU.subtract))
                step(dve.tensor_tensor(bn[:, 3:4], bn[:, 3:4], bn[:, 3:4], ALU.mult))
                dve.tensor_tensor(bn[:, 3:4], bn[:, 3:4], bn[:, 1:2], ALU.add).then_inc(bn_mm, 1)
                dve.wait_ge(bn_mm, l * 4 + 4)
                dve.tensor_scalar(bn[:, 4:5], PD[0][:, 1:2], EPS, None, ALU.add).then_inc(bn_sq, 1)
                dve.wait_ge(bn_sq, 2 * l + 2)
                step(dve.reciprocal(bn[:, 6:7], bn[:, 5:6]))
                step(dve.tensor_tensor(bn[:, 8:9], bn[:, 6:7], cur[:, 129:130], ALU.mult))
                step(dve.tensor_tensor(bn[:, 7:8], bn[:, 2:3], bn[:, 8:9], ALU.mult))
                step(dve.tensor_tensor(bn[:, 9:10], cur[:, 130:131], bn[:, 7:8], ALU.subtract))
                step(dve.tensor_copy(bn[:, 10:11], bn[:, 9:10]))
                dve.sem_inc(bn_done, 1)

            dve.wait_ge(consts_in, NCONST)
            forward(0)
            with dve.Fori(0, LAYERS - 1) as l:
                mixing(l)
                inverse(l)
                norm(l)
                forward(l + 1)
            mixing(LAYERS - 1)
            inverse(LAYERS - 1)
            norm(LAYERS - 1)
            ht4 = ht.rearrange("p (j q x) -> p j x q", j=JN, q=QG)
            b0 = B0 + LAYERS * BL
            with dve.Fori(0, JN) as j:
                for h in range(2):
                    dve.wait_ge(v_free, j * NC + LAYERS * JN * NC + h * 4 + 8)
                    dve.tensor_scalar(ht4[:, j, h * 16:(h + 1) * 16, :],
                                      PB[h][:, 0:64].rearrange("p (x q) -> p x q", q=QG), qb[:, 0:1], None,
                                      ALU.add).then_inc(b_free, 1)

            n = [0]

            def step(ins):
                n[0] += 1
                ins.then_inc(tail_chain, 1)
                dve.wait_ge(tail_chain, n[0])

            def spread(a, k):
                return a.unsqueeze(2).to_broadcast([a.shape[0], a.shape[1], k])

            def grouped(a, k):
                return a.rearrange("p (g k) -> p g k", k=k)

            def normalise(src, dst, groups, k, scale, add, turn):
                width = groups * k
                s, c, w = grouped(src, k), grouped(xc[:, 0:width], k), grouped(sq[:, 0:width], k)
                step(dve.tensor_reduce(red[:, 0:groups], s, mybir.AxisListType.X, ALU.add))
                step(dve.tensor_scalar(red[:, 0:groups], red[:, 0:groups], 1.0 / k, None, ALU.mult))
                step(dve.tensor_tensor(c, s, spread(red[:, 0:groups], k), ALU.subtract))
                step(dve.tensor_tensor(w, c, c, ALU.mult))
                step(dve.tensor_reduce(red2[:, 0:groups], w, mybir.AxisListType.X, ALU.add))
                if scale is not None:
                    step(dve.tensor_scalar(red2[:, 0:groups], red2[:, 0:groups], scale, EPS, ALU.mult, ALU.add))
                dve.sem_inc(var_ready, 1)
                dve.wait_ge(std_ready, turn)
                if scale is None:
                    step(dve.tensor_scalar(red3[:, 0:groups], red3[:, 0:groups], add, None, ALU.add))
                step(dve.reciprocal(red3[:, 0:groups], red3[:, 0:groups]))
                step(dve.tensor_tensor(grouped(dst, k), c, spread(red3[:, 0:groups], k), ALU.mult))

            for b in range(2):
                dve.wait_ge(h_full, b + 1)
                step(dve.tensor_copy(res[:, b * 512:(b + 1) * 512], PA[b][:, :]))
            normalise(res, xn, TT, 64, 1.0 / 64, 0.0, 1)
            dve.sem_inc(xn_ready, 1)
            for b in range(4):
                dve.wait_ge(kv_full, b + 1)
                step(dve.tensor_copy(kv[:, b * 512:(b + 1) * 512], (PA + PB)[b][:, :]))
            normalise(kv, kv, 512, 4, None, EPS, 2)
            dve.wait_ge(tail_in, 13 * 16)
            kv3 = kv.rearrange("p (t n) -> p t n", t=TT)
            for n0_, op in ((0, ALU.mult), (1, ALU.add)):
                wb = lnwb[:, n0_ * 128:(n0_ + 1) * 128].unsqueeze(1).to_broadcast([128, TT, 128])
                step(dve.tensor_tensor(kv3, kv3, wb, op))
            dve.sem_inc(kv_ready, 1)
            for q in range(QG):
                dve.wait_ge(kvm_full, q + 1)
                step(dve.tensor_tensor(grouped(kvm[:, q * 512:(q + 1) * 512], 64), grouped((PA + PB)[q][0:64, :], 64),
                                       mask.unsqueeze(1).to_broadcast([64, JN, 64]), ALU.mult))
            dve.sem_inc(kvm_ready, 1)
            for b in range(4):
                dve.wait_ge(att_full, b + 1)
                dve.tensor_tensor(rt[0:64, b * 512:(b + 1) * 512], (PC + PD)[b][0:64, :], xt[0:64, b * 512:(b + 1) * 512],
                                  ALU.add).then_inc(rt_ready, 1)
            step(dve.tensor_tensor(res, res, xn, ALU.add))
            dve.wait_ge(gelu_ready, 2)
            step(dve.tensor_tensor(res, res, gl, ALU.add))
            normalise(res, xn, TT, 64, 1.0 / 64, 0.0, 3)
            dve.sem_inc(xn_ready, 1)
            for b in range(2):
                dve.wait_ge(lg_full, b + 1)
                step(dve.tensor_copy(lg[:, b * 512:(b + 1) * 512], PA[b][:, :]))
            for t in range(TT):
                step(dve.max(mx[:, t * 8:t * 8 + 8], lg[:, t * 64:t * 64 + 64]))
                step(dve.max_index(ixs[:, t * 8:t * 8 + 8], mx[:, t * 8:t * 8 + 8], lg[:, t * 64:t * 64 + 64]))
            step(dve.tensor_copy(ixf, ixs[:, :]))
            m8, i8 = grouped(mx, 8), grouped(ixf, 8)
            step(dve.tensor_tensor(gate[:, 0:16], m8[:, :, 1], m8[:, :, 0], ALU.subtract))
            dve.sem_inc(dif_ready, 1)
            dve.wait_ge(exp_ready, 1)
            step(dve.tensor_scalar(gate[:, 32:48], gate[:, 16:32], 1.0, None, ALU.add))
            step(dve.reciprocal(gate[:, 48:64], gate[:, 32:48]))
            step(dve.tensor_tensor(gate[:, 32:48], gate[:, 16:32], gate[:, 48:64], ALU.mult))
            it = iota.unsqueeze(1).to_broadcast([128, TT, 64])
            c3, e3 = grouped(comb, 64), grouped(eq, 64)
            step(dve.tensor_tensor(c3, it, i8[:, :, 0:1].to_broadcast([128, TT, 64]), ALU.is_equal))
            step(dve.tensor_tensor(e3, it, i8[:, :, 1:2].to_broadcast([128, TT, 64]), ALU.is_equal))
            step(dve.tensor_tensor(c3, c3, spread(gate[:, 48:64], 64), ALU.mult))
            step(dve.tensor_tensor(e3, e3, spread(gate[:, 32:48], 64), ALU.mult))
            step(dve.tensor_tensor(comb, comb, eq, ALU.add))
            dve.sem_inc(comb_ready, 1)
            for b in range(4):
                dve.wait_ge(ct_full, b + 1)
                dve.tensor_copy(ct[:, b * 512:(b + 1) * 512], (PB + PC)[b][0:64, :]).then_inc(ct_ready, 1)
            for b in range(2):
                dve.wait_ge(bias_full, b + 1)
                s_ = slice(b * 512, (b + 1) * 512)
                step(dve.tensor_tensor(acc[:, s_], PD[b][:, :], res[:, s_], ALU.add))
            dve.sem_inc(acc_ready, 1)
            with dve.Fori(0, EXPERTS // 2) as i:
                for e in range(2):
                    for half in range(2):
                        m = e * 2 + half
                        dve.wait_ge(acc_done, i * 4 + m + 1)
                        dve.wait_ge(hid_used, (i * 4 + m) * 2 + 10)
                        g = c3[:, half * 8:(half + 1) * 8, bass.ds(i * 2 + e, 1)].to_broadcast([128, 8, 64])
                        dve.tensor_tensor(grouped(gated[:, m, :], 64), grouped((PC, PD)[e][half][:, :], 64), g,
                                          ALU.mult).then_inc(y_taken, 1)

        @block.tensor
        def _(pe):
            pe.wait_ge(consts_in, NCONST)
            with pe.Fori(0, JN) as j:
                for c in range(NC):
                    if c % 4 == 0:
                        pe.wait_ge(xin_in[c // 4], j * 32 + 32)
                    pe.wait_ge(b_free, j * NC + c + 1)
                    mm = pe.matmul(PB[c % 2][:, :], lift[:, :], xin[:, c // 4, (c % 4) * CW:(c % 4 + 1) * CW],
                                   start=True, stop=True)
                    mm.then_inc(b_full, 1)
                    if c % 4 == 3:
                        pe.wait_ge(b_full, j * NC + c + 1)
                        pe.sem_inc(xin_free, 1)

            def forward(l):
                def turn(j, c):
                    pe.wait_ge(v_ready, (l * JN + j) * NC + c + 1)
                    pe.wait_ge(a_free, l * AL + j * NC + c + 1)
                    for n in range(4):
                        last = pe.transpose(PA[c % 2][:, n * 128:(n + 1) * 128], vch[:, c % 4, n * 128:(n + 1) * 128],
                                            ident[:, :])
                    last.then_inc(a_full, 1)

                def rows(j, c):
                    pe.wait_ge(a_free, l * AL + j * NC + c + 3)
                    pe.wait_ge(b_free, B0 + l * BL + j * NC + c + 1)
                    for n in range(4):
                        last = pe.matmul(PB[c % 2][:, n * 48:(n + 1) * 48], vt[:, c % 4, n * 128:(n + 1) * 128], fy[:, :],
                                         start=True, stop=True)
                    last.then_inc(b_full, 1)
                    pe.wait_ge(a_full, l * AL + j * NC + c + 1)
                    pe.sem_inc(v_free, 1)

                def columns(j):
                    pe.wait_ge(b_free, B0 + l * BL + j * NC + NC + 2)
                    for n in range(4):
                        pe.wait_ge(c_free, l * CL + j * 4 + n + 1)
                        for k in range(3):
                            last = pe.transpose(PC[n % 2][:, k * 128:(k + 1) * 128], cy_[:, (n * 3 + k) * 128:(n * 3 + k + 1) * 128],
                                                ident[:, :])
                        last.then_inc(c_full, 1)
                    for h in range(2):
                        pe.wait_ge(c_free, l * CL + j * 4 + 2 * h + 4)
                        pe.wait_ge(d_free, l * DL + j * 2 + h + 1)
                        for k in range(6):
                            ky = h * 6 + k
                            last = pe.matmul(PD[h][:, k * 48:(k + 1) * 48], dx_[:, ky * 128:(ky + 1) * 128], fx[:, :],
                                             start=True, stop=True)
                        last.then_inc(d_full, 1)

                def group(j, last):
                    for c in range(NC):
                        rows(j, c)
                        if c < NC - 2:
                            turn(j, c + 2)
                        elif not last:
                            turn(j + 1, c - (NC - 2))
                    columns(j)
                turn(0, 0)
                turn(0, 1)
                with pe.Fori(0, JN - 1) as j:
                    group(j, False)
                group(JN - 1, True)

            def mixing(l):
                with pe.Fori(0, KG) as k:
                    for h in range(2):
                        n = k * 2 + h
                        pe.wait_ge(exp_dve, (l * MSTEPS + n) * 2 + 2)
                        pe.wait_ge(exp_pool, (l * MSTEPS + n) * 2 + 2)
                        pe.wait_ge(exp_act, (l * MSTEPS + n) * 3 + 3)
                        pe.wait_ge(a_free, l * AL + AF + n + 1)
                        for m in range(MK):
                            o = PA[h][:, m * 64:(m + 1) * 64]
                            pe.matmul(o, wring[:, h, 2 * m, :], xring[:, h, m, 1:3, :].rearrange("p t b -> p (t b)"),
                                      start=True, stop=False)
                            last = pe.matmul(o, wring[:, h, 2 * m + 1, :],
                                             xring[:, h, m, 0:2, :].rearrange("p t b -> p (t b)"), start=False, stop=True)
                        last.then_inc(a_full, 1)

            def inverse(l):
                dbase = l * DL + DF

                def spectra(j, n):
                    if n == 0:
                        pe.wait_ge(yp_ready, l * JN + j + 1)
                    pe.wait_ge(d_free, dbase + j * 6 + n + 1)
                    for k in range(3):
                        last = pe.transpose(PD[n][0:96, k * 128:(k + 1) * 128], yp[:, (n * 3 + k) * 96:(n * 3 + k + 1) * 96], ident[:, :])
                    last.then_inc(d_full, 1)

                def columns(j, p):
                    pe.wait_ge(d_free, dbase + j * 6 + p // 3 + 3)
                    pe.wait_ge(c_free, l * CL + CF + j * 6 + p + 1)
                    pe.matmul(PC[p % 2][:, 0:256], yt[:, p * 128:(p + 1) * 128], tx[:, :], start=True,
                              stop=True).then_inc(c_full, 1)

                def turn(j, s):
                    pe.wait_ge(c_free, l * CL + CF + j * 6 + 8)
                    pe.wait_ge(d_free, dbase + j * 6 + 2 + s + 1)
                    for k in range(4):
                        g = s * 4 + k
                        last = pe.transpose(PD[s % 2][0:96, k * 128:(k + 1) * 128], z1[:, g * 96:(g + 1) * 96], ident[:, :])
                    last.then_inc(d_full, 1)

                def rows(j, c):
                    full, free, P, base = ((a_full, a_free, PA, l * AL + AF + AM),
                                           (b_full, b_free, PB, B0 + l * BL + BF))[c % 2]
                    s = c // 2
                    pe.wait_ge(d_free, dbase + j * 6 + 2 + s + 3)
                    pe.wait_ge(free, base + j * 4 + s + 1)
                    o = P[s % 2]
                    pe.matmul(o[:, :], cur[:, 0:128], big[:, j, c * CW:(c + 1) * CW], start=True, stop=False)
                    for k in range(2):
                        t = (c % 2) * 2 + k
                        last = pe.matmul(o[:, k * 256:(k + 1) * 256], z1t[:, s, t * 128:(t + 1) * 128], ty[:, :],
                                         start=False, stop=(k == 1))
                    last.then_inc(full, 1)

                def group(j, last):
                    turn(j, 0)
                    turn(j, 1)
                    rows(j, 0)
                    turn(j, 2)
                    rows(j, 1)
                    turn(j, 3)
                    rows(j, 2)
                    if not last:
                        spectra(j + 1, 0)
                    rows(j, 3)
                    if not last:
                        spectra(j + 1, 1)
                    for c in range(4, NC):
                        rows(j, c)
                        if c < 7 and not last:
                            columns(j + 1, 2 * (c - 4))
                            columns(j + 1, 2 * (c - 4) + 1)

                pe.wait_ge(cur_ready, l + 1)
                pe.wait_ge(v_copied, l * JN * NC + 4)
                spectra(0, 0)
                spectra(0, 1)
                for p in range(6):
                    columns(0, p)
                with pe.Fori(0, JN - 1) as j:
                    group(j, False)
                group(JN - 1, True)

            def norm(l):
                pe.wait_ge(bn_mm, l * 4 + 1)
                pe.matmul(PD[0][:, 0:1], avg[:, :], bn[:, 0:1], start=True, stop=True).then_inc(bn_mm, 1)
                pe.wait_ge(bn_mm, l * 4 + 3)
                pe.matmul(PD[0][:, 1:2], avg[:, :], bn[:, 3:4], start=True, stop=True).then_inc(bn_mm, 1)

            forward(0)
            with pe.Fori(0, LAYERS - 1) as l:
                mixing(l)
                inverse(l)
                norm(l)
                forward(l + 1)
            mixing(LAYERS - 1)
            inverse(LAYERS - 1)
            norm(LAYERS - 1)
            n0, b0 = LAYERS * JN * NC, B0 + LAYERS * BL
            with pe.Fori(0, JN) as j:
                for c in range(NC):
                    pe.wait_ge(v_ready, j * NC + n0 + c + 1)
                    if c % 4 == 0:
                        pe.wait_ge(b_free, j * 2 + b0 + c // 4 + 1)
                    for n in range(4):
                        k = (c % 4) * 4 + n
                        last = pe.matmul(PB[c // 4][:, k * 4:k * 4 + 4], vch[:, c % 4, n * 128:(n + 1) * 128],
                                         qcol[:, :], start=True, stop=True)
                    last.then_inc(v_free, 1)

            pe.wait_ge(b_free, B0 + LAYERS * BL + JN * 2 + 2)
            for j in range(JN):
                last = pe.transpose(PA[j // 4][:, (j % 4) * 128:(j % 4 + 1) * 128], ht[:, j * 128:(j + 1) * 128], ident[:, :])
                if j % 4 == 3:
                    last.then_inc(h_full, 1)

            def tokens_to_columns(src, banks_, full):
                for t in range(TT):
                    last = pe.transpose(banks_[t // 4][0:64, (t % 4) * 128:(t % 4 + 1) * 128], src[:, t * 64:(t + 1) * 64],
                                        ident[:, :])
                    if t % 4 == 3:
                        last.then_inc(full, 1)

            pe.wait_ge(xn_ready, 1)
            tokens_to_columns(xn, PB + PC, xt_full)
            pe.wait_ge(tail_in, 13 * 16)
            pe.wait_ge(ones_set, 2)
            pe.wait_ge(xt_ready, 4)
            for t in range(TT):
                last = pe.matmul((PA + PB)[t // 4][:, (t % 4) * 128:(t % 4 + 1) * 128], xt[:, t * 128:(t + 1) * 128],
                                 wqkv[:, 64:192], start=True, stop=True)
                if t % 4 == 3:
                    last.then_inc(kv_full, 1)
            for b in range(4):
                pe.matmul((PC + PD)[b][0:64, :], wqkv[:, 0:64], xt[:, b * 512:(b + 1) * 512], start=True,
                          stop=True).then_inc(q_full, 1)
            pe.wait_ge(kv_ready, 1)
            for q in range(QG):
                r = slice(q * 32, (q + 1) * 32)
                for j in range(JN):
                    for x2 in range(2):
                        o = (j * 2 + x2) * 128
                        last = pe.matmul((PA + PB)[q][0:64, j * 64:(j + 1) * 64], kv[r, o:o + 64], kv[r, o + 64:o + 128],
                                         start=(x2 == 0), stop=(x2 == 1))
                last.then_inc(kvm_full, 1)
            pe.wait_ge(kvm_ready, 1)
            pe.wait_ge(qt_ready, 4)
            for j in range(JN):
                for q in range(QG):
                    qv = qt[:, j * 256:(j + 1) * 256].rearrange("p (x n) -> p x n", x=2)[:, :, q * 32:(q + 1) * 32]
                    o = (PC + PD)[j // 2][0:64, (j % 2) * 256:(j % 2 + 1) * 256]
                    last = pe.matmul(o.rearrange("p (x n) -> p x n", x=2)[:, :, q * 32:(q + 1) * 32],
                                     kvm[:, q * 512 + j * 64:q * 512 + (j + 1) * 64], qv, start=True, stop=True)
                if j % 2 == 1:
                    last.then_inc(att_full, 1)
            for t in range(TT):
                if t % 4 == 0:
                    pe.wait_ge(rt_ready, t // 4 + 1)
                last = pe.matmul(PA[t // 8][:, (t % 8) * 64:(t % 8 + 1) * 64], rt[:, t * 128:(t + 1) * 128], wproj[:, :],
                                 start=True, stop=True)
                if t % 8 == 7:
                    last.then_inc(proj_full, 1)
            pe.wait_ge(xn_ready, 2)
            tokens_to_columns(xn, PB + PC, xt_full)
            pe.wait_ge(xt_ready, 8)
            for t in range(TT):
                last = pe.matmul(PA[t // 8][:, (t % 8) * 64:(t % 8 + 1) * 64], xt[:, t * 128:(t + 1) * 128], wroute[:, :],
                                 start=True, stop=True)
                if t % 8 == 7:
                    last.then_inc(lg_full, 1)
            pe.wait_ge(comb_ready, 1)
            tokens_to_columns(comb, PB + PC, ct_full)
            pe.wait_ge(ct_ready, 4)
            for t in range(TT):
                last = pe.matmul(PD[t // 8][:, (t % 8) * 64:(t % 8 + 1) * 64], ct[:, t * 128:(t + 1) * 128], b2all[:, :],
                                 start=True, stop=True)
                if t % 8 == 7:
                    last.then_inc(bias_full, 1)
            pe.wait_ge(acc_ready, 1)

            def hidden(i, e):
                if e % 2 == 0:
                    pe.wait_ge(e_in[e // 2], i * 48 + 48)
                for c in range(4):
                    pe.wait_ge(hid_ready, i * 16 + e * 4 + c + 1)
                    pe.matmul((PA + PB)[c][:, :], w1r[:, e // 2, e % 2, :], xt[:, c * 512:(c + 1) * 512], start=True,
                              stop=True).then_inc(hid_full, 1)

            def outputs(i, e, after=0):
                for half in range(2):
                    pe.wait_ge(y_taken, i * 8 + e * 2 + half + 1)
                    for c in range(2):
                        n = half * 2 + c
                        pe.wait_ge(hid_ready, i * 16 + e * 4 + n + 5)
                        for k in range(4):
                            last = pe.matmul((PC, PD)[e % 2][half][:, (c * 4 + k) * 64:(c * 4 + k + 1) * 64],
                                             hid[:, (e % 2) * 4 + n, k * 128:(k + 1) * 128], w2r[:, e // 2, e % 2, :],
                                             start=True, stop=True)
                        last.then_inc(hid_used, 1)

            with pe.Fori(0, EXPERTS // 4) as i:
                hidden(i, 0)
                for e in range(1, 4):
                    hidden(i, e)
                    outputs(i, e - 1)
                outputs(i, 3)


_INS = ['x', 'L0_tok_p_w', 'L0_tok_p_b', 'L0_tok_fw1', 'L0_tok_fw2', 'L0_tok_w_w', 'L0_tok_w_b', 'L0_tok_bn_g',
        'L0_tok_bn_b', 'L0_tok_q_w', 'L0_tok_q_b', 'L0_attn_W_qkv', 'L0_attn_b_qkv', 'L0_attn_kln_w', 'L0_attn_kln_b',
        'L0_attn_vln_w', 'L0_attn_vln_b', 'L0_attn_W_proj', 'L0_attn_b_proj', 'L0_ffn_Wr', 'L0_ffn_br', 'L0_ffn_W1',
        'L0_ffn_b1', 'L0_ffn_W2', 'L0_ffn_b2']


def kernel(**inputs):
    import concourse.bacc as _bacc
    from concourse import mybir as _mybir
    from concourse.bass_utils import run_bass_kernel_spmd as _run

    nc = _bacc.Bacc("TRN2", target_bir_lowering=False, num_devices=1)
    arrays, args = {}, []

    def give(name, a):
        arrays[name] = a
        args.append(nc.dram_tensor(name, a.shape, _mybir.dt.from_np(a.dtype), kind="ExternalInput").ap())

    for name in _INS:
        a = np.ascontiguousarray(inputs[name])
        if name in ('L0_tok_fw1', 'L0_tok_fw2'):
            a = a.reshape(LAYERS, CH, CH, 12 * KY * 2)
        if name == 'L0_attn_W_qkv':
            a = np.ascontiguousarray(a.reshape(16, 3, 4, 64).transpose(3, 1, 0, 2).reshape(64, 192))
        if name == 'L0_attn_b_qkv':
            a = np.ascontiguousarray(a.reshape(16, 3, 4).transpose(1, 0, 2).reshape(192))
        if name == 'L0_attn_W_proj':
            a = np.ascontiguousarray(a.T)
        give("in_" + name, a)
    for name, a in constants().items():
        give("const_" + name, a)
    args.append(nc.dram_tensor("out_0", (B, S, S), _mybir.dt.float32, kind="ExternalOutput").ap())
    vit_tower(nc, *args)
    r = _run(nc, [arrays], core_ids=[0])
    return r.results[0]["out_0"]
```

```python
import concourse.bass as bass
from concourse import mybir
from contextlib import ExitStack
import numpy as np

B, S, CH, LAYERS = 32, 64, 32, 4
QG, JN = 4, 8
KX, KY = 24, 12
KG = KX // QG
GM = KG * KY * 2
NPIX = S * S
CW = 512
NC = NPIX // CW
YF = KY * 2
XB = 4
MK = 6
MSTEPS = KG * KY // MK
EPS = 1e-5
EXPERTS, TOKENS = 64, B * S
SLOT_TILES = 2 * TOKENS // 128 + EXPERTS
PCOLS = 128 + 3


def constants():
    f = np.float64
    two_pi = 2 * np.pi / S
    y, ky = np.arange(S, dtype=f), np.arange(KY, dtype=f)
    kx = np.array(list(range(12)) + list(range(52, 64)), dtype=f)
    cy, sy = np.cos(two_pi * np.outer(y, ky)), np.sin(two_pi * np.outer(y, ky))
    cx, sx = np.cos(two_pi * np.outer(y, kx)), np.sin(two_pi * np.outer(y, kx))
    fy = np.zeros((2, S, 2, KY, 2), f)
    for a in range(2):
        fy[a, :, a, :, 0], fy[a, :, a, :, 1] = cy, -sy
    fx = np.zeros((2, S, KX, 2), f)
    fx[0, :, :, 0], fx[1, :, :, 0] = cx, sx
    fx[0, :, :, 1], fx[1, :, :, 1] = -sx, cx
    tx = np.zeros((KX, 2, 2, S, 2, 2), f)
    for a in range(2):
        tx[:, a, 0, :, a, 0], tx[:, a, 1, :, a, 0] = cx.T / S, -sx.T / S
        tx[:, a, 0, :, a, 1], tx[:, a, 1, :, a, 1] = sx.T / S, cx.T / S
    wk = np.where(ky == 0, 1.0, 2.0)[:, None] / S
    ty = np.zeros((XB, KY, 2, XB, S), f)
    for a in range(XB):
        ty[a, :, 0, a], ty[a, :, 1, a] = wk * cy.T, -wk * sy.T
    avg = np.kron(np.full((QG, QG), 1.0 / QG), np.eye(CH))
    f1 = np.zeros((2, S, 2, KX, 2), f)
    for a in range(2):
        f1[a, :, 0, :, a], f1[a, :, 1, :, a] = cx, -sx
    f2 = np.zeros((2, S, KY, 2), f)
    f2[0, :, :, 0], f2[0, :, :, 1], f2[1, :, :, 0], f2[1, :, :, 1] = cy, -sy, sy, cy
    lin = np.linspace(0.0, 1.0, S, dtype=np.float32)
    fft = np.exp(-1j * two_pi * np.outer(kx, y)), np.exp(-1j * two_pi * np.outer(y, ky))
    gs = np.zeros((QG, 3, KG, KY, 2), f)
    for n, (u, v) in enumerate(((lin, np.ones(S)), (np.ones(S), lin), (np.ones(S), np.ones(S)))):
        z = (fft[0] @ np.outer(u, v) @ fft[1]).reshape(QG, KG, KY)
        gs[:, n, :, :, 0], gs[:, n, :, :, 1] = z.real, z.imag
    grid = np.stack([np.repeat(lin, S), np.tile(lin, S), np.ones(NPIX, np.float32)])
    mask = np.kron(np.eye(16), np.ones((4, 4))) / S
    iota = np.tile(np.arange(64), (128, 1))
    tri = np.triu(np.ones((128, 128)), 1)
    pid = np.arange(128)[:, None]
    out = dict(tri=tri, pid=pid, fy=fy.reshape(128, 48), fx=fx.reshape(128, 48), tx=tx.reshape(96, 256), ty=ty.reshape(96, 256),
               ident=np.eye(128), avg=avg, grid=grid, mask=mask, iota=iota,
               f1=f1.reshape(128, 96), f2=f2.reshape(128, 24), gs=gs.reshape(12, GM))
    return {k: np.ascontiguousarray(v.astype(np.float32)) for k, v in out.items()}


def vit_tower(nc, x, lift_w, fw1, fw2, w_w, scales, q_w, q_b, W_qkv, b_qkv, kln_w, kln_b, vln_w, vln_b,
              W_proj, b_proj, Wr, br, wexp, b2, c_tri, c_pid, c_fy, c_fx, c_tx, c_ty, c_ident, c_avg, c_grid, c_mask, c_iota,
              c_f1, c_f2, c_gs,
              slots_x, slots_y, out):
    fp32 = mybir.dt.float32
    ALU = mybir.AluOpType
    ACT = mybir.ActivationFunctionType
    ctx = ExitStack()
    with ctx:
        def sb(name, shape, dt=fp32):
            return ctx.enter_context(nc.sbuf_tensor(name, shape, dt))

        def sem(name):
            return ctx.enter_context(nc.semaphore(name))

        big = sb("big", [128, JN, NPIX])
        modes = sb("modes", [128, B * GM])
        wmode = sb("wmode", [128, CH, GM])
        work = sb("work", [128, 8832])
        xmode = modes[:, :].rearrange("p (b f) -> p b f", b=B)
        z1t = modes[0:96, 0:2048].rearrange("p (s n) -> p s n", s=4)
        vch = work[:, 0:2048].rearrange("p (s n) -> p s n", s=4)
        vt = work[:, 2048:4096].rearrange("p (s n) -> p s n", s=4)
        cy_ = work[:, 4096:5632]
        dx_ = work[:, 5632:7168]
        xj = work[:, 7168:7744]
        xrow = work[0:4, 0:4608]
        xin = work[:, 4608:5632].rearrange("p (n y) -> p n y", n=B // 2)
        xk = work[0:64, 5632:7168]
        xs_ = work[0:96, 7168:7360].rearrange("p (m f) -> p m f", m=8)
        gsum = work[:, 7360:7504]
        f1, f2 = work[:, 7504:7600], work[0:64, 7600:7648].rearrange("p (a f) -> p a f", a=2)
        gspec = work[0:12, 7648:7792]
        typix = modes[0:103, 2048:4096].rearrange("p (s n) -> p s n", s=2)
        z1mix = modes[0:103, 0:2048].rearrange("p (s n) -> p s n", s=4)
        ymode = work[:, 0:4608].rearrange("p (b f) -> p b f", b=B)
        wring = work[:, 4608:7680].rearrange("p (s m c) -> p s m c", s=2, c=128)
        xring = work[:, 7680:8832].rearrange("p (s m t b) -> p s m t b", s=2, m=MK, t=3)
        z1 = work[:, 4608:6144]
        yq = work[:, 6144:6720]
        stats = work[:, 8064:8448].rearrange("p (n s) -> p n s", s=6)
        yp = work[:, 7488:8064]
        yt = work[0:96, 6720:7488]
        ht = work[:, 2048:3072]

        flat = big[:, :, :].rearrange("p j n -> p (j n)")
        pos = [0]

        def tail(n, rows=128):
            pos[0] += n
            return flat[0:rows, pos[0] - n:pos[0]]

        TT = 16
        res = tail(1024)
        xn, xc, sq = tail(1024), tail(2048), tail(2048)
        red, red2, red3 = tail(512), tail(512), tail(512)
        kv = tail(2048)
        xt, rt = tail(2048, 65), tail(2048, 65)
        qt, kvm, ct = tail(2048, 64), tail(2048, 64), tail(2048, 64)
        gl, lg, comb = tail(1024), tail(1024), tail(1024)
        mx, ixf, gate = tail(128), tail(128), tail(64)
        acc = tail(1024)
        first, second, chosen = tail(1024), tail(1024), tail(1024)
        before = tail(17 * 64)
        pos_ = xc[:, 0:1024]
        ntile, base = tail(64), tail(64)
        run = [tail(128), tail(128)]
        slotf, texf = tail(32), tail(1)
        ones_m = tail(128)
        xg = tail(512).rearrange("p (s n) -> p s n", s=2)
        xgt = tail(1024).rearrange("p (s n) -> p s n", s=2)
        hid = tail(1024).rearrange("p (s n) -> p s n", s=2)
        yg = tail(512).rearrange("p (s n) -> p s n", s=2)
        ysel = [gl, lg]
        assert pos[0] <= JN * NPIX
        wpos = [0]

        def tailw(n, rows):
            wpos[0] += n
            return modes[0:rows, wpos[0] - n:wpos[0]]

        wqkv, wproj, wroute = tailw(192, 65), tailw(64, 65), tailw(64, 65)
        b2all, mask, iota, lnwb = tailw(64, 64), tailw(64, 64), tailw(64, 128), tailw(256, 128)
        tri, pid = tailw(128, 128), tailw(1, 128)
        wflat = wmode[:, :, :].rearrange("p o f -> p (o f)")
        wt = wflat[:, 0:1536].rearrange("p (s k n) -> p s k n", s=2, k=4)
        qscaled = sb("qscaled", [128, 4])
        shift = work[:, 3072:3200]
        ixs = sb("ixs", [128, 128], mybir.dt.uint32)
        slot = sb("slot", [128, 32], mybir.dt.uint32)
        texp = sb("texp", [1, 128], mybir.dt.int32)

        fy, fx = sb("fy", [128, 48]), sb("fx", [128, 48])
        tx, ty = sb("tx", [96, 256]), sb("ty", [96, 256])
        ident, avg = sb("ident", [128, 128]), sb("avg", [128, 128])
        liftx = work[0:4, 7792:7920]
        liftg = work[0:12, 7920:8048]
        liftt = sb("liftt", [128, 7])
        lmix = sb("lmix", [7, 128])
        params = sb("params", [128, LAYERS, PCOLS])
        cur = sb("cur", [128, PCOLS])
        bn = sb("bn", [128, 16])
        qcol = sb("qcol", [128, 4])
        qb = sb("qb", [128, 1])
        qbias = sb("qbias", [128, 1])

        banks = [ctx.enter_context(nc.psum_tensor(f"bank{i}", [128, 512], fp32)) for i in range(8)]
        PA, PB, PC, PD = banks[0:2], banks[2:4], banks[4:6], banks[6:8]

        consts_in = sem("consts_in")
        zeroed = sem("zeroed")
        a_full, b_full, c_full, d_full = sem("a_full"), sem("b_full"), sem("c_full"), sem("d_full")
        a_free, b_free, c_free, d_free = sem("a_free"), sem("b_free"), sem("c_free"), sem("d_free")
        first_in, rows_in, pix_in = sem("first_in"), sem("rows_in"), [sem("pix_in0"), sem("pix_in1")]
        xs_ready, lmix_ready = sem("xs_ready"), sem("lmix_ready")
        v_ready, v_copied = sem("v_ready"), sem("v_copied")
        v_free = sem("v_free")
        x_sent = sem("x_sent")
        w_in, w_used = sem("w_in"), sem("w_used")
        cur_ready = sem("cur_ready")
        ring_clear = sem("ring_clear")
        exp_dve, exp_act = sem("exp_dve"), sem("exp_act")
        y_done = sem("y_done")
        yq_in, yp_ready = sem("yq_in"), sem("yp_ready")
        stat_done = sem("stat_done")
        bn_chain, bn_mm, bn_sq, bn_done = sem("bn_chain"), sem("bn_mm"), sem("bn_sq"), sem("bn_done")
        pool_past, dve_past, pe_past = sem("pool_past"), sem("dve_past"), sem("pe_past")
        out_sent, q_prep = sem("out_sent"), sem("q_prep")
        tail_in, ones_set, tail_chain = sem("tail_in"), sem("ones_set"), sem("tail_chain")
        h_full, xn_ready, xt_full, xt_ready = sem("h_full"), sem("xn_ready"), sem("xt_full"), sem("xt_ready")
        var_ready, std_ready = sem("var_ready"), sem("std_ready")
        kv_full, q_full, qt_ready, kv_taken, kv_ready = (sem("kv_full"), sem("q_full"), sem("qt_ready"),
                                                         sem("kv_taken"), sem("kv_ready"))
        kvm_full, kvm_ready, att_full, rt_ready = sem("kvm_full"), sem("kvm_ready"), sem("att_full"), sem("rt_ready")
        proj_full, gelu_ready, lg_full, lg_taken = sem("proj_full"), sem("gelu_ready"), sem("lg_full"), sem("lg_taken")
        dif_ready, exp_ready, comb_ready = sem("dif_ready"), sem("exp_ready"), sem("comb_ready")
        ct_full, ct_ready, bias_full, acc_ready = sem("ct_full"), sem("ct_ready"), sem("bias_full"), sem("acc_ready")
        slots_zeroed, chosen_ready, tot_full = sem("slots_zeroed"), sem("chosen_ready"), sem("tot_full")
        texf_ready, texr_full, texp_ready, slot_ready = (sem("texf_ready"), sem("texr_full"), sem("texp_ready"),
                                                         sem("slot_ready"))
        scattered = sem("scattered")
        wt_in, xg_in, yg_out = [sem("wt_in0"), sem("wt_in1")], [sem("xg_in0"), sem("xg_in1")], [sem("yg_out0"), sem("yg_out1")]
        xg_turned, xgt_ready, hid_full, hid_ready = sem("xg_turned"), sem("xgt_ready"), sem("hid_full"), sem("hid_ready")
        yg_full, yg_ready = sem("yg_full"), sem("yg_ready")
        gathered, sum_ready = [sem("gathered0"), sem("gathered1")], sem("sum_ready")

        A0, B0, C0, D0 = 2, 2, 2, 14
        AM, AI, AF = MSTEPS, 32, 64
        BI, BF = 32, 64
        CI, CF = 48, 32
        DI, DF = 48, 16
        AL, BL, CL, DL = AM + AI + AF, BI + BF, CI + CF, DI + DF
        GROUPS = SLOT_TILES // 4
        NFIRST = 16 * (5 + 2 * QG)
        NCONST = 16 * (5 * QG + 6 + 1)
        XJ = 16 * QG * QG

        block = ctx.enter_context(nc.Block())

        @block.sync
        def _(sp):
            sp.dma_start(f1, c_f1).then_inc(first_in, 16)
            for a in range(2):
                sp.dma_start(xin[a * 64:(a + 1) * 64], x.rearrange("(n a) x y o -> a x n (y o)", a=2)[a]).then_inc(first_in, 16)
            sp.dma_start(f2, c_f2.rearrange("(a y) f -> y a f", a=2)).then_inc(first_in, 16)
            sp.dma_start(gspec, c_gs).then_inc(first_in, 16)
            sp.wait_ge(zeroed, 5)
            for g in range(QG):
                r = slice(g * CH, (g + 1) * CH)
                sp.dma_start(liftx[g:g + 1, r], lift_w[0:1, :]).then_inc(first_in, 16)
                sp.dma_start(liftg[g * 3:g * 3 + 3, r], lift_w[1:4, :]).then_inc(first_in, 16)
            def load_weights(l):
                for g in range(QG):
                    fw = (fw1, fw2)[g // 2]
                    k0 = (g % 2) * GM
                    sp.dma_start(wmode[g * CH:(g + 1) * CH, :, :], fw[l, :, :, k0:k0 + GM]).then_inc(w_in, 16)

            def send_spectra(l):
                with sp.Fori(0, JN) as j:
                    sp.wait_ge(d_free, D0 + l * DL + DI + j * 2 + 4)
                    for q in range(QG):
                        for g in range(QG):
                            sp.dma_start(xmode[g * CH:(g + 1) * CH, q * JN + j, :],
                                         xj[q * CH:(q + 1) * CH, g * GM:(g + 1) * GM]).then_inc(x_sent, 16)

            def fetch_mixed(j):
                for q in range(QG):
                    for g in range(QG):
                        sp.dma_start(yq[q * CH:(q + 1) * CH, g * GM:(g + 1) * GM],
                                     ymode[g * CH:(g + 1) * CH, q * JN + j, :]).then_inc(yq_in, 16)

            xv = x.rearrange("(q j) (k r) y o -> j k q (r y o)", q=QG, k=4)
            gv = c_grid.rearrange("p (k n) -> k p n", k=4)

            def pixels(j, k):
                sp.dma_start(typix[96:100, k % 2, :], xv[j, k]).then_inc(pix_in[k % 2], 16)
                sp.dma_start(typix[100:103, k % 2, :], gv[k]).then_inc(pix_in[k % 2], 16)

            load_weights(0)
            for q in range(QG):
                r = slice(q * CH, (q + 1) * CH)
                sp.dma_start(params[r, :, r], w_w.rearrange("l c d -> c l d")).then_inc(consts_in, 16)
                sp.dma_start(params[r, :, 128:131], scales.rearrange("l c n -> c l n")).then_inc(consts_in, 16)
                sp.dma_start(liftt[r, q:q + 1], lift_w[0:1, :].rearrange("n c -> c n")).then_inc(consts_in, 16)
                sp.dma_start(liftt[r, 4:7], lift_w[1:4, :].rearrange("n c -> c n"),
                             allow_slow_non_contiguous=True).then_inc(consts_in, 16)
                sp.dma_start(qcol[r, q:q + 1], q_w).then_inc(consts_in, 16)
            for dst, src in ((fy, c_fy), (fx, c_fx), (tx, c_tx), (ty, c_ty), (ident, c_ident), (avg, c_avg)):
                sp.dma_start(dst[:, :], src).then_inc(consts_in, 16)
            sp.dma_start(qb[:, :], q_b.rearrange("(a c) -> a c", a=1).broadcast_to([128, 1])).then_inc(consts_in, 16)
            sp.wait_ge(xs_ready, 1)
            for m in range(8):
                g, k0 = m // 2, (m % 2) * 3
                sp.dma_start(xrow[g:g + 1, k0 * B * YF:(k0 + 3) * B * YF], xs_[:, m, :]).then_inc(rows_in, 16)
            sp.wait_ge(a_free, A0 + AM + 2)
            fetch_mixed(0)
            pixels(0, 0)
            pixels(0, 1)

            def first_group(j, last):
                if not last:
                    sp.wait_ge(yp_ready, j + 1)
                    fetch_mixed(j + 1)
                for k in range(2):
                    sp.wait_ge(b_full, B0 + j * 4 + k + 1)
                    pixels(j, k + 2)
                if not last:
                    for k in range(2):
                        sp.wait_ge(b_full, B0 + j * 4 + k + 3)
                        pixels(j + 1, k)
            with sp.Fori(0, JN - 1) as j:
                first_group(j, False)
            first_group(JN - 1, True)

            def rest_of_layer(l):
                sp.wait_ge(a_free, A0 + l * AL + AM + 2)
                fetch_mixed(0)
                with sp.Fori(0, JN - 1) as j:
                    sp.wait_ge(yp_ready, l * JN + j + 1)
                    fetch_mixed(j + 1)

            def next_layer(l):
                sp.wait_ge(w_used, l + 1)
                load_weights(l + 1)
                send_spectra(l)
            next_layer(0)
            with sp.Fori(1, LAYERS - 1) as l:
                rest_of_layer(l)
                next_layer(l)
            rest_of_layer(LAYERS - 1)
            sp.wait_ge(bn_done, LAYERS)
            for dst, src in ((wqkv[0:64, :], W_qkv), (wqkv[64:65, :], b_qkv.rearrange("(a n) -> a n", a=1)),
                             (wproj[0:64, :], W_proj), (wproj[64:65, :], b_proj.rearrange("(a n) -> a n", a=1)),
                             (wroute[0:64, :], Wr), (wroute[64:65, :], br.rearrange("(a n) -> a n", a=1)),
                             (b2all, b2), (mask, c_mask), (iota, c_iota), (tri, c_tri), (pid, c_pid)):
                sp.dma_start(dst, src).then_inc(tail_in, 16)
            for n, src in enumerate((kln_w, vln_w, kln_b, vln_b)):
                sp.dma_start(lnwb[:, n * 64:(n + 1) * 64],
                             src.rearrange("h (a o) d -> a (h o d)", a=1).broadcast_to([128, 64])).then_inc(tail_in, 16)
            sp.wait_ge(texp_ready, 1)

            def weights(i, s):
                for k in range(4):
                    e = sp.value_load(texp[0:1, bass.ds(i * 8 + s * 4 + k, 1)], min_val=0, max_val=EXPERTS - 1)
                    sp.dma_start(wt[:, s, k, :], wexp[bass.ds(e, 1), :, :].rearrange("e p n -> (e p) n")).then_inc(wt_in[s], 16)

            def tokens(i, s):
                rows = slots_x[bass.ds((i * 2 + s) * 512, 512), :].rearrange("(k p) n -> p k n", k=4)
                sp.dma_start(xg[:, s, :].rearrange("p (k n) -> p k n", k=4), rows).then_inc(xg_in[s], 16)

            for s in range(2):
                weights(0, s)
            sp.wait_ge(scattered, 32 * 16)
            for s in range(2):
                tokens(0, s)
            with sp.Fori(0, GROUPS // 2 - 1) as i:
                for s in range(2):
                    sp.wait_ge(xg_turned, i * 2 + s + 1)
                    tokens(i + 1, s)
                    sp.wait_ge(yg_full, i * 2 + s + 2)
                    weights(i + 1, s)
            sp.wait_ge(sum_ready, 2)
            for q in range(QG):
                sp.dma_start(out[q * JN:(q + 1) * JN].rearrange("j (xp x) y -> xp j (x y)", x=2),
                             acc[q * 32:(q + 1) * 32, :].rearrange("p (j n) -> p j n", j=JN)).then_inc(out_sent, 16)
            sp.wait_ge(out_sent, 64)

        @block.gpsimd
        def _(pool):
            pool.memset(params[:, :, :], 0.0).then_inc(zeroed, 1)
            pool.memset(liftx[:, :], 0.0).then_inc(zeroed, 1)
            pool.memset(liftg[:, :], 0.0).then_inc(zeroed, 1)
            pool.memset(liftt[:, :], 0.0).then_inc(zeroed, 1)
            pool.memset(qcol[:, :], 0.0).then_inc(zeroed, 1)
            nz = SLOT_TILES * 64 // 2
            pool.memset(big[:, 0, 0:nz], 0.0).then_inc(zeroed, 1)
            pool.wait_ge(zeroed, 6)
            for h in range(2):
                pool.dma_start(slots_x[h * SLOT_TILES * 64:(h + 1) * SLOT_TILES * 64, :].rearrange("(p r) n -> p (r n)", p=128),
                               big[:, 0, 0:nz]).then_inc(slots_zeroed, 16)

            def mixing(l):
                pool.wait_ge(x_sent, (l + 1) * JN * XJ)
                pool.sem_inc(pool_past, 1)
                pool.memset(work[:, 4608:7680], 0.0).then_inc(ring_clear, 1)

            def regroup(l):
                with pool.Fori(0, JN) as j:
                    pool.wait_ge(yq_in, (l * JN + j + 1) * XJ)
                    pool.wait_ge(d_full, D0 + l * DL + j * 6 - 4)
                    pool.sem_inc(pool_past, 1)
                    pool.tensor_copy(yp.rearrange("p (y k f) -> p k y f", y=KY // 2, k=KX),
                                     yq.rearrange("p (k y f) -> p k y f", k=KX, y=KY // 2)).then_inc(yp_ready, 1)

            with pool.Fori(0, LAYERS - 1) as l:
                mixing(l)
                regroup(l)
            mixing(LAYERS - 1)
            regroup(LAYERS - 1)
            pool.wait_ge(b_free, B0 + LAYERS * BL - BF + JN * 2 + 2)
            fills = ((xt[64:65, :], 1.0), (rt[64:65, :], 1.0), (ones_m[:, :], 1.0), (xgt[64:128, :, :], 0.0),
                     (xgt[64:65, :, :], 1.0), (run[0][:, 0:64], 0.0), (run[1][:, 0:64], 0.0), (before[:, 0:64], 0.0))
            for n, (dst, value) in enumerate(fills):
                if n:
                    pool.wait_ge(ones_set, n)
                pool.memset(dst, value).then_inc(ones_set, 1)
            pool.wait_ge(slots_zeroed, 32)
            pool.wait_ge(slot_ready, 1)
            for k in range(2):
                for t in range(TT):
                    pool.indirect_dma_start(slots_x, bass.IndirectOffsetOnAxis(ap=slot[:, k * TT + t:k * TT + t + 1], axis=0),
                                            xn[:, t * 64:(t + 1) * 64], None).then_inc(scattered, 16)

            def send(i, s):
                pool.wait_ge(yg_ready, i * 2 + s + 3)
                pool.dma_start(slots_y[bass.ds((i * 2 + s) * 512, 512), :].rearrange("(k p) n -> p k n", k=4),
                               yg[:, s, :].rearrange("p (k n) -> p k n", k=4)).then_inc(yg_out[s], 16)

            with pool.Fori(0, GROUPS // 2) as i:
                send(i, 0)
                send(i, 1)
            for s in range(2):
                pool.wait_ge(yg_out[s], GROUPS // 2 * 16)
            for t in range(TT):
                for k in range(2):
                    pool.indirect_dma_start(ysel[k][:, t * 64:(t + 1) * 64], None, slots_y,
                                            bass.IndirectOffsetOnAxis(ap=slot[:, k * TT + t:k * TT + t + 1],
                                                                      axis=0)).then_inc(gathered[t // 8], 16)

        @block.scalar
        def _(act):
            act.wait_ge(consts_in, NCONST)

            def forward(l):
                def apply(j, c):
                    act.wait_ge(v_free, (l * JN + j) * NC + c + 1)
                    act.wait_ge(v_copied, (l * JN + j) * NC + c + 1)
                    act.activation(vch[:, c % 4, :], big[:, j, c * CW:(c + 1) * CW], ACT.Relu, bias=bn[:, 9:10],
                                   scale=bn[:, 8:9]).then_inc(v_ready, 1)

                def cy_out(j, c):
                    act.wait_ge(b_full, B0 + l * BL + BI + j * NC + c + 1)
                    act.activation(cy_.rearrange("p (f x) -> p f x", f=YF)[:, :, c * 8:(c + 1) * 8],
                                   PB[c % 2][:, 0:192].rearrange("p (x f) -> p f x", x=8), ACT.Copy).then_inc(b_free, 1)

                def x_out(j, h):
                    act.wait_ge(d_full, D0 + l * DL + DI + j * 2 + h + 1)
                    dst = xj.rearrange("p (k y r) -> p y k r", k=KX, y=KY)[:, h * 6:h * 6 + 6]
                    act.activation(dst, PD[h][:, 0:288].rearrange("p (y k r) -> p y k r", y=6, k=KX),
                                   ACT.Copy).then_inc(d_free, 1)

                def group(j, last):
                    for c in range(NC):
                        if c < NC - 3:
                            apply(j, c + 3)
                        elif not last:
                            apply(j + 1, c - (NC - 3))
                        if c == 0:
                            act.wait_ge(c_free, C0 + l * CL + CI + j * 4 + 2)
                        cy_out(j, c)
                    act.wait_ge(x_sent, ((l + 1) * JN + j) * XJ)
                    x_out(j, 0)
                    x_out(j, 1)

                for c in range(3):
                    apply(0, c)
                with act.Fori(0, JN - 1) as j:
                    group(j, False)
                group(JN - 1, True)

            def mixing(l):
                act.wait_ge(x_sent, (l + 1) * JN * XJ)

                def xs(k, h):
                    act.wait_ge(a_full, A0 + l * AL + k * 2 + h - 1)
                    src = xmode[:, :, bass.ds(k * YF + h * 12, 12)].rearrange("p b (m r) -> p m r b", r=2)
                    act.activation(xring[:, h, :, 0, :], src[:, :, 1, :], ACT.Copy, scale=-1.0).then_inc(exp_act, 1)
                    act.activation(xring[:, h, :, 1, :], src[:, :, 0, :], ACT.Copy).then_inc(exp_act, 1)
                    act.activation(xring[:, h, :, 2, :], src[:, :, 1, :], ACT.Copy).then_inc(exp_act, 1)

                def y_out(k, h):
                    act.wait_ge(a_full, A0 + l * AL + k * 2 + h + 1)
                    dst = ymode[:, :, bass.ds(k * YF + h * 12, 12)].rearrange("p b m -> p m b")
                    act.activation(dst, PA[h][:, 0:384].rearrange("p (m b) -> p m b", b=B), ACT.Copy).then_inc(a_free, 1)

                xs(0, 0)
                with act.Fori(0, KG - 1) as k:
                    xs(k, 1)
                    y_out(k, 0)
                    xs(k + 1, 0)
                    y_out(k, 1)
                xs(KG - 1, 1)
                y_out(KG - 1, 0)
                y_out(KG - 1, 1)

            def inverse(l):
                def z1_out(j, p):
                    if p == 0:
                        act.wait_ge(d_full, D0 + l * DL + j * 6)
                    act.wait_ge(c_full, C0 + l * CL + j * 6 + p + 1)
                    dst = z1.rearrange("p (x f) -> p x f", f=YF)[:, :, p * 4:p * 4 + 4]
                    act.activation(dst, PC[p % 2][:, 0:256].rearrange("p (x f) -> p x f", f=4),
                                   ACT.Copy).then_inc(c_free, 1)

                def u_out(j, c):
                    full, free, P, base = ((a_full, a_free, PA, A0 + l * AL + AM), (b_full, b_free, PB, B0 + l * BL))[c % 2]
                    act.wait_ge(full, base + j * 4 + c // 2 + 1)
                    act.activation(big[:, j, c * CW:(c + 1) * CW], P[(c // 2) % 2][:, :], ACT.Identity,
                                   bias=cur[:, 128:129]).then_inc(free, 1)

                for p in range(6):
                    z1_out(0, p)

                def group(j, last):
                    for c in range(NC):
                        u_out(j, c)
                        if c >= 4 and c < 7 and not last:
                            z1_out(j + 1, 2 * (c - 4))
                            z1_out(j + 1, 2 * (c - 4) + 1)
                with act.Fori(0, JN - 1) as j:
                    group(j, False)
                group(JN - 1, True)

            def norm(l):
                act.wait_ge(bn_sq, 2 * l + 1)
                act.activation(bn[:, 5:6], bn[:, 4:5], ACT.Sqrt).then_inc(bn_sq, 1)

            with act.Fori(0, LAYERS - 1) as l:
                mixing(l)
                act.wait_ge(cur_ready, l + 1)
                act.wait_ge(slots_zeroed, 32)
                inverse(l)
                norm(l)
                act.wait_ge(bn_done, l + 1)
                forward(l)
            mixing(LAYERS - 1)
            act.wait_ge(cur_ready, LAYERS)
            inverse(LAYERS - 1)
            norm(LAYERS - 1)
            act.wait_ge(ring_clear, LAYERS + 1)
            ht4 = ht.rearrange("p (j q x) -> p j x q", j=JN, q=QG)
            b0 = B0 + LAYERS * BL - BF
            with act.Fori(0, JN) as j:
                for h in range(2):
                    act.wait_ge(v_free, j * NC + (LAYERS - 1) * JN * NC + h * 4 + 8)
                    act.activation(ht4[:, j, h * 16:(h + 1) * 16, :], PB[h][:, 0:64].rearrange("p (x q) -> p x q", q=QG),
                                   ACT.Identity, bias=qbias[:, 0:1]).then_inc(b_free, 1)

            def deviation(n, scale, bias):
                act.wait_ge(var_ready, n)
                act.activation(red3[:, 0:bias], red2[:, 0:bias], ACT.Sqrt, scale=scale).then_inc(std_ready, 1)

            def xt_out(n):
                for b in range(4):
                    act.wait_ge(xt_full, n * 4 + b + 1)
                    act.activation(xt[0:64, b * 512:(b + 1) * 512], (PB + PC)[b][0:64, :], ACT.Copy).then_inc(xt_ready, 1)

            deviation(1, 1.0, TT)
            xt_out(0)
            for b in range(4):
                act.wait_ge(q_full, b + 1)
                act.activation(qt[:, b * 512:(b + 1) * 512], (PC + PD)[b][0:64, :], ACT.Copy).then_inc(qt_ready, 1)
            deviation(2, 1.0 / 3, 512)
            for b in range(2):
                act.wait_ge(proj_full, b + 1)
                act.activation(gl[:, b * 512:(b + 1) * 512], PA[b][:, :], ACT.Gelu).then_inc(gelu_ready, 1)
            deviation(3, 1.0, TT)
            xt_out(1)
            act.wait_ge(dif_ready, 1)
            act.activation(gate[:, 16:32], gate[:, 0:16], ACT.Exp).then_inc(exp_ready, 1)
            def turned(i, s):
                act.wait_ge(xg_turned, i * 2 + s + 1)
                act.activation(xgt[0:64, s, :], PA[s][0:64, :], ACT.Copy).then_inc(xgt_ready, 1)

            def units(i, s):
                act.wait_ge(hid_full, i * 2 + s + 1)
                act.activation(hid[:, s, :], PB[s][:, :], ACT.Relu).then_inc(hid_ready, 1)

            def group(i, s, last):
                if not last:
                    act.wait_ge(hid_full, i * 2 + s + 1)
                    turned(i + 1, s)
                if s == 0:
                    act.wait_ge(yg_full, i * 2 + 1)
                    units(i, 1)
                elif not last:
                    act.wait_ge(yg_full, i * 2 + 2)
                    units(i + 1, 0)

            turned(0, 0)
            turned(0, 1)
            units(0, 0)
            with act.Fori(0, GROUPS // 2 - 1) as i:
                group(i, 0, False)
                group(i, 1, False)
            group(GROUPS // 2 - 1, 0, True)

        @block.vector
        def _(dve):
            for s, n in ((a_free, 2), (b_free, 2), (c_free, 2), (d_free, 2), (v_free, 4), (v_copied, 4),
                         (yg_ready, 2), (hid_ready, 1), (yg_full, 1)):
                dve.sem_inc(s, n)

            def forward(l):
                with dve.Fori(0, JN) as j:
                    for c in range(NC):
                        dve.wait_ge(a_full, A0 + l * AL + AM + AI + j * NC + c + 1)
                        dve.wait_ge(b_full, B0 + l * BL + BI + j * NC + c - 3)
                        dve.tensor_copy(vt[:, c % 4, :], PA[c % 2][:, :]).then_inc(a_free, 1)
                        dve.tensor_copy(big[:, j, c * CW:(c + 1) * CW], vch[:, c % 4, :]).then_inc(v_copied, 1)
                    dve.wait_ge(d_full, D0 + l * DL + DI + j * 2)
                    for n in range(4):
                        dve.wait_ge(c_full, C0 + l * CL + CI + j * 4 + n + 1)
                        dve.tensor_copy(dx_[:, n * 384:(n + 1) * 384], PC[n % 2][:, 0:384]).then_inc(c_free, 1)

            def mixing(l):
                dve.wait_ge(ring_clear, l + 1)
                dve.wait_ge(w_in, (l + 1) * 64)
                dve.tensor_copy(cur[:, :], params[:, l, :]).then_inc(cur_ready, 1)
                with dve.Fori(0, KG) as k:
                    for h in range(2):
                        dve.wait_ge(a_full, A0 + l * AL + k * 2 + h - 1)
                        for g in range(QG):
                            r = slice(g * CH, (g + 1) * CH)
                            src = wmode[r, :, bass.ds(k * YF + h * 12, 12)].rearrange("p o m -> p m o")
                            dve.tensor_copy(wring[r, h, :, r], src).then_inc(exp_dve, 1)
                dve.wait_ge(exp_dve, (l + 1) * MSTEPS * QG)
                dve.sem_inc(w_used, 1)

            def first_mix():
                dve.wait_ge(a_full, A0 + AM)
                dve.tensor_copy(z1mix[96:103].rearrange("p s (k n) -> p (s k) n", k=4),
                                lmix[:, :].unsqueeze(1).to_broadcast([7, 16, 128])).then_inc(lmix_ready, 1)
                dve.tensor_copy(typix[0:96].rearrange("p s (k n) -> p (s k) n", k=4),
                                ty[:, :].unsqueeze(1).to_broadcast([96, 8, 256])).then_inc(lmix_ready, 1)

            def inverse(l):
                def yt_out(j, n):
                    if n == 0:
                        dve.wait_ge(c_full, C0 + l * CL + j * 6)
                    dve.wait_ge(d_full, D0 + l * DL + j * 6 + n + 1)
                    dve.tensor_copy(yt[:, n * 384:(n + 1) * 384], PD[n][0:96, 0:384]).then_inc(d_free, 1)

                def z1t_out(j, s):
                    dve.wait_ge(d_full, D0 + l * DL + j * 6 + 2 + s + 1)
                    dve.tensor_copy(z1t[:, s, :], PD[s % 2][0:96, :]).then_inc(d_free, 1)

                def take(j, c):
                    free, base = ((a_free, A0 + l * AL + AM), (b_free, B0 + l * BL))[c % 2]
                    dve.wait_ge(free, base + j * 4 + c // 2 + 3)
                    dve.bn_stats(stats[:, bass.ds(j * NC + c, 1), :],
                                 big[:, j, c * CW:(c + 1) * CW]).then_inc(stat_done, 1)

                yt_out(0, 0)
                yt_out(0, 1)

                def group(j, last):
                    z1t_out(j, 0)
                    z1t_out(j, 1)
                    take(j, 0)
                    z1t_out(j, 2)
                    take(j, 1)
                    z1t_out(j, 3)
                    take(j, 2)
                    if not last:
                        yt_out(j + 1, 0)
                    take(j, 3)
                    if not last:
                        yt_out(j + 1, 1)
                    for c in range(4, NC):
                        take(j, c)
                with dve.Fori(0, JN - 1) as j:
                    group(j, False)
                group(JN - 1, True)

            def norm(l):
                n = [0]

                def step(ins):
                    n[0] += 1
                    ins.then_inc(bn_chain, 1)
                    dve.wait_ge(bn_chain, l * 8 + n[0])
                dve.wait_ge(stat_done, (l + 1) * JN * NC)
                dve.sem_inc(dve_past, 1)
                dve.bn_aggr(bn[:, 0:2], stats[:, :, :]).then_inc(bn_mm, 1)
                dve.wait_ge(bn_mm, l * 4 + 2)
                step(dve.tensor_copy(bn[:, 2:3], PD[0][:, 0:1]))
                step(dve.tensor_tensor(bn[:, 3:4], bn[:, 0:1], bn[:, 2:3], ALU.subtract))
                step(dve.tensor_tensor(bn[:, 3:4], bn[:, 3:4], bn[:, 3:4], ALU.mult))
                dve.tensor_tensor(bn[:, 3:4], bn[:, 3:4], bn[:, 1:2], ALU.add).then_inc(bn_mm, 1)
                dve.wait_ge(bn_mm, l * 4 + 4)
                dve.tensor_scalar(bn[:, 4:5], PD[0][:, 1:2], EPS, None, ALU.add).then_inc(bn_sq, 1)
                dve.wait_ge(bn_sq, 2 * l + 2)
                step(dve.reciprocal(bn[:, 6:7], bn[:, 5:6]))
                step(dve.tensor_tensor(bn[:, 8:9], bn[:, 6:7], cur[:, 129:130], ALU.mult))
                step(dve.tensor_tensor(bn[:, 7:8], bn[:, 2:3], bn[:, 8:9], ALU.mult))
                step(dve.tensor_tensor(bn[:, 9:10], cur[:, 130:131], bn[:, 7:8], ALU.subtract))
                step(dve.tensor_copy(bn[:, 10:11], bn[:, 9:10]))
                dve.sem_inc(bn_done, 1)

            for n, (P, full, free, k) in enumerate(((PA, a_full, a_free, 0), (PA, a_full, a_free, 1),
                                                    (PB, b_full, b_free, 0), (PB, b_full, b_free, 1))):
                dve.wait_ge(full, k + 1)
                dst = xk.rearrange("p (f n a) -> p f n a", f=2 * KX, n=B // 2)[:, :, n * 4:(n + 1) * 4, :]
                dve.tensor_copy(dst, P[k][0:64, 0:384].rearrange("p (n f a) -> p f n a", n=4, f=2 * KX)).then_inc(free, 1)
            dve.wait_ge(c_full, 1)
            dve.tensor_copy(gsum, PC[0][:, 0:GM]).then_inc(c_free, 1)
            dve.wait_ge(c_full, 2)
            dve.tensor_copy(xs_, PC[1][0:96, 0:192].rearrange("p (m f) -> p m f", m=8)).then_inc(c_free, 1)
            dve.wait_ge(c_free, 4)
            dve.sem_inc(xs_ready, 1)
            for n in range(2 * KG):
                k, b = slice((n // 2) * YF, (n // 2 + 1) * YF), slice((n % 2) * 16, (n % 2 + 1) * 16)
                dve.wait_ge(d_full, n + 1)
                dve.tensor_tensor(xmode[:, b, k], PD[n % 2][:, 0:384].rearrange("p (b f) -> p b f", b=16),
                                  gsum[:, k].unsqueeze(1).to_broadcast([128, 16, YF]), ALU.add).then_inc(d_free, 1)
            dve.wait_ge(d_free, 14)
            dve.sem_inc(x_sent, JN * XJ)
            for n in range(2):
                dve.wait_ge(d_full, 13 + n)
                dve.tensor_copy(lmix[:, n * 64:(n + 1) * 64], PD[n][0:7, 0:64]).then_inc(d_free, 1)
            mixing(0)
            first_mix()
            inverse(0)
            norm(0)
            forward(0)
            with dve.Fori(1, LAYERS - 1) as l:
                mixing(l)
                inverse(l)
                norm(l)
                forward(l)
            mixing(LAYERS - 1)
            inverse(LAYERS - 1)
            norm(LAYERS - 1)
            dve.tensor_scalar(qscaled[:, :], qcol[:, :], bn[:, 8:9], None, ALU.mult).then_inc(q_prep, 1)
            dve.tensor_copy(shift[:, :], bn[:, 9:10].to_broadcast([128, 128])).then_inc(q_prep, 1)
            dve.wait_ge(q_prep, 3)
            dve.tensor_scalar(qbias[:, :], PD[0][:, 2:3], qb[:, 0:1], None, ALU.add).then_inc(ring_clear, 1)
            n0 = (LAYERS - 1) * JN * NC
            with dve.Fori(0, JN) as j:
                for c in range(NC):
                    dve.wait_ge(v_free, j * NC + n0 + c + 1)
                    dve.tensor_copy(vch[:, c % 4, :], big[:, j, c * CW:(c + 1) * CW]).then_inc(v_ready, 1)
            dve.wait_ge(b_free, B0 + LAYERS * BL - BF + JN * 2 + 2)

            n = [0]

            def step(ins):
                n[0] += 1
                ins.then_inc(tail_chain, 1)
                dve.wait_ge(tail_chain, n[0])

            def spread(a, k):
                return a.unsqueeze(2).to_broadcast([a.shape[0], a.shape[1], k])

            def grouped(a, k):
                return a.rearrange("p (g k) -> p g k", k=k)

            def normalise(src, dst, groups, k, scale, add, turn):
                width = groups * k
                s, c, w = grouped(src, k), grouped(xc[:, 0:width], k), grouped(sq[:, 0:width], k)
                step(dve.tensor_reduce(red[:, 0:groups], s, mybir.AxisListType.X, ALU.add))
                step(dve.tensor_scalar(red[:, 0:groups], red[:, 0:groups], 1.0 / k, None, ALU.mult))
                step(dve.tensor_tensor(c, s, spread(red[:, 0:groups], k), ALU.subtract))
                step(dve.tensor_tensor(w, c, c, ALU.mult))
                step(dve.tensor_reduce(red2[:, 0:groups], w, mybir.AxisListType.X, ALU.add))
                if scale is not None:
                    step(dve.tensor_scalar(red2[:, 0:groups], red2[:, 0:groups], scale, EPS, ALU.mult, ALU.add))
                dve.sem_inc(var_ready, 1)
                dve.wait_ge(std_ready, turn)
                if scale is None:
                    step(dve.tensor_scalar(red3[:, 0:groups], red3[:, 0:groups], add, None, ALU.add))
                step(dve.reciprocal(red3[:, 0:groups], red3[:, 0:groups]))
                step(dve.tensor_tensor(grouped(dst, k), c, spread(red3[:, 0:groups], k), ALU.mult))

            for b in range(2):
                dve.wait_ge(h_full, b + 1)
                step(dve.tensor_copy(res[:, b * 512:(b + 1) * 512], PA[b][:, :]))
            normalise(res, xn, TT, 64, 1.0 / 64, 0.0, 1)
            dve.sem_inc(xn_ready, 1)
            for b in range(4):
                dve.wait_ge(kv_full, b + 1)
                step(dve.tensor_copy(kv[:, b * 512:(b + 1) * 512], (PA + PB)[b][:, :]))
            normalise(kv, kv, 512, 4, None, EPS, 2)
            dve.wait_ge(tail_in, 15 * 16)
            kv3 = kv.rearrange("p (t n) -> p t n", t=TT)
            for n0_, op in ((0, ALU.mult), (1, ALU.add)):
                wb = lnwb[:, n0_ * 128:(n0_ + 1) * 128].unsqueeze(1).to_broadcast([128, TT, 128])
                step(dve.tensor_tensor(kv3, kv3, wb, op))
            dve.sem_inc(kv_ready, 1)
            for q in range(QG):
                dve.wait_ge(kvm_full, q + 1)
                step(dve.tensor_tensor(grouped(kvm[:, q * 512:(q + 1) * 512], 64), grouped((PA + PB)[q][0:64, :], 64),
                                       mask.unsqueeze(1).to_broadcast([64, JN, 64]), ALU.mult))
            dve.sem_inc(kvm_ready, 1)
            for b in range(4):
                dve.wait_ge(att_full, b + 1)
                dve.tensor_tensor(rt[0:64, b * 512:(b + 1) * 512], (PC + PD)[b][0:64, :], xt[0:64, b * 512:(b + 1) * 512],
                                  ALU.add).then_inc(rt_ready, 1)
            step(dve.tensor_tensor(res, res, xn, ALU.add))
            dve.wait_ge(gelu_ready, 2)
            step(dve.tensor_tensor(res, res, gl, ALU.add))
            normalise(res, xn, TT, 64, 1.0 / 64, 0.0, 3)
            dve.sem_inc(xn_ready, 1)
            for b in range(2):
                dve.wait_ge(lg_full, b + 1)
                step(dve.tensor_copy(lg[:, b * 512:(b + 1) * 512], PA[b][:, :]))
            for t in range(TT):
                top = dve.max(mx[:, t * 8:t * 8 + 8], lg[:, t * 64:t * 64 + 64])
            step(top)
            for t in range(TT):
                top = dve.max_index(ixs[:, t * 8:t * 8 + 8], mx[:, t * 8:t * 8 + 8], lg[:, t * 64:t * 64 + 64])
            step(top)
            step(dve.tensor_copy(ixf, ixs[:, :]))
            m8, i8 = grouped(mx, 8), grouped(ixf, 8)
            it = iota.unsqueeze(1).to_broadcast([128, TT, 64])
            f3, s3, c3 = grouped(first, 64), grouped(second, 64), grouped(comb, 64)
            step(dve.tensor_tensor(f3, it, i8[:, :, 0:1].to_broadcast([128, TT, 64]), ALU.is_equal))
            step(dve.tensor_tensor(s3, it, i8[:, :, 1:2].to_broadcast([128, TT, 64]), ALU.is_equal))
            step(dve.tensor_tensor(chosen, first, second, ALU.add))
            dve.sem_inc(chosen_ready, 1)
            step(dve.tensor_tensor(gate[:, 0:16], m8[:, :, 1], m8[:, :, 0], ALU.subtract))
            dve.sem_inc(dif_ready, 1)
            dve.wait_ge(ones_set, 8)
            dve.wait_ge(tot_full, 1)
            for t in range(TT):
                step(dve.tensor_tensor(before[:, (t + 1) * 64:(t + 2) * 64], before[:, t * 64:(t + 1) * 64],
                                       PC[t // 8][:, (t % 8) * 64:(t % 8 + 1) * 64], ALU.add))
            step(dve.tensor_scalar(base, before[:, TT * 64:(TT + 1) * 64], 1.0 / 128, None, ALU.mult))
            step(dve.tensor_tensor(grouped(sq[:, 0:1024], 16), spread(base, 16),
                                   iota[:, 0:16].unsqueeze(1).to_broadcast([128, 64, 16]), ALU.is_gt))
            step(dve.tensor_reduce(ntile, grouped(sq[:, 0:1024], 16), mybir.AxisListType.X, ALU.add))
            step(dve.tensor_copy(run[0][:, 64:128], ntile))
            for k in range(6):
                a, b = run[k % 2], run[(k + 1) % 2]
                step(dve.tensor_tensor(b[:, 64:128], a[:, 64:128], a[:, 64 - 2 ** k:128 - 2 ** k], ALU.add))
            ends = run[0][:, 64:128]
            step(dve.tensor_scalar(sq[:, 0:64], ends, pid[:, 0:1], None, ALU.is_le))
            step(dve.tensor_reduce(texf, sq[:, 0:64], mybir.AxisListType.X, ALU.add))
            step(dve.tensor_scalar(texf, texf, float(EXPERTS - 1), None, ALU.min))
            dve.sem_inc(texf_ready, 1)
            step(dve.tensor_tensor(base, ends, ntile, ALU.subtract))
            step(dve.tensor_scalar(base, base, 128.0, None, ALU.mult))
            for b in range(2):
                step(dve.tensor_tensor(pos_[:, b * 512:(b + 1) * 512], PB[b][:, :], before[:, b * 512:(b + 1) * 512], ALU.add))
            dve.wait_ge(texr_full, 1)
            dve.tensor_copy(texp[0:1, :], PD[0][0:1, 0:128]).then_inc(texp_ready, 1)
            step(dve.tensor_tensor(grouped(pos_, 64), grouped(pos_, 64), base.unsqueeze(1).to_broadcast([128, TT, 64]), ALU.add))
            for n_, hot in enumerate((first, second)):
                step(dve.tensor_tensor(sq[:, 0:1024], pos_, hot, ALU.mult))
                step(dve.tensor_reduce(slotf[:, n_ * TT:(n_ + 1) * TT], grouped(sq[:, 0:1024], 64), mybir.AxisListType.X, ALU.add))
            dve.tensor_copy(slot[:, :], slotf).then_inc(slot_ready, 1)
            dve.wait_ge(exp_ready, 1)
            step(dve.tensor_scalar(gate[:, 32:48], gate[:, 16:32], 1.0, None, ALU.add))
            step(dve.reciprocal(gate[:, 48:64], gate[:, 32:48]))
            step(dve.tensor_tensor(gate[:, 32:48], gate[:, 16:32], gate[:, 48:64], ALU.mult))
            step(dve.tensor_tensor(f3, f3, spread(gate[:, 48:64], 64), ALU.mult))
            step(dve.tensor_tensor(s3, s3, spread(gate[:, 32:48], 64), ALU.mult))
            step(dve.tensor_tensor(comb, first, second, ALU.add))
            dve.sem_inc(comb_ready, 1)

            def outputs(i, s, wait):
                dve.wait_ge(yg_full, i * 2 + s + 2)
                if wait:
                    dve.wait_ge(yg_out[s], i * 16)
                dve.tensor_copy(yg[:, s, :], PC[s][:, 0:256]).then_inc(yg_ready, 1)
            outputs(0, 0, False)
            outputs(0, 1, False)
            with dve.Fori(1, GROUPS // 2) as i:
                outputs(i, 0, True)
                outputs(i, 1, True)
            for b in range(4):
                dve.wait_ge(ct_full, b + 1)
                dve.tensor_copy(ct[:, b * 512:(b + 1) * 512], (PB + PC)[b][0:64, :]).then_inc(ct_ready, 1)
            for b in range(2):
                dve.wait_ge(bias_full, b + 1)
                s_ = slice(b * 512, (b + 1) * 512)
                step(dve.tensor_tensor(acc[:, s_], PD[b][:, :], res[:, s_], ALU.add))
            for b in range(2):
                s_ = slice(b * 512, (b + 1) * 512)
                dve.wait_ge(gathered[b], 16 * 16)
                for k, g0 in ((0, 48), (1, 32)):
                    y = grouped(ysel[k][:, s_], 64)
                    step(dve.tensor_tensor(y, y, spread(gate[:, g0 + b * 8:g0 + b * 8 + 8], 64), ALU.mult))
                    step(dve.tensor_tensor(acc[:, s_], acc[:, s_], ysel[k][:, s_], ALU.add))
                dve.sem_inc(sum_ready, 1)

        @block.tensor
        def _(pe):
            pe.wait_ge(first_in, NFIRST)
            for n in range(B // 2):
                P, full = ((PA, a_full), (PB, b_full))[n // 8]
                mm = pe.matmul(P[(n // 4) % 2][0:64, (n % 4) * 96:(n % 4 + 1) * 96], xin[:, n, :], f1, start=True, stop=True)
                if n % 4 == 3:
                    mm.then_inc(full, 1)
            pe.matmul(PC[0][:, 0:GM], liftg[:, :], gspec, start=True, stop=True).then_inc(c_full, 1)
            pe.wait_ge(a_free, 4)
            pe.wait_ge(b_free, 4)
            for m in range(8):
                for a in range(2):
                    o = a * KX * B + m * 96
                    mm = pe.matmul(PC[1][0:96, m * YF:(m + 1) * YF], xk[:, o:o + 96], f2[:, a, :], start=(a == 0),
                                   stop=(a == 1))
            mm.then_inc(c_full, 1)
            pe.wait_ge(rows_in, 8 * 16)
            for n in range(2 * KG):
                pe.wait_ge(d_free, n + 1)
                pe.matmul(PD[n % 2][:, 0:384], liftx[:, :], xrow[:, n * 384:(n + 1) * 384], start=True,
                          stop=True).then_inc(d_full, 1)
            pe.wait_ge(consts_in, NCONST)
            for n in range(2):
                pe.wait_ge(d_free, 13 + n)
                pe.matmul(PD[n][0:7, 0:64], liftt[:, :], params[:, 0, n * 64:(n + 1) * 64], start=True,
                          stop=True).then_inc(d_full, 1)

            def forward(l):
                fa, fb, fc, fd = A0 + l * AL + AM + AI, B0 + l * BL + BI, C0 + l * CL + CI, D0 + l * DL + DI

                def turn(j, c):
                    pe.wait_ge(v_ready, (l * JN + j) * NC + c + 1)
                    pe.wait_ge(a_free, fa + j * NC + c + 1)
                    for n in range(4):
                        last = pe.transpose(PA[c % 2][:, n * 128:(n + 1) * 128], vch[:, c % 4, n * 128:(n + 1) * 128],
                                            ident[:, :])
                    last.then_inc(a_full, 1)

                def rows(j, c):
                    pe.wait_ge(a_free, fa + j * NC + c + 3)
                    pe.wait_ge(b_free, fb + j * NC + c + 1)
                    for n in range(4):
                        last = pe.matmul(PB[c % 2][:, n * 48:(n + 1) * 48], vt[:, c % 4, n * 128:(n + 1) * 128], fy[:, :],
                                         start=True, stop=True)
                    last.then_inc(b_full, 1)
                    pe.wait_ge(a_full, fa + j * NC + c + 1)
                    pe.sem_inc(v_free, 1)

                def columns(j):
                    pe.wait_ge(b_free, fb + j * NC + NC + 2)
                    for n in range(4):
                        pe.wait_ge(c_free, fc + j * 4 + n + 1)
                        for k in range(3):
                            last = pe.transpose(PC[n % 2][:, k * 128:(k + 1) * 128], cy_[:, (n * 3 + k) * 128:(n * 3 + k + 1) * 128],
                                                ident[:, :])
                        last.then_inc(c_full, 1)
                    for h in range(2):
                        pe.wait_ge(c_free, fc + j * 4 + 2 * h + 4)
                        pe.wait_ge(d_free, fd + j * 2 + h + 1)
                        for k in range(6):
                            ky = h * 6 + k
                            last = pe.matmul(PD[h][:, k * 48:(k + 1) * 48], dx_[:, ky * 128:(ky + 1) * 128], fx[:, :],
                                             start=True, stop=True)
                        last.then_inc(d_full, 1)

                def group(j, last):
                    for c in range(NC):
                        rows(j, c)
                        if c < NC - 2:
                            turn(j, c + 2)
                        elif not last:
                            turn(j + 1, c - (NC - 2))
                    columns(j)
                turn(0, 0)
                turn(0, 1)
                with pe.Fori(0, JN - 1) as j:
                    group(j, False)
                group(JN - 1, True)

            def mixing(l):
                with pe.Fori(0, KG) as k:
                    for h in range(2):
                        n = k * 2 + h
                        pe.wait_ge(exp_dve, (l * MSTEPS + n) * QG + QG)
                        pe.wait_ge(exp_act, (l * MSTEPS + n) * 3 + 3)
                        pe.wait_ge(a_free, A0 + l * AL + n + 1)
                        for m in range(MK):
                            o = PA[h][:, m * 64:(m + 1) * 64]
                            pe.matmul(o, wring[:, h, 2 * m, :], xring[:, h, m, 1:3, :].rearrange("p t b -> p (t b)"),
                                      start=True, stop=False)
                            last = pe.matmul(o, wring[:, h, 2 * m + 1, :],
                                             xring[:, h, m, 0:2, :].rearrange("p t b -> p (t b)"), start=False, stop=True)
                        last.then_inc(a_full, 1)

            def inverse(l, first):
                dbase = D0 + l * DL

                def spectra(j, n):
                    if n == 0:
                        pe.wait_ge(yp_ready, l * JN + j + 1)
                    pe.wait_ge(d_free, dbase + j * 6 + n + 1)
                    for k in range(3):
                        last = pe.transpose(PD[n][0:96, k * 128:(k + 1) * 128], yp[:, (n * 3 + k) * 96:(n * 3 + k + 1) * 96], ident[:, :])
                    last.then_inc(d_full, 1)

                def columns(j, p):
                    pe.wait_ge(d_free, dbase + j * 6 + p // 3 + 3)
                    pe.wait_ge(c_free, C0 + l * CL + j * 6 + p + 1)
                    pe.matmul(PC[p % 2][:, 0:256], yt[:, p * 128:(p + 1) * 128], tx[:, :], start=True,
                              stop=True).then_inc(c_full, 1)

                def turn(j, s):
                    pe.wait_ge(c_free, C0 + l * CL + j * 6 + 8)
                    pe.wait_ge(d_free, dbase + j * 6 + 2 + s + 1)
                    for k in range(4):
                        g = s * 4 + k
                        last = pe.transpose(PD[s % 2][0:96, k * 128:(k + 1) * 128], z1[:, g * 96:(g + 1) * 96], ident[:, :])
                    last.then_inc(d_full, 1)

                def rows(j, c):
                    full, free, P, base = ((a_full, a_free, PA, A0 + l * AL + AM), (b_full, b_free, PB, B0 + l * BL))[c % 2]
                    s = c // 2
                    pe.wait_ge(d_free, dbase + j * 6 + 2 + s + 3)
                    pe.wait_ge(free, base + j * 4 + s + 1)
                    o = P[s % 2]
                    if first:
                        if c % 2 == 0:
                            pe.wait_ge(pix_in[s % 2], j * 64 + (s // 2) * 32 + 32)
                    else:
                        pe.matmul(o[:, :], cur[:, 0:128], big[:, j, c * CW:(c + 1) * CW], start=True, stop=False)
                    for k in range(2):
                        t = (c % 2) * 2 + k
                        half = o[:, k * 256:(k + 1) * 256]
                        if first:
                            last = pe.matmul(half, z1mix[:, s, t * 128:(t + 1) * 128],
                                             typix[:, s % 2, t * 256:(t + 1) * 256], start=(k == 0), stop=(k == 1))
                        else:
                            last = pe.matmul(half, z1t[:, s, t * 128:(t + 1) * 128], ty[:, :], start=False, stop=(k == 1))
                    last.then_inc(full, 1)

                def group(j, last):
                    turn(j, 0)
                    turn(j, 1)
                    rows(j, 0)
                    turn(j, 2)
                    rows(j, 1)
                    turn(j, 3)
                    rows(j, 2)
                    if not last:
                        spectra(j + 1, 0)
                    rows(j, 3)
                    if not last:
                        spectra(j + 1, 1)
                    for c in range(4, NC):
                        rows(j, c)
                        if c < 7 and not last:
                            columns(j + 1, 2 * (c - 4))
                            columns(j + 1, 2 * (c - 4) + 1)

                pe.wait_ge(cur_ready, l + 1)
                if first:
                    pe.wait_ge(lmix_ready, 2)
                else:
                    pe.wait_ge(v_copied, l * JN * NC + 4)
                spectra(0, 0)
                spectra(0, 1)
                for p in range(6):
                    columns(0, p)
                with pe.Fori(0, JN - 1) as j:
                    group(j, False)
                group(JN - 1, True)

            def norm(l):
                pe.wait_ge(bn_mm, l * 4 + 1)
                pe.matmul(PD[0][:, 0:1], avg[:, :], bn[:, 0:1], start=True, stop=True).then_inc(bn_mm, 1)
                pe.wait_ge(bn_mm, l * 4 + 3)
                pe.matmul(PD[0][:, 1:2], avg[:, :], bn[:, 3:4], start=True, stop=True).then_inc(bn_mm, 1)

            mixing(0)
            inverse(0, True)
            norm(0)
            forward(0)
            with pe.Fori(1, LAYERS - 1) as l:
                mixing(l)
                inverse(l, False)
                norm(l)
                forward(l)
            mixing(LAYERS - 1)
            inverse(LAYERS - 1, False)
            norm(LAYERS - 1)
            pe.wait_ge(q_prep, 2)
            n0, b0 = (LAYERS - 1) * JN * NC, B0 + LAYERS * BL - BF
            pe.matmul(PD[0][:, 2:3], shift, qcol[:, 0:1], start=True, stop=True).then_inc(q_prep, 1)
            with pe.Fori(0, JN) as j:
                for c in range(NC):
                    pe.wait_ge(v_ready, j * NC + n0 + c + 1)
                    if c % 4 == 0:
                        pe.wait_ge(b_free, j * 2 + b0 + c // 4 + 1)
                    for n in range(4):
                        k = (c % 4) * 4 + n
                        last = pe.matmul(PB[c // 4][:, k * 4:k * 4 + 4], vch[:, c % 4, n * 128:(n + 1) * 128],
                                         qscaled[:, :], start=True, stop=True)
                    last.then_inc(v_free, 1)

            pe.wait_ge(b_free, B0 + LAYERS * BL - BF + JN * 2 + 2)
            for j in range(JN):
                last = pe.transpose(PA[j // 4][:, (j % 4) * 128:(j % 4 + 1) * 128], ht[:, j * 128:(j + 1) * 128], ident[:, :])
                if j % 4 == 3:
                    last.then_inc(h_full, 1)

            def tokens_to_columns(src, banks_, full):
                for t in range(TT):
                    last = pe.transpose(banks_[t // 4][0:64, (t % 4) * 128:(t % 4 + 1) * 128], src[:, t * 64:(t + 1) * 64],
                                        ident[:, :])
                    if t % 4 == 3:
                        last.then_inc(full, 1)

            pe.wait_ge(xn_ready, 1)
            tokens_to_columns(xn, PB + PC, xt_full)
            pe.wait_ge(tail_in, 15 * 16)
            pe.wait_ge(ones_set, 2)
            pe.wait_ge(xt_ready, 4)
            for t in range(TT):
                last = pe.matmul((PA + PB)[t // 4][:, (t % 4) * 128:(t % 4 + 1) * 128], xt[:, t * 128:(t + 1) * 128],
                                 wqkv[:, 64:192], start=True, stop=True)
                if t % 4 == 3:
                    last.then_inc(kv_full, 1)
            for b in range(4):
                pe.matmul((PC + PD)[b][0:64, :], wqkv[:, 0:64], xt[:, b * 512:(b + 1) * 512], start=True,
                          stop=True).then_inc(q_full, 1)
            pe.wait_ge(kv_ready, 1)
            for q in range(QG):
                r = slice(q * 32, (q + 1) * 32)
                for j in range(JN):
                    for x2 in range(2):
                        o = (j * 2 + x2) * 128
                        last = pe.matmul((PA + PB)[q][0:64, j * 64:(j + 1) * 64], kv[r, o:o + 64], kv[r, o + 64:o + 128],
                                         start=(x2 == 0), stop=(x2 == 1))
                last.then_inc(kvm_full, 1)
            pe.wait_ge(kvm_ready, 1)
            pe.wait_ge(qt_ready, 4)
            for j in range(JN):
                for q in range(QG):
                    qv = qt[:, j * 256:(j + 1) * 256].rearrange("p (x n) -> p x n", x=2)[:, :, q * 32:(q + 1) * 32]
                    o = (PC + PD)[j // 2][0:64, (j % 2) * 256:(j % 2 + 1) * 256]
                    last = pe.matmul(o.rearrange("p (x n) -> p x n", x=2)[:, :, q * 32:(q + 1) * 32],
                                     kvm[:, q * 512 + j * 64:q * 512 + (j + 1) * 64], qv, start=True, stop=True)
                if j % 2 == 1:
                    last.then_inc(att_full, 1)
            for t in range(TT):
                if t % 4 == 0:
                    pe.wait_ge(rt_ready, t // 4 + 1)
                last = pe.matmul(PA[t // 8][:, (t % 8) * 64:(t % 8 + 1) * 64], rt[:, t * 128:(t + 1) * 128], wproj[:, :],
                                 start=True, stop=True)
                if t % 8 == 7:
                    last.then_inc(proj_full, 1)
            pe.wait_ge(xn_ready, 2)
            tokens_to_columns(xn, PB + PC, xt_full)
            pe.wait_ge(xt_ready, 8)
            for t in range(TT):
                last = pe.matmul(PA[t // 8][:, (t % 8) * 64:(t % 8 + 1) * 64], xt[:, t * 128:(t + 1) * 128], wroute[:, :],
                                 start=True, stop=True)
                if t % 8 == 7:
                    last.then_inc(lg_full, 1)
            pe.wait_ge(chosen_ready, 1)
            pe.wait_ge(ones_set, 8)
            for b in range(2):
                pe.matmul(PC[b][:, :], ones_m[:, :], chosen[:, b * 512:(b + 1) * 512], start=True, stop=True)
            for b in range(2):
                last = pe.matmul(PB[b][:, :], tri[:, :], chosen[:, b * 512:(b + 1) * 512], start=True, stop=True)
            last.then_inc(tot_full, 1)
            pe.wait_ge(texf_ready, 1)
            pe.matmul(PD[0][0:1, 0:128], texf[:, 0:1], ident[:, :], start=True, stop=True).then_inc(texr_full, 1)

            def turn(i, s):
                pe.wait_ge(xg_in[s], i * 16 + 16)
                pe.sem_inc(pe_past, 1)
                for k in range(4):
                    last = pe.transpose(PA[s][0:64, k * 128:(k + 1) * 128], xg[:, s, k * 64:(k + 1) * 64], ident[:, :])
                last.then_inc(xg_turned, 1)

            def hidden(i, s):
                pe.wait_ge(wt_in[s], i * 64 + 64)
                pe.wait_ge(xgt_ready, i * 2 + s + 1)
                for k in range(4):
                    last = pe.matmul(PB[s][:, k * 128:(k + 1) * 128], wt[:, s, k, 64:192], xgt[:, s, k * 128:(k + 1) * 128],
                                     start=True, stop=True)
                last.then_inc(hid_full, 1)

            def outputs(i, s):
                pe.wait_ge(hid_ready, i * 2 + s + 2)
                for k in range(4):
                    last = pe.matmul(PC[s][:, k * 64:(k + 1) * 64], hid[:, s, k * 128:(k + 1) * 128], wt[:, s, k, 0:64],
                                     start=True, stop=True)
                last.then_inc(yg_full, 1)

            def group(i, s, last):
                if not last:
                    pe.wait_ge(xgt_ready, i * 2 + s + 1)
                    turn(i + 1, s)
                if s == 0 or not last:
                    pe.wait_ge(hid_ready, i * 2 + s + 1)
                    hidden(i + s, 1 - s)
                pe.wait_ge(yg_ready, i * 2 + s + 1)
                outputs(i, s)
            turn(0, 0)
            turn(0, 1)
            hidden(0, 0)
            with pe.Fori(0, GROUPS // 2 - 1) as i:
                group(i, 0, False)
                group(i, 1, False)
            group(GROUPS // 2 - 1, 0, True)
            group(GROUPS // 2 - 1, 1, True)
            pe.wait_ge(comb_ready, 1)
            pe.wait_ge(yg_ready, GROUPS + 2)
            tokens_to_columns(comb, PB + PC, ct_full)
            pe.wait_ge(ct_ready, 4)
            for t in range(TT):
                last = pe.matmul(PD[t // 8][:, (t % 8) * 64:(t % 8 + 1) * 64], ct[:, t * 128:(t + 1) * 128], b2all[:, :],
                                 start=True, stop=True)
                if t % 8 == 7:
                    last.then_inc(bias_full, 1)


_INS = ['x', 'L0_tok_p_w', 'L0_tok_p_b', 'L0_tok_fw1', 'L0_tok_fw2', 'L0_tok_w_w', 'L0_tok_w_b', 'L0_tok_bn_g',
        'L0_tok_bn_b', 'L0_tok_q_w', 'L0_tok_q_b', 'L0_attn_W_qkv', 'L0_attn_b_qkv', 'L0_attn_kln_w', 'L0_attn_kln_b',
        'L0_attn_vln_w', 'L0_attn_vln_b', 'L0_attn_W_proj', 'L0_attn_b_proj', 'L0_ffn_Wr', 'L0_ffn_br', 'L0_ffn_W1',
        'L0_ffn_b1', 'L0_ffn_W2', 'L0_ffn_b2']


def kernel(**inputs):
    import concourse.bacc as _bacc
    from concourse import mybir as _mybir
    from concourse.bass_utils import run_bass_kernel_spmd as _run

    nc = _bacc.Bacc("TRN2", target_bir_lowering=False, num_devices=1)
    arrays, args = {}, []

    def give(name, a):
        arrays[name] = a
        args.append(nc.dram_tensor(name, a.shape, _mybir.dt.from_np(a.dtype), kind="ExternalInput").ap())

    for name in _INS:
        a = np.ascontiguousarray(inputs[name])
        if name in ('L0_tok_p_b', 'L0_tok_w_b', 'L0_tok_bn_b'):
            continue
        if name == 'L0_tok_p_w':
            a = np.concatenate([a, np.asarray(inputs['L0_tok_p_b'])[None]])
        if name == 'L0_tok_bn_g':
            a = np.stack([np.asarray(inputs['L0_tok_w_b']), a, np.asarray(inputs['L0_tok_bn_b'])], axis=-1)
        if name in ('L0_tok_fw1', 'L0_tok_fw2'):
            a = a.reshape(LAYERS, CH, CH, 12 * KY * 2)
        if name == 'L0_attn_W_qkv':
            a = np.ascontiguousarray(a.reshape(16, 3, 4, 64).transpose(3, 1, 0, 2).reshape(64, 192))
        if name == 'L0_attn_b_qkv':
            a = np.ascontiguousarray(a.reshape(16, 3, 4).transpose(1, 0, 2).reshape(192))
        if name == 'L0_attn_W_proj':
            a = np.ascontiguousarray(a.T)
        if name in ('L0_ffn_b1', 'L0_ffn_W2'):
            continue
        if name == 'L0_ffn_W1':
            w = np.zeros((EXPERTS, 128, 192), a.dtype)
            w[:, :, 0:64], w[:, 0:64, 64:192] = np.asarray(inputs['L0_ffn_W2']), a
            w[:, 64, 64:192], a = np.asarray(inputs['L0_ffn_b1']), w
        give("in_" + name, a)
    for name, a in constants().items():
        give("const_" + name, a)
    for name in ("slots_x", "slots_y"):
        args.append(nc.dram_tensor(name, (SLOT_TILES * 128, 64), _mybir.dt.float32, kind="Internal").ap())
    args.append(nc.dram_tensor("out_0", (B, S, S), _mybir.dt.float32, kind="ExternalOutput").ap())
    vit_tower(nc, *args)
    r = _run(nc, [arrays], core_ids=[0])
    return r.results[0]["out_0"]
```

```python
import concourse.bass as bass
from concourse import mybir
from contextlib import ExitStack
import numpy as np

B, S, CH, LAYERS = 32, 64, 32, 4
QG, JN = 4, 8
KX, KY = 24, 12
KG = KX // QG
GM = KG * KY * 2
NPIX = S * S
CW = 512
NC = NPIX // CW
YF = KY * 2
XB = 4
MK = 6
MSTEPS = KG * KY // MK
EPS = 1e-5
EXPERTS, TOKENS = 64, B * S
SLOT_TILES = 2 * TOKENS // 128 + EXPERTS
PCOLS = 128 + 3


def constants():
    f = np.float64
    two_pi = 2 * np.pi / S
    y, ky = np.arange(S, dtype=f), np.arange(KY, dtype=f)
    kx = np.array(list(range(12)) + list(range(52, 64)), dtype=f)
    cy, sy = np.cos(two_pi * np.outer(y, ky)), np.sin(two_pi * np.outer(y, ky))
    cx, sx = np.cos(two_pi * np.outer(y, kx)), np.sin(two_pi * np.outer(y, kx))
    fy = np.zeros((2, S, 2, KY, 2), f)
    for a in range(2):
        fy[a, :, a, :, 0], fy[a, :, a, :, 1] = cy, -sy
    fx = np.zeros((2, S, KX, 2), f)
    fx[0, :, :, 0], fx[1, :, :, 0] = cx, sx
    fx[0, :, :, 1], fx[1, :, :, 1] = -sx, cx
    tx = np.zeros((KX, 2, 2, S, 2, 2), f)
    for a in range(2):
        tx[:, a, 0, :, a, 0], tx[:, a, 1, :, a, 0] = cx.T / S, -sx.T / S
        tx[:, a, 0, :, a, 1], tx[:, a, 1, :, a, 1] = sx.T / S, cx.T / S
    wk = np.where(ky == 0, 1.0, 2.0)[:, None] / S
    ty = np.zeros((XB, KY, 2, XB, S), f)
    for a in range(XB):
        ty[a, :, 0, a], ty[a, :, 1, a] = wk * cy.T, -wk * sy.T
    avg = np.kron(np.full((QG, QG), 1.0 / QG), np.eye(CH))
    f1 = np.zeros((2, S, 2, KX, 2), f)
    for a in range(2):
        f1[a, :, 0, :, a], f1[a, :, 1, :, a] = cx, -sx
    f2 = np.zeros((2, S, KY, 2), f)
    f2[0, :, :, 0], f2[0, :, :, 1], f2[1, :, :, 0], f2[1, :, :, 1] = cy, -sy, sy, cy
    lin = np.linspace(0.0, 1.0, S, dtype=np.float32)
    fft = np.exp(-1j * two_pi * np.outer(kx, y)), np.exp(-1j * two_pi * np.outer(y, ky))
    gs = np.zeros((QG, 3, KG, KY, 2), f)
    for n, (u, v) in enumerate(((lin, np.ones(S)), (np.ones(S), lin), (np.ones(S), np.ones(S)))):
        z = (fft[0] @ np.outer(u, v) @ fft[1]).reshape(QG, KG, KY)
        gs[:, n, :, :, 0], gs[:, n, :, :, 1] = z.real, z.imag
    grid = np.stack([np.repeat(lin, S), np.tile(lin, S), np.ones(NPIX, np.float32)])
    mask = np.kron(np.eye(16), np.ones((4, 4))) / S
    iota = np.tile(np.arange(64), (128, 1))
    tri = np.triu(np.ones((128, 128)), 1)
    pid = np.arange(128)[:, None]
    out = dict(tri=tri, pid=pid, fxy=np.concatenate([fx.reshape(128, 48), fy.reshape(128, 48)], axis=1), tx=tx.reshape(96, 256), ty=ty.reshape(96, 256),
               ident=np.eye(128), avg=avg, grid=grid, mask=mask, iota=iota,
               f1=f1.reshape(128, 96), f2=f2.reshape(128, 24), gs=gs.reshape(12, GM))
    return {k: np.ascontiguousarray(v.astype(np.float32)) for k, v in out.items()}


def vit_tower(nc, x, lift_w, fw1, fw2, w_w, scales, q_w, q_b, W_qkv, b_qkv, kln_w, kln_b, vln_w, vln_b,
              W_proj, b_proj, Wr, br, wexp, b2, c_tri, c_pid, c_fxy, c_tx, c_ty, c_ident, c_avg, c_grid, c_mask, c_iota,
              c_f1, c_f2, c_gs,
              slots_x, slots_y, pixels_out, spectra_x, spectra_y, out):
    fp32, bf16 = mybir.dt.float32, mybir.dt.bfloat16
    ALU = mybir.AluOpType
    ACT = mybir.ActivationFunctionType
    ctx = ExitStack()
    with ctx:
        def sb(name, shape, dt=fp32):
            return ctx.enter_context(nc.sbuf_tensor(name, shape, dt))

        def sem(name):
            return ctx.enter_context(nc.semaphore(name))

        big = sb("big", [128, JN, NPIX])
        modes = sb("modes", [128, B * GM])
        wmode = sb("wmode", [128, CH, GM])
        work = sb("work", [128, 9280])
        xmode = modes[:, :].rearrange("p (b f) -> p b f", b=B)
        z1t = modes[0:96, 0:2048].rearrange("p (s n) -> p s n", s=4)
        vch = work[:, 0:2048].rearrange("p (s n) -> p s n", s=4)
        vt = work[:, 2048:4096].rearrange("p (s n) -> p s n", s=4)
        cy_ = [work[:, 4096:5632], work[:, 7168:8704]]
        dx_ = work[:, 5632:7168]
        xj = work[:, 8704:9280]
        xrow = work[:, 0:4608]
        xin = work[:, 4608:5632].rearrange("p (n y) -> p n y", n=B // 2)
        xk = work[0:64, 5632:7168]
        xs_ = work[0:96, 7168:7360].rearrange("p (m f) -> p m f", m=8)
        gsum = work[:, 7360:7504]
        f1, f2 = work[:, 7504:7600], work[0:64, 7600:7648].rearrange("p (a f) -> p a f", a=2)
        gspec = work[0:12, 7648:7792]
        typix = modes[0:103, 2048:4096].rearrange("p (s n) -> p s n", s=2)
        z1mix = modes[0:103, 0:2048].rearrange("p (s n) -> p s n", s=4)
        ymode = work[:, 0:4608].rearrange("p (b f) -> p b f", b=B)
        wring = work[:, 4608:7680].rearrange("p (s m c) -> p s m c", s=2, c=128)
        xslot = work[:, 7680:8896].rearrange("p (s n) -> p s n", s=2)
        xring = xslot[:, :, 32:].rearrange("p s (m t b) -> p s m t b", m=MK, t=3)
        z1 = work[:, 4608:6144]
        yq = work[:, 6144:6720]
        stats = work[:, 8064:8448].rearrange("p (n s) -> p n s", s=6)
        yp = work[:, 7488:8064]
        yt = work[0:96, 6720:7488]

        wflat = wmode[:, :, :].rearrange("p o f -> p (o f)")
        flat = big[:, :, :].rearrange("p j n -> p (j n)")
        pos = [0]

        def tail(n, rows=128):
            pos[0] += n
            return flat[0:rows, pos[0] - n:pos[0]]

        TT = 16
        res = tail(1024)
        xn, xc, sq = tail(1024), tail(2048), tail(2048)
        red, red2, red3 = tail(512), tail(512), tail(512)
        kv = tail(2048)
        xt, rt = tail(2048, 65), tail(2048, 65)
        qt, kvm, ct = tail(2048, 64), tail(2048, 64), tail(2048, 64)
        gl, lg, comb = tail(1024), tail(1024), tail(1024)
        mx, ixf, gate = tail(128), tail(128), tail(64)
        acc = tail(1024)
        first, second, chosen = tail(1024), tail(1024), tail(512).bitcast(bf16)
        before = tail(17 * 64)
        pos_ = xc[:, 0:1024]
        ntile, base = tail(64), tail(64)
        run = [tail(128), tail(128)]
        slotf, texf = tail(32), tail(1)
        ones_m = tail(64).bitcast(bf16)
        xg = wflat[:, 3072:4096].rearrange("p (s n) -> p s n", s=4)
        xgt = tail(1024).rearrange("p (s n) -> p s n", s=2)
        hid = tail(1024).rearrange("p (s n) -> p s n", s=2)
        yg = tail(512).rearrange("p (s n) -> p s n", s=2)
        ysel = [gl, lg]
        assert pos[0] <= JN * NPIX
        wpos = [0]

        def tailw(n, rows):
            wpos[0] += n
            return modes[0:rows, wpos[0] - n:wpos[0]]

        wqkv, wproj, wroute = tailw(192, 65), tailw(64, 65), tailw(64, 65)
        b2all, mask, iota, lnwb = tailw(64, 64), tailw(64, 64), tailw(64, 128), tailw(256, 128)
        tri, pid = tailw(128, 128), tailw(1, 128)
        wt = wflat[:, 0:3072].rearrange("p (s k n) -> p s k n", s=4, k=4)
        qscaled = sb("qscaled", [128, 32])
        shift = work[:, 8192:8320]
        tri16 = work[:, 8352:8416].bitcast(bf16)
        wmean = work[0:65, 8320:8352]
        proj = work[:, 0:8192].rearrange("p (j h n) -> p j h n", j=JN, h=2)
        ixs = sb("ixs", [128, 128], mybir.dt.uint32)
        slot = sb("slot", [128, 32], mybir.dt.uint32)
        texp = sb("texp", [1, 128], mybir.dt.int32)

        fxy = sb("fxy", [128, 96])
        tx, ty = sb("tx", [96, 256]), sb("ty", [96, 256])
        ident, avg = sb("ident", [128, 128]), sb("avg", [128, 128])
        liftx = work[:, 7792:7920]
        liftg = work[0:12, 7920:8048]
        liftt = sb("liftt", [128, 7])
        lmix = work[0:7, 8896:9024]
        params = sb("params", [128, LAYERS, PCOLS])
        cur = sb("cur", [128, PCOLS])
        bn = sb("bn", [128, 16])
        qcol = sb("qcol", [128, 32])
        qb = sb("qb", [128, 1])
        qbias = sb("qbias", [128, 1])

        banks = [ctx.enter_context(nc.psum_tensor(f"bank{i}", [128, 512], fp32)) for i in range(8)]
        PA, PB, PC, PD = banks[0:2], banks[2:4], banks[4:6], banks[6:8]

        consts_in = sem("consts_in")
        zeroed = sem("zeroed")
        a_full, b_full, c_full, d_full = sem("a_full"), sem("b_full"), sem("c_full"), sem("d_full")
        a_free, b_free, c_free, d_free = sem("a_free"), sem("b_free"), sem("c_free"), sem("d_free")
        images_in, rows_clear = sem("images_in"), sem("rows_clear")
        first_in, rows_in, pix_in = sem("first_in"), sem("rows_in"), [sem("pix_in0"), sem("pix_in1")]
        xs_ready, lmix_ready = sem("xs_ready"), sem("lmix_ready")
        v_ready, v_copied = sem("v_ready"), sem("v_copied")
        v_free = sem("v_free")
        x_sent, x_in = sem("x_sent"), sem("x_in")
        y_sent = sem("y_sent")
        pads_clear = sem("pads_clear")
        w_in, w_used = sem("w_in"), sem("w_used")
        cur_ready = sem("cur_ready")
        ring_clear = sem("ring_clear")
        exp_dve, exp_act = sem("exp_dve"), sem("exp_act")
        yq_in, yp_ready = sem("yq_in"), sem("yp_ready")
        stat_done = sem("stat_done")
        bn_chain, bn_mm, bn_sq, bn_done = sem("bn_chain"), sem("bn_mm"), sem("bn_sq"), sem("bn_done")
        pool_past, dve_past, pe_past = sem("pool_past"), sem("dve_past"), sem("pe_past")
        out_sent, q_prep = sem("out_sent"), sem("q_prep")
        tail_in, ones_set, tail_chain = sem("tail_in"), sem("ones_set"), sem("tail_chain")
        pixels_sent, res_in = sem("pixels_sent"), sem("res_in")
        xn_ready, xt_full, xt_ready = sem("xn_ready"), sem("xt_full"), sem("xt_ready")
        var_ready, std_ready, sq_ready = sem("var_ready"), sem("std_ready"), sem("sq_ready")
        kv_full, q_full, qt_ready, kv_taken, kv_ready = (sem("kv_full"), sem("q_full"), sem("qt_ready"),
                                                         sem("kv_taken"), sem("kv_ready"))
        kvm_full, kvm_ready, att_full, rt_ready = sem("kvm_full"), sem("kvm_ready"), sem("att_full"), sem("rt_ready")
        proj_full, gelu_ready, lg_full = sem("proj_full"), sem("gelu_ready"), sem("lg_full")
        dif_ready, exp_ready, comb_ready = sem("dif_ready"), sem("exp_ready"), sem("comb_ready")
        ct_full, ct_ready, bias_full = sem("ct_full"), sem("ct_ready"), sem("bias_full")
        slots_zeroed, chosen_ready, tot_full = sem("slots_zeroed"), sem("chosen_ready"), sem("tot_full")
        texf_ready, texr_full, texp_ready, slot_ready = (sem("texf_ready"), sem("texr_full"), sem("texp_ready"),
                                                         sem("slot_ready"))
        scattered = sem("scattered")
        wd_in = [sem(f"wd_in{s}") for s in range(4)]
        wt_in, xg_in = [sem(f"wt_in{s}") for s in range(4)], [sem(f"xg_in{s}") for s in range(4)]
        yg_out = [sem("yg_out0"), sem("yg_out1")]
        xg_turned, xgt_ready, hid_full, hid_ready = sem("xg_turned"), sem("xgt_ready"), sem("hid_full"), sem("hid_ready")
        yg_full, yg_ready = sem("yg_full"), sem("yg_ready")
        gathered, sum_ready = [sem("gathered0"), sem("gathered1")], sem("sum_ready")

        A0, B0, C0, D0 = 2, 2, 2, 14
        AM, AI, AF = MSTEPS, 32, 64
        BI, BF = 32, 64
        CI, CF = 48, 32
        DI, DF = 48, 16
        AL, BL, CL, DL = AM + AI + AF, BI + BF, CI + CF, DI + DF
        GROUPS = SLOT_TILES // 4
        NFIRST = 16 * (2 + 2 * QG)
        NCONST = 16 * (5 * QG + 5 + 1)
        XJ = 16 * QG

        block = ctx.enter_context(nc.Block())

        @block.sync
        def _(sp):
            sp.dma_start(f1, c_f1).then_inc(images_in, 16)
            for a in range(2):
                sp.dma_start(xin[a * 64:(a + 1) * 64], x.rearrange("(n a) x y o -> a x n (y o)", a=2)[a]).then_inc(images_in, 16)
            sp.dma_start(f2, c_f2.rearrange("(a y) f -> y a f", a=2)).then_inc(first_in, 16)
            sp.dma_start(gspec, c_gs).then_inc(first_in, 16)
            sp.wait_ge(zeroed, 5)
            for g in range(QG):
                r = slice(g * CH, (g + 1) * CH)
                sp.dma_start(liftx[g:g + 1, r], lift_w[0:1, :]).then_inc(first_in, 16)
                sp.dma_start(liftg[g * 3:g * 3 + 3, r], lift_w[1:4, :]).then_inc(first_in, 16)
            def load_weights(l):
                for g in range(QG):
                    fw = (fw1, fw2)[g // 2]
                    k0 = (g % 2) * GM
                    sp.dma_start(wmode[g * CH:(g + 1) * CH, :, :], fw[l, :, :, k0:k0 + GM]).then_inc(w_in, 16)

            def send_spectra(l):
                def send(j):
                    sp.wait_ge(d_free, D0 + l * DL + DI + j * 2 + 4)
                    sp.dma_start(spectra_x[bass.ds(j, 1)].rearrange("a p f -> (a p) f"), xj[:, :]).then_inc(x_sent, 16)

                def fetch(j):
                    sp.wait_ge(x_sent, (l * JN + j + 2) * 16)
                    src = spectra_x[bass.ds(j, 1)].rearrange("a (q c) f -> c (a q) f", q=QG)
                    for g in range(QG):
                        sp.dma_start(xmode[g * CH:(g + 1) * CH, :, :].rearrange("p (q j) f -> p j q f", q=QG)[:, j],
                                     src[:, :, g * GM:(g + 1) * GM]).then_inc(x_in, 16)
                with sp.Fori(0, JN) as j:
                    send(j)
                    fetch(j)

            def send_mixed(j):
                sp.dma_start(spectra_y[bass.ds(j, 1)].rearrange("a p q f -> (a p) q f"),
                             ymode.rearrange("p (q j) f -> p j q f", q=QG)[:, j]).then_inc(y_sent, 16)

            def fetch_mixed(l, j, sent=JN):
                sp.wait_ge(y_sent, (l * JN + sent) * 16)
                src = spectra_y[bass.ds(j, 1)].rearrange("a (g o) q f -> o (a q) g f", g=QG)
                for q in range(QG):
                    sp.dma_start(yq[q * CH:(q + 1) * CH, :].rearrange("p (g f) -> p g f", g=QG),
                                 src[:, q, :, :]).then_inc(yq_in, 16)

            xv = x.rearrange("(q j) (k r) y o -> j k q (r y o)", q=QG, k=4)
            gv = c_grid.rearrange("p (k n) -> k p n", k=4)

            def pixels(j, k):
                sp.dma_start(typix[96:100, k % 2, :], xv[j, k]).then_inc(pix_in[k % 2], 16)
                sp.dma_start(typix[100:103, k % 2, :], gv[k]).then_inc(pix_in[k % 2], 16)

            load_weights(0)
            sp.wait_ge(rows_clear, 1)
            sp.wait_ge(xs_ready, 1)
            for m in range(8):
                g, k0 = m // 2, (m % 2) * 3
                sp.dma_start(xrow[g:g + 1, k0 * B * YF:(k0 + 3) * B * YF], xs_[:, m, :]).then_inc(rows_in, 16)
            for q in range(QG):
                r = slice(q * CH, (q + 1) * CH)
                sp.dma_start(params[r, :, r], w_w.rearrange("l c d -> c l d")).then_inc(consts_in, 16)
                sp.dma_start(params[r, :, 128:131], scales.rearrange("l c n -> c l n")).then_inc(consts_in, 16)
                sp.dma_start(liftt[r, q:q + 1], lift_w[0:1, :].rearrange("n c -> c n")).then_inc(consts_in, 16)
                sp.dma_start(liftt[r, 4:7], lift_w[1:4, :].rearrange("n c -> c n"),
                             allow_slow_non_contiguous=True).then_inc(consts_in, 16)
                sp.dma_start(qcol[r, q:q + 1], q_w).then_inc(consts_in, 16)
            for dst, src in ((fxy, c_fxy), (tx, c_tx), (ty, c_ty), (ident, c_ident), (avg, c_avg)):
                sp.dma_start(dst[:, :], src).then_inc(consts_in, 16)
            sp.dma_start(qb[:, :], q_b.rearrange("(a c) -> a c", a=1).broadcast_to([128, 1])).then_inc(consts_in, 16)
            sp.wait_ge(a_free, A0 + AM + 2)
            send_mixed(0)
            fetch_mixed(0, 0, 1)
            pixels(0, 0)
            pixels(0, 1)
            with sp.Fori(1, JN) as j:
                send_mixed(j)

            def first_group(j, last):
                if not last:
                    sp.wait_ge(yp_ready, j + 1)
                    fetch_mixed(0, j + 1)
                for k in range(2):
                    sp.wait_ge(b_full, B0 + j * 4 + k + 1)
                    pixels(j, k + 2)
                if not last:
                    for k in range(2):
                        sp.wait_ge(b_full, B0 + j * 4 + k + 3)
                        pixels(j + 1, k)
            with sp.Fori(0, JN - 1) as j:
                first_group(j, False)
            first_group(JN - 1, True)

            def rest_of_layer(l):
                sp.wait_ge(a_free, A0 + l * AL + AM + 2)
                send_mixed(0)
                fetch_mixed(l, 0, 1)
                with sp.Fori(1, JN) as j:
                    send_mixed(j)
                with sp.Fori(0, JN - 1) as j:
                    sp.wait_ge(yp_ready, l * JN + j + 1)
                    fetch_mixed(l, j + 1)

            def next_layer(l):
                sp.wait_ge(w_used, l + 1)
                load_weights(l + 1)
                send_spectra(l)
            next_layer(0)
            with sp.Fori(1, LAYERS - 1) as l:
                rest_of_layer(l)
                next_layer(l)
            rest_of_layer(LAYERS - 1)
            sp.wait_ge(bn_done, LAYERS)
            for dst, src in ((wqkv[0:64, :], W_qkv), (wqkv[64:65, :], b_qkv.rearrange("(a n) -> a n", a=1)),
                             (wproj[0:64, :], W_proj), (wproj[64:65, :], b_proj.rearrange("(a n) -> a n", a=1)),
                             (wroute[0:64, :], Wr), (wroute[64:65, :], br.rearrange("(a n) -> a n", a=1)),
                             (b2all, b2), (mask, c_mask), (iota, c_iota), (tri, c_tri), (pid, c_pid)):
                sp.dma_start(dst, src).then_inc(tail_in, 16)
            for n, src in enumerate((kln_w, vln_w, kln_b, vln_b)):
                sp.dma_start(lnwb[:, n * 64:(n + 1) * 64],
                             src.rearrange("h (a o) d -> a (h o d)", a=1).broadcast_to([128, 64])).then_inc(tail_in, 16)
            sp.wait_ge(b_free, B0 + LAYERS * BL - BF + JN * 2 + 2)
            pv = pixels_out.rearrange("(q j) (h r n) -> r q j h n", q=QG, h=2, r=4)
            for r in range(4):
                sp.dma_start(pv[r], proj[r * 32:r * 32 + QG, :, :, :]).then_inc(pixels_sent, 16)
            sp.wait_ge(pixels_sent, 64)
            for q in range(QG):
                sp.dma_start(res[q * 32:(q + 1) * 32, :].rearrange("p (j n) -> p j n", j=JN),
                             pixels_out[q * JN:(q + 1) * JN].rearrange("j (xp n) -> xp j n", xp=32)).then_inc(res_in, 16)

            def weights(s, es):
                for k in range(4):
                    sp.dma_start(wt[:, s, k, :], wexp[bass.ds(es[k], 1), :, :].rearrange("e p n -> (e p) n")).then_inc(wd_in[s], 16)

            def first_weights(i, s):
                e = bass.ds(i * 16 + s * 4, 4)
                sp.dma_start(wt[:, s], wexp[e, :, :].rearrange("e p n -> p e n")).then_inc(wt_in[s], 16)

            def tokens(i, s):
                rows = slots_x[bass.ds((i * 4 + s) * 512, 512), :].rearrange("(k p) n -> p k n", k=4)
                sp.dma_start(xg[:, s, :].rearrange("p (k n) -> p k n", k=4), rows).then_inc(xg_in[s], 16)

            for s in range(4):
                first_weights(0, s)
            sp.wait_ge(texp_ready, 1)
            es = nc.values_load_multi_w_load_instructions(texp[0:1, 0:SLOT_TILES - EXPERTS],
                                                          engines=(mybir.EngineType.SP,), min_val=0,
                                                          max_val=EXPERTS - 1)[1]
            sp.wait_ge(scattered, 32 * 16)
            for s in range(4):
                tokens(0, s)
            with sp.Fori(1, EXPERTS // 16) as i:
                for s in range(4):
                    sp.wait_ge(xg_turned, i * 4 + s - 3)
                    tokens(i, s)
                    sp.wait_ge(yg_full, i * 4 + s - 2)
                    first_weights(i, s)
            for i in range(EXPERTS // 16, GROUPS // 4):
                for s in range(4):
                    sp.wait_ge(xg_turned, i * 4 + s - 3)
                    tokens(i, s)
                    sp.wait_ge(yg_full, i * 4 + s - 2)
                    weights(s, es[(i * 4 + s) * 4 - EXPERTS:][:4])
            sp.wait_ge(sum_ready, 2)
            for q in range(QG):
                sp.dma_start(out[q * JN:(q + 1) * JN].rearrange("j (xp x) y -> xp j (x y)", x=2),
                             acc[q * 32:(q + 1) * 32, :].rearrange("p (j n) -> p j n", j=JN)).then_inc(out_sent, 16)
            sp.wait_ge(out_sent, 64)

        @block.gpsimd
        def _(pool):
            pool.memset(params[:, :, :], 0.0).then_inc(zeroed, 1)
            pool.memset(liftx[:, :], 0.0).then_inc(zeroed, 1)
            pool.memset(liftg[:, :], 0.0).then_inc(zeroed, 1)
            pool.memset(liftt[:, :], 0.0).then_inc(zeroed, 1)
            pool.memset(qcol[:, :], 0.0).then_inc(zeroed, 1)
            nz = SLOT_TILES * 64 // 2
            pool.memset(big[:, 0, 0:nz], 0.0).then_inc(zeroed, 1)
            pool.wait_ge(zeroed, 6)
            for h in range(2):
                pool.dma_start(slots_x[h * SLOT_TILES * 64:(h + 1) * SLOT_TILES * 64, :].rearrange("(p r) n -> p (r n)", p=128),
                               big[:, 0, 0:nz]).then_inc(slots_zeroed, 16)

            def clear_ring(l):
                pool.sem_inc(pool_past, 1)
                pool.memset(xslot[:, :, 0:32], 0.0).then_inc(pads_clear, 1)
                pool.wait_ge(pads_clear, l + 1)
                pool.sem_inc(pool_past, 1)
                pool.memset(work[:, 4608:7680], 0.0).then_inc(ring_clear, 1)

            pool.wait_ge(x_in, JN * XJ)
            clear_ring(0)
            with pool.Fori(1, LAYERS) as l:
                pool.wait_ge(d_full, D0 + l * DL)
                clear_ring(l)
            pool.wait_ge(b_free, B0 + LAYERS * BL - BF + JN * 2 + 2)
            fills = ((xt[64:65, :], 1.0), (rt[64:65, :], 1.0), (ones_m[:, :], 1.0), (xgt[64:128, :, :], 0.0),
                     (xgt[64:65, :, :], 1.0), (run[0][:, 0:64], 0.0), (run[1][:, 0:64], 0.0), (before[:, 0:64], 0.0))
            for n, (dst, value) in enumerate(fills):
                if n:
                    pool.wait_ge(ones_set, n)
                pool.memset(dst, value).then_inc(ones_set, 1)
            pool.wait_ge(slots_zeroed, 32)
            for k in range(2):
                pool.wait_ge(slot_ready, k + 1)
                for t in range(TT):
                    pool.indirect_dma_start(slots_x, bass.IndirectOffsetOnAxis(ap=slot[:, k * TT + t:k * TT + t + 1], axis=0),
                                            xn[:, t * 64:(t + 1) * 64], None).then_inc(scattered, 16)

            def send(i, s):
                pool.wait_ge(yg_ready, i * 4 + s + 3)
                pool.dma_start(slots_y[bass.ds((i * 4 + s) * 512, 512), :].rearrange("(k p) n -> p k n", k=4),
                               yg[:, s % 2, :].rearrange("p (k n) -> p k n", k=4)).then_inc(yg_out[s % 2], 16)

            with pool.Fori(0, GROUPS // 4) as i:
                for s in range(4):
                    send(i, s)
            for s in range(2):
                pool.wait_ge(yg_out[s], GROUPS // 2 * 16)
            for t in range(TT):
                for k in range(2):
                    pool.indirect_dma_start(ysel[k][:, t * 64:(t + 1) * 64], None, slots_y,
                                            bass.IndirectOffsetOnAxis(ap=slot[:, k * TT + t:k * TT + t + 1],
                                                                      axis=0)).then_inc(gathered[t // 8], 16)

        @block.scalar
        def _(act):
            act.wait_ge(consts_in, NCONST)

            def forward(l):
                def apply(j, c):
                    act.wait_ge(v_free, (l * JN + j) * NC + c + 1)
                    act.wait_ge(v_copied, (l * JN + j) * NC + c + 1)
                    act.activation(vch[:, c % 4, :], big[:, j, c * CW:(c + 1) * CW], ACT.Relu, bias=bn[:, 9:10],
                                   scale=bn[:, 8:9]).then_inc(v_ready, 1)

                def cy_out(j, c, odd):
                    act.wait_ge(b_full, B0 + l * BL + BI + j * NC + c + 1)
                    act.activation(cy_[odd].rearrange("p (f x) -> p f x", f=YF)[:, :, c * 8:(c + 1) * 8],
                                   PB[c % 2][:, 48:240].rearrange("p (x f) -> p f x", x=8), ACT.Copy).then_inc(b_free, 1)

                def x_out(j, h):
                    act.wait_ge(d_full, D0 + l * DL + DI + j * 2 + h + 1)
                    dst = xj.rearrange("p (k y r) -> p y k r", k=KX, y=KY)[:, h * 6:h * 6 + 6]
                    act.activation(dst, PD[h][:, 0:288].rearrange("p (y k r) -> p y k r", y=6, k=KX),
                                   ACT.Copy).then_inc(d_free, 1)

                def spectra(j):
                    act.wait_ge(x_sent, (l * JN + j + 1) * 16)
                    x_out(j, 0)
                    x_out(j, 1)

                def group(j, odd, first=False, last=False):
                    for c in range(NC):
                        if c < NC - 3:
                            apply(j, c + 3)
                        elif not last:
                            apply(j + 1, c - (NC - 3))
                        if c == 0 and not first:
                            act.wait_ge(c_free, C0 + l * CL + CI + j * 4 - 2)
                        cy_out(j, c, odd)
                        if c == 6 and not first:
                            spectra(j - 1)

                for c in range(3):
                    apply(0, c)
                group(0, 0, first=True)
                with act.Fori(0, JN // 2 - 1) as i:
                    group(i * 2 + 1, 1)
                    group(i * 2 + 2, 0)
                group(JN - 1, 1, last=True)
                spectra(JN - 1)

            def mixing(l):
                act.preload_act_table(ACT.Copy)
                act.wait_ge(x_in, (l + 1) * JN * XJ)

                def xs(k, h):
                    act.wait_ge(a_full, A0 + l * AL + k * 2 + h - 1)
                    src = xmode[:, :, bass.ds(k * YF + h * 12, 12)].rearrange("p b (m r) -> p m r b", r=2)
                    act.activation(xring[:, h, :, 0, :], src[:, :, 1, :], ACT.Copy, scale=-1.0).then_inc(exp_act, 1)
                    act.activation(xring[:, h, :, 1, :], src[:, :, 0, :], ACT.Copy).then_inc(exp_act, 1)
                    act.activation(xring[:, h, :, 2, :], src[:, :, 1, :], ACT.Copy).then_inc(exp_act, 1)

                def y_out(k, h):
                    act.wait_ge(a_full, A0 + l * AL + k * 2 + h + 1)
                    dst = ymode[:, :, bass.ds(k * YF + h * 12, 12)].rearrange("p b m -> p m b")
                    act.activation(dst, PA[h][:, 32:416].rearrange("p (m b) -> p m b", b=B), ACT.Copy).then_inc(a_free, 1)

                xs(0, 0)
                with act.Fori(0, KG - 1) as k:
                    xs(k, 1)
                    y_out(k, 0)
                    xs(k + 1, 0)
                    y_out(k, 1)
                xs(KG - 1, 1)
                y_out(KG - 1, 0)
                y_out(KG - 1, 1)

            def inverse(l):
                def z1_out(j, p):
                    if p == 0:
                        act.wait_ge(d_full, D0 + l * DL + j * 6)
                    act.wait_ge(c_full, C0 + l * CL + j * 6 + p + 1)
                    dst = z1.rearrange("p (x f) -> p x f", f=YF)[:, :, p * 4:p * 4 + 4]
                    act.activation(dst, PC[p % 2][:, 0:256].rearrange("p (x f) -> p x f", f=4),
                                   ACT.Copy).then_inc(c_free, 1)

                def u_out(j, c):
                    full, free, P, base = ((a_full, a_free, PA, A0 + l * AL + AM), (b_full, b_free, PB, B0 + l * BL))[c % 2]
                    act.wait_ge(full, base + j * 4 + c // 2 + 1)
                    act.activation(big[:, j, c * CW:(c + 1) * CW], P[(c // 2) % 2][:, :], ACT.Identity,
                                   bias=cur[:, 128:129]).then_inc(free, 1)

                for p in range(6):
                    z1_out(0, p)

                def group(j, last):
                    for c in range(NC):
                        u_out(j, c)
                        if c >= 3 and c < 6 and not last:
                            z1_out(j + 1, 2 * (c - 3))
                            z1_out(j + 1, 2 * (c - 3) + 1)
                with act.Fori(0, JN - 1) as j:
                    group(j, False)
                group(JN - 1, True)

            def norm(l):
                act.wait_ge(bn_sq, 2 * l + 1)
                act.activation(bn[:, 5:6], bn[:, 4:5], ACT.Sqrt).then_inc(bn_sq, 1)

            with act.Fori(0, LAYERS - 1) as l:
                mixing(l)
                act.wait_ge(cur_ready, l + 1)
                act.wait_ge(slots_zeroed, 32)
                inverse(l)
                norm(l)
                act.preload_act_table(ACT.Relu)
                act.wait_ge(bn_done, l + 1)
                forward(l)
            mixing(LAYERS - 1)
            act.wait_ge(cur_ready, LAYERS)
            inverse(LAYERS - 1)
            norm(LAYERS - 1)
            act.wait_ge(ring_clear, LAYERS + 1)
            b0 = B0 + LAYERS * BL - BF
            with act.Fori(0, JN) as j:
                for h in range(2):
                    act.wait_ge(v_free, j * NC + (LAYERS - 1) * JN * NC + h * 4 + 8)
                    act.activation(proj[:, j, h, :], PB[h][:, :], ACT.Identity, bias=qbias[:, 0:1]).then_inc(b_free, 1)

            def deviation(n, scale, bias):
                act.wait_ge(var_ready, n)
                act.activation(red3[:, 0:bias], red2[:, 0:bias], ACT.Sqrt, scale=scale).then_inc(std_ready, 1)

            def xt_out(n):
                for b in range(4):
                    act.wait_ge(xt_full, n * 4 + b + 1)
                    act.activation(xt[0:64, b * 512:(b + 1) * 512], (PB + PC)[b][0:64, :], ACT.Copy).then_inc(xt_ready, 1)

            deviation(1, 1.0, TT)
            xt_out(0)
            for b in range(4):
                act.wait_ge(kv_taken, b + 1)
                act.activation(sq[:, b * 512:(b + 1) * 512], xc[:, b * 512:(b + 1) * 512], ACT.Square).then_inc(sq_ready, 1)
            for b in range(4):
                act.wait_ge(q_full, b + 1)
                act.activation(qt[:, b * 512:(b + 1) * 512], (PC + PD)[b][0:64, :], ACT.Copy).then_inc(qt_ready, 1)
            deviation(2, 1.0 / 3, 512)
            act.preload_act_table(ACT.Gelu)
            for b in range(2):
                act.wait_ge(proj_full, b + 1)
                act.activation(gl[:, b * 512:(b + 1) * 512], PA[b][:, :], ACT.Gelu).then_inc(gelu_ready, 1)
            act.preload_act_table(ACT.Sqrt)
            deviation(3, 1.0, TT)
            xt_out(1)
            act.wait_ge(dif_ready, 1)
            act.activation(gate[:, 16:32], gate[:, 0:16], ACT.Exp).then_inc(exp_ready, 1)
            def turned(i, s):
                act.wait_ge(xg_turned, i * 4 + s + 1)
                act.activation(xgt[0:64, s % 2, :], PA[s % 2][0:64, :], ACT.Copy).then_inc(xgt_ready, 1)

            def units(i, s):
                act.wait_ge(hid_full, i * 4 + s + 1)
                act.activation(hid[:, s % 2, :], PB[s % 2][:, :], ACT.Relu).then_inc(hid_ready, 1)

            def group(i, s, last):
                if s < 2 or not last:
                    act.wait_ge(hid_full, i * 4 + s + 1)
                    turned(i + (s + 2) // 4, (s + 2) % 4)
                if s < 3 or not last:
                    act.wait_ge(yg_full, i * 4 + s + 1)
                    units(i + (s + 1) // 4, (s + 1) % 4)

            turned(0, 0)
            turned(0, 1)
            units(0, 0)
            with act.Fori(0, GROUPS // 4 - 1) as i:
                for s in range(4):
                    group(i, s, False)
            for s in range(4):
                group(GROUPS // 4 - 1, s, True)

        @block.vector
        def _(dve):
            for s, n in ((a_free, 2), (b_free, 2), (c_free, 2), (d_free, 2), (v_free, 4), (v_copied, 4),
                         (yg_ready, 2), (hid_ready, 1), (yg_full, 1)):
                dve.sem_inc(s, n)
            dve.memset(xrow, 0.0).then_inc(rows_clear, 1)

            def forward(l):
                def chunk(j, c):
                    dve.wait_ge(a_full, A0 + l * AL + AM + AI + j * NC + c + 1)
                    dve.wait_ge(b_full, B0 + l * BL + BI + j * NC + c - 3)
                    dve.tensor_copy(vt[:, c % 4, :], PA[c % 2][:, :]).then_inc(a_free, 1)
                    dve.tensor_copy(big[:, j, c * CW:(c + 1) * CW], vch[:, c % 4, :]).then_inc(v_copied, 1)

                def dx_out(j, n):
                    if n == 0:
                        dve.wait_ge(d_full, D0 + l * DL + DI + j * 2)
                    dve.wait_ge(c_full, C0 + l * CL + CI + j * 4 + n + 1)
                    dve.tensor_copy(dx_[:, n * 384:(n + 1) * 384], PC[n % 2][:, 0:384]).then_inc(c_free, 1)

                def group(j, first=False):
                    for c in range(NC):
                        chunk(j, c)
                        if c >= 2 and c < 6 and not first:
                            dx_out(j - 1, c - 2)
                group(0, first=True)
                with dve.Fori(1, JN) as j:
                    group(j)
                for n in range(4):
                    dx_out(JN - 1, n)

            def mixing(l):
                dve.wait_ge(ring_clear, l + 1)
                dve.wait_ge(w_in, (l + 1) * 64)
                dve.tensor_copy(cur[:, :], params[:, l, :]).then_inc(cur_ready, 1)
                with dve.Fori(0, KG) as k:
                    for h in range(2):
                        dve.wait_ge(a_full, A0 + l * AL + k * 2 + h - 1)
                        for g in range(QG):
                            r = slice(g * CH, (g + 1) * CH)
                            src = wmode[r, :, bass.ds(k * YF + h * 12, 12)].rearrange("p o m -> p m o")
                            dve.tensor_copy(wring[r, h, :, r], src).then_inc(exp_dve, 1)
                dve.wait_ge(exp_dve, (l + 1) * MSTEPS * QG)
                dve.sem_inc(w_used, 1)

            def first_mix():
                dve.wait_ge(a_full, A0 + AM)
                dve.tensor_copy(z1mix[96:103].rearrange("p s (k n) -> p (s k) n", k=4),
                                lmix[:, :].unsqueeze(1).to_broadcast([7, 16, 128])).then_inc(lmix_ready, 1)
                dve.tensor_copy(typix[0:96].rearrange("p s (k n) -> p (s k) n", k=4),
                                ty[:, :].unsqueeze(1).to_broadcast([96, 8, 256])).then_inc(lmix_ready, 1)

            def inverse(l):
                def yt_out(j, n):
                    if n == 0:
                        dve.wait_ge(c_full, C0 + l * CL + j * 6)
                    dve.wait_ge(d_full, D0 + l * DL + j * 6 + n + 1)
                    dve.tensor_copy(yt[:, n * 384:(n + 1) * 384], PD[n][0:96, 0:384]).then_inc(d_free, 1)

                def z1t_out(j, s):
                    dve.wait_ge(d_full, D0 + l * DL + j * 6 + 2 + s + 1)
                    dve.tensor_copy(z1t[:, s, :], PD[s % 2][0:96, :]).then_inc(d_free, 1)

                def take(j, c):
                    free, base = ((a_free, A0 + l * AL + AM), (b_free, B0 + l * BL))[c % 2]
                    dve.wait_ge(free, base + j * 4 + c // 2 + 3)
                    dve.bn_stats(stats[:, bass.ds(j * NC + c, 1), :],
                                 big[:, j, c * CW:(c + 1) * CW]).then_inc(stat_done, 1)

                def regroup(j):
                    dve.wait_ge(yq_in, (l * JN + j + 1) * XJ)
                    dve.wait_ge(d_full, D0 + l * DL + j * 6 - 4)
                    dve.sem_inc(dve_past, 1)
                    dve.tensor_copy(yp.rearrange("p (y k f) -> p k y f", y=KY // 2, k=KX),
                                    yq.rearrange("p (k y f) -> p k y f", k=KX, y=KY // 2)).then_inc(yp_ready, 1)

                regroup(0)
                yt_out(0, 0)
                yt_out(0, 1)
                z1t_out(0, 0)
                z1t_out(0, 1)

                def group(j, last):
                    z1t_out(j, 2)
                    take(j, 0)
                    if not last:
                        regroup(j + 1)
                    z1t_out(j, 3)
                    take(j, 1)
                    take(j, 2)
                    if not last:
                        yt_out(j + 1, 0)
                        yt_out(j + 1, 1)
                    for c in range(3, 7):
                        take(j, c)
                    if not last:
                        z1t_out(j + 1, 0)
                        z1t_out(j + 1, 1)
                    take(j, 7)
                with dve.Fori(0, JN - 1) as j:
                    group(j, False)
                group(JN - 1, True)

            def norm(l):
                n = [0]

                def step(ins):
                    n[0] += 1
                    ins.then_inc(bn_chain, 1)
                    dve.wait_ge(bn_chain, l * 8 + n[0])
                dve.wait_ge(stat_done, (l + 1) * JN * NC)
                dve.sem_inc(dve_past, 1)
                dve.bn_aggr(bn[:, 0:2], stats[:, :, :]).then_inc(bn_mm, 1)
                dve.wait_ge(bn_mm, l * 4 + 2)
                step(dve.tensor_copy(bn[:, 2:3], PD[0][:, 0:1]))
                step(dve.tensor_tensor(bn[:, 3:4], bn[:, 0:1], bn[:, 2:3], ALU.subtract))
                step(dve.tensor_tensor(bn[:, 3:4], bn[:, 3:4], bn[:, 3:4], ALU.mult))
                dve.tensor_tensor(bn[:, 3:4], bn[:, 3:4], bn[:, 1:2], ALU.add).then_inc(bn_mm, 1)
                dve.wait_ge(bn_mm, l * 4 + 4)
                dve.tensor_scalar(bn[:, 4:5], PD[0][:, 1:2], EPS, None, ALU.add).then_inc(bn_sq, 1)
                dve.wait_ge(bn_sq, 2 * l + 2)
                step(dve.reciprocal(bn[:, 6:7], bn[:, 5:6]))
                step(dve.tensor_tensor(bn[:, 8:9], bn[:, 6:7], cur[:, 129:130], ALU.mult))
                step(dve.tensor_tensor(bn[:, 7:8], bn[:, 2:3], bn[:, 8:9], ALU.mult))
                step(dve.tensor_tensor(bn[:, 9:10], cur[:, 130:131], bn[:, 7:8], ALU.subtract))
                step(dve.tensor_copy(bn[:, 10:11], bn[:, 9:10]))
                dve.sem_inc(bn_done, 1)

            for n, (P, full, free, k) in enumerate(((PA, a_full, a_free, 0), (PA, a_full, a_free, 1),
                                                    (PB, b_full, b_free, 0), (PB, b_full, b_free, 1))):
                dve.wait_ge(full, k + 1)
                dst = xk.rearrange("p (f n a) -> p f n a", f=2 * KX, n=B // 2)[:, :, n * 4:(n + 1) * 4, :]
                dve.tensor_copy(dst, P[k][0:64, 0:384].rearrange("p (n f a) -> p f n a", n=4, f=2 * KX)).then_inc(free, 1)
            dve.wait_ge(c_full, 1)
            dve.tensor_copy(gsum, PC[0][:, 0:GM]).then_inc(c_free, 1)
            dve.wait_ge(c_full, 2)
            dve.tensor_copy(xs_, PC[1][0:96, 0:192].rearrange("p (m f) -> p m f", m=8)).then_inc(c_free, 1)
            dve.wait_ge(c_free, 4)
            dve.sem_inc(xs_ready, 1)
            for n in range(2 * KG):
                k, b = slice((n // 2) * YF, (n // 2 + 1) * YF), slice((n % 2) * 16, (n % 2 + 1) * 16)
                dve.wait_ge(d_full, n + 1)
                dve.tensor_tensor(xmode[:, b, k], PD[n % 2][:, 0:384].rearrange("p (b f) -> p b f", b=16),
                                  gsum[:, k].unsqueeze(1).to_broadcast([128, 16, YF]), ALU.add).then_inc(d_free, 1)
            dve.wait_ge(d_free, 14)
            dve.sem_inc(x_sent, 16)
            dve.sem_inc(x_in, JN * XJ)
            for n in range(2):
                dve.wait_ge(d_full, 13 + n)
                dve.tensor_copy(lmix[:, n * 64:(n + 1) * 64], PD[n][0:7, 0:64]).then_inc(d_free, 1)
            mixing(0)
            first_mix()
            inverse(0)
            norm(0)
            forward(0)
            with dve.Fori(1, LAYERS - 1) as l:
                mixing(l)
                inverse(l)
                norm(l)
                forward(l)
            mixing(LAYERS - 1)
            inverse(LAYERS - 1)
            norm(LAYERS - 1)
            dve.tensor_scalar(qscaled[:, :], qcol[:, :], bn[:, 8:9], None, ALU.mult).then_inc(q_prep, 1)
            dve.tensor_copy(shift[:, :], bn[:, 9:10].to_broadcast([128, 128])).then_inc(q_prep, 1)
            dve.wait_ge(q_prep, 3)
            dve.tensor_scalar(qbias[:, :], PD[0][:, 2:3], qb[:, 0:1], None, ALU.add).then_inc(ring_clear, 1)
            n = [0]

            def step(ins):
                n[0] += 1
                ins.then_inc(tail_chain, 1)
                dve.wait_ge(tail_chain, n[0])

            def spread(a, k):
                return a.unsqueeze(2).to_broadcast([a.shape[0], a.shape[1], k])

            def grouped(a, k):
                return a.rearrange("p (g k) -> p g k", k=k)

            def over_deviation(dst, groups, k):
                step(dve.reciprocal(red3[:, 0:groups], red3[:, 0:groups]))
                step(dve.tensor_tensor(grouped(dst, k), grouped(xc[:, 0:groups * k], k), spread(red3[:, 0:groups], k),
                                       ALU.mult))

            def normalise(src, dst, turn):
                c, w = grouped(xc[:, 0:1024], 64), grouped(sq[:, 0:1024], 64)
                step(dve.tensor_reduce(red[:, 0:TT], grouped(src, 64), mybir.AxisListType.X, ALU.add))
                step(dve.tensor_scalar(red[:, 0:TT], red[:, 0:TT], 1.0 / 64, None, ALU.mult))
                step(dve.tensor_tensor(c, grouped(src, 64), spread(red[:, 0:TT], 64), ALU.subtract))
                step(dve.tensor_tensor(w, c, c, ALU.mult))
                step(dve.tensor_reduce(red2[:, 0:TT], w, mybir.AxisListType.X, ALU.add))
                step(dve.tensor_scalar(red2[:, 0:TT], red2[:, 0:TT], 1.0 / 64, EPS, ALU.mult, ALU.add))
                dve.sem_inc(var_ready, 1)
                dve.wait_ge(std_ready, turn)
                over_deviation(dst, TT, 64)

            dve.wait_ge(tail_in, 15 * 16)
            step(dve.tensor_copy(tri16[:, :], tri[:, :]))
            w4 = grouped(wqkv[:, 64:192], 4)
            step(dve.tensor_reduce(wmean, w4, mybir.AxisListType.X, ALU.add))
            step(dve.tensor_scalar(wmean, wmean, 0.25, None, ALU.mult))
            step(dve.tensor_tensor(w4, w4, spread(wmean, 4), ALU.subtract))
            dve.wait_ge(res_in, 64)
            normalise(res, xn, 1)
            dve.sem_inc(xn_ready, 1)
            for b in range(4):
                dve.wait_ge(kv_full, b + 1)
                dve.tensor_copy(xc[:, b * 512:(b + 1) * 512], (PA + PB)[b][:, :]).then_inc(kv_taken, 1)
            for b in range(4):
                dve.wait_ge(sq_ready, b + 1)
                step(dve.tensor_reduce(red2[:, b * 128:(b + 1) * 128], grouped(sq[:, b * 512:(b + 1) * 512], 4),
                                       mybir.AxisListType.X, ALU.add))
            dve.sem_inc(var_ready, 1)
            dve.wait_ge(std_ready, 2)
            step(dve.tensor_scalar(red3[:, 0:512], red3[:, 0:512], EPS, None, ALU.add))
            kv3 = kv.rearrange("p (t n) -> p t n", t=TT)
            for h in range(2):
                s_, r = slice(h * 1024, (h + 1) * 1024), red3[:, h * 256:(h + 1) * 256]
                step(dve.reciprocal(r, r))
                step(dve.tensor_tensor(grouped(kv[:, s_], 4), grouped(xc[:, s_], 4), spread(r, 4), ALU.mult))
                for n0_, op in ((0, ALU.mult), (1, ALU.add)):
                    wb = lnwb[:, n0_ * 128:(n0_ + 1) * 128].unsqueeze(1).to_broadcast([128, TT // 2, 128])
                    half = kv3[:, h * TT // 2:(h + 1) * TT // 2]
                    step(dve.tensor_tensor(half, half, wb, op))
                dve.sem_inc(kv_ready, 1)
            for q in range(QG):
                dve.wait_ge(kvm_full, q + 1)
                step(dve.tensor_tensor(grouped(kvm[:, q * 512:(q + 1) * 512], 64), grouped((PA + PB)[q][0:64, :], 64),
                                       mask.unsqueeze(1).to_broadcast([64, JN, 64]), ALU.mult))
            dve.sem_inc(kvm_ready, 1)
            for b in range(4):
                dve.wait_ge(att_full, b + 1)
                dve.tensor_tensor(rt[0:64, b * 512:(b + 1) * 512], (PC + PD)[b][0:64, :], xt[0:64, b * 512:(b + 1) * 512],
                                  ALU.add).then_inc(rt_ready, 1)
            step(dve.tensor_tensor(res, res, xn, ALU.add))
            dve.wait_ge(gelu_ready, 2)
            step(dve.tensor_tensor(res, res, gl, ALU.add))
            normalise(res, xn, 3)
            dve.sem_inc(xn_ready, 1)
            for b in range(2):
                dve.wait_ge(lg_full, b + 1)
                step(dve.tensor_copy(lg[:, b * 512:(b + 1) * 512], PA[b][:, :]))
            for t in range(TT):
                top = dve.max(mx[:, t * 8:t * 8 + 8], lg[:, t * 64:t * 64 + 64])
            step(top)
            for t in range(TT):
                top = dve.max_index(ixs[:, t * 8:t * 8 + 8], mx[:, t * 8:t * 8 + 8], lg[:, t * 64:t * 64 + 64])
            step(top)
            step(dve.tensor_copy(ixf, ixs[:, :]))
            m8, i8 = grouped(mx, 8), grouped(ixf, 8)
            it = iota.unsqueeze(1).to_broadcast([128, TT, 64])
            f3, s3, c3 = grouped(first, 64), grouped(second, 64), grouped(comb, 64)
            step(dve.tensor_tensor(f3, it, i8[:, :, 0:1].to_broadcast([128, TT, 64]), ALU.is_equal))
            step(dve.tensor_tensor(s3, it, i8[:, :, 1:2].to_broadcast([128, TT, 64]), ALU.is_equal))
            step(dve.tensor_tensor(chosen, first, second, ALU.add))
            dve.sem_inc(chosen_ready, 1)
            step(dve.tensor_tensor(gate[:, 0:16], m8[:, :, 1], m8[:, :, 0], ALU.subtract))
            dve.sem_inc(dif_ready, 1)
            step(dve.tensor_scalar(ixf, ixf, 128.0, None, ALU.mult))
            e8 = grouped(ixf, 8)
            dve.wait_ge(ones_set, 8)
            dve.wait_ge(tot_full, 1)
            for t in range(TT):
                step(dve.tensor_tensor(before[:, (t + 1) * 64:(t + 2) * 64], before[:, t * 64:(t + 1) * 64],
                                       PC[t // 8][:, (t % 8) * 64:(t % 8 + 1) * 64], ALU.add))
            step(dve.tensor_scalar(base, before[:, TT * 64:(TT + 1) * 64], 1.0 / 128, None, ALU.mult))
            more = grouped(sq[:, 0:960], 15)
            step(dve.tensor_tensor(more, spread(base, 15), iota[:, 1:16].unsqueeze(1).to_broadcast([128, 64, 15]), ALU.is_gt))
            step(dve.tensor_reduce(ntile, more, mybir.AxisListType.X, ALU.add))
            step(dve.tensor_copy(run[0][:, 64:128], ntile))
            for k in range(6):
                a, b = run[k % 2], run[(k + 1) % 2]
                step(dve.tensor_tensor(b[:, 64:128], a[:, 64:128], a[:, 64 - 2 ** k:128 - 2 ** k], ALU.add))
            ends = run[0][:, 64:128]
            step(dve.tensor_scalar(sq[:, 0:64], ends, pid[:, 0:1], None, ALU.is_le))
            step(dve.tensor_reduce(texf, sq[:, 0:64], mybir.AxisListType.X, ALU.add))
            step(dve.tensor_scalar(texf, texf, float(EXPERTS - 1), None, ALU.min))
            dve.sem_inc(texf_ready, 1)
            step(dve.tensor_tensor(base, ends, ntile, ALU.subtract))
            step(dve.tensor_tensor(base, base, iota, ALU.subtract))
            step(dve.tensor_scalar(base, base, 128.0, float((EXPERTS - 1) * 128), ALU.mult, ALU.add))
            for b in range(2):
                step(dve.tensor_tensor(pos_[:, b * 512:(b + 1) * 512], PB[b][:, :], before[:, b * 512:(b + 1) * 512], ALU.add))
            step(dve.scalar_tensor_tensor(grouped(sq[:, 0:1024], 64), grouped(pos_, 64), 128.0,
                                          base.unsqueeze(1).to_broadcast([128, TT, 64]), ALU.is_ge, ALU.mult))
            step(dve.tensor_tensor(pos_, pos_, sq[:, 0:1024], ALU.add))
            for n_, hot in enumerate((first, second)):
                step(dve.tensor_tensor(sq[:, 0:1024], pos_, hot, ALU.mult))
                s_ = slice(n_ * TT, (n_ + 1) * TT)
                step(dve.tensor_reduce(slotf[:, s_], grouped(sq[:, 0:1024], 64), mybir.AxisListType.X, ALU.add))
                step(dve.tensor_tensor(slotf[:, s_], slotf[:, s_], e8[:, :, n_], ALU.add))
                dve.tensor_copy(slot[:, s_], slotf[:, s_]).then_inc(slot_ready, 1)
            dve.wait_ge(texr_full, 1)
            dve.tensor_copy(texp[0:1, :], PD[0][0:1, 0:128]).then_inc(texp_ready, 1)
            dve.wait_ge(exp_ready, 1)
            step(dve.tensor_scalar(gate[:, 32:48], gate[:, 16:32], 1.0, None, ALU.add))
            step(dve.reciprocal(gate[:, 48:64], gate[:, 32:48]))
            step(dve.tensor_tensor(gate[:, 32:48], gate[:, 16:32], gate[:, 48:64], ALU.mult))
            step(dve.tensor_tensor(f3, f3, spread(gate[:, 48:64], 64), ALU.mult))
            step(dve.tensor_tensor(s3, s3, spread(gate[:, 32:48], 64), ALU.mult))
            step(dve.tensor_tensor(comb, first, second, ALU.add))
            dve.sem_inc(comb_ready, 1)

            def outputs(i, s, wait=True):
                dve.wait_ge(yg_full, i * 4 + s + 2)
                if wait:
                    dve.wait_ge(yg_out[s % 2], i * 32 + (s // 2) * 16)
                dve.tensor_copy(yg[:, s % 2, :], PC[s % 2][:, 0:256]).then_inc(yg_ready, 1)
            for s in range(4):
                outputs(0, s, s > 1)
            with dve.Fori(1, GROUPS // 4) as i:
                for s in range(4):
                    outputs(i, s)
            for b in range(4):
                dve.wait_ge(ct_full, b + 1)
                dve.tensor_copy(ct[:, b * 512:(b + 1) * 512], (PB + PC)[b][0:64, :]).then_inc(ct_ready, 1)
            for b in range(2):
                dve.wait_ge(bias_full, b + 1)
                s_ = slice(b * 512, (b + 1) * 512)
                step(dve.tensor_tensor(acc[:, s_], PD[b][:, :], res[:, s_], ALU.add))
            for b in range(2):
                s_ = slice(b * 512, (b + 1) * 512)
                dve.wait_ge(gathered[b], 16 * 16)
                for k, g0 in ((0, 48), (1, 32)):
                    y = grouped(ysel[k][:, s_], 64)
                    step(dve.tensor_tensor(y, y, spread(gate[:, g0 + b * 8:g0 + b * 8 + 8], 64), ALU.mult))
                    step(dve.tensor_tensor(acc[:, s_], acc[:, s_], ysel[k][:, s_], ALU.add))
                dve.sem_inc(sum_ready, 1)

        @block.tensor
        def _(pe):
            pe.wait_ge(images_in, 3 * 16)
            for n in range(B // 2):
                P, full = ((PA, a_full), (PB, b_full))[n // 8]
                mm = pe.matmul(P[(n // 4) % 2][0:64, (n % 4) * 96:(n % 4 + 1) * 96], xin[:, n, :], f1, start=True, stop=True)
                if n % 4 == 3:
                    mm.then_inc(full, 1)
            pe.wait_ge(first_in, NFIRST)
            pe.matmul(PC[0][:, 0:GM], liftg[:, :], gspec, start=True, stop=True).then_inc(c_full, 1)
            pe.wait_ge(a_free, 4)
            pe.wait_ge(b_free, 4)
            for m in range(8):
                for a in range(2):
                    o = a * KX * B + m * 96
                    mm = pe.matmul(PC[1][0:96, m * YF:(m + 1) * YF], xk[:, o:o + 96], f2[:, a, :], start=(a == 0),
                                   stop=(a == 1))
            mm.then_inc(c_full, 1)
            pe.wait_ge(rows_in, 8 * 16)
            for n in range(2 * KG):
                pe.wait_ge(d_free, n + 1)
                pe.matmul(PD[n % 2][:, 0:384], liftx[:, :], xrow[:, n * 384:(n + 1) * 384], start=True,
                          stop=True).then_inc(d_full, 1)
            pe.wait_ge(consts_in, NCONST)
            for n in range(2):
                pe.wait_ge(d_free, 13 + n)
                pe.matmul(PD[n][0:7, 0:64], liftt[:, :], params[:, 0, n * 64:(n + 1) * 64], start=True,
                          stop=True).then_inc(d_full, 1)

            def forward(l):
                fa, fb, fc, fd = A0 + l * AL + AM + AI, B0 + l * BL + BI, C0 + l * CL + CI, D0 + l * DL + DI

                def turn(j, c):
                    pe.wait_ge(v_ready, (l * JN + j) * NC + c + 1)
                    pe.wait_ge(a_free, fa + j * NC + c + 1)
                    for n in range(4):
                        last = pe.transpose(PA[c % 2][:, n * 128:(n + 1) * 128], vch[:, c % 4, n * 128:(n + 1) * 128],
                                            ident[:, :])
                    last.then_inc(a_full, 1)

                def rows(j, c):
                    pe.wait_ge(a_free, fa + j * NC + c + 3)
                    pe.wait_ge(b_free, fb + j * NC + c + 1)
                    for n in reversed(range(4)):
                        last = pe.matmul(PB[c % 2][:, n * 48:n * 48 + 96], vt[:, c % 4, n * 128:(n + 1) * 128], fxy[:, :],
                                         start=True, stop=True)
                    last.then_inc(b_full, 1)
                    pe.wait_ge(a_full, fa + j * NC + c + 1)
                    pe.sem_inc(v_free, 1)

                def columns(j, n, odd):
                    if n == 0:
                        pe.wait_ge(b_free, fb + j * NC + NC + 2)
                    pe.wait_ge(c_free, fc + j * 4 + n + 1)
                    for k in range(3):
                        last = pe.transpose(PC[n % 2][:, k * 128:(k + 1) * 128], cy_[odd][:, (n * 3 + k) * 128:(n * 3 + k + 1) * 128],
                                            ident[:, :])
                    last.then_inc(c_full, 1)

                def spectra(j, h):
                    pe.wait_ge(c_free, fc + j * 4 + 2 * h + 4)
                    pe.wait_ge(d_free, fd + j * 2 + h + 1)
                    for k in range(6):
                        ky = h * 6 + k
                        last = pe.matmul(PD[h][:, k * 48:k * 48 + 96], dx_[:, ky * 128:(ky + 1) * 128], fxy[:, :],
                                         start=True, stop=True)
                    last.then_inc(d_full, 1)

                def group(j, odd, first=False, last=False):
                    for c in range(NC):
                        rows(j, c)
                        if c < NC - 2:
                            turn(j, c + 2)
                        elif not last:
                            turn(j + 1, c - (NC - 2))
                        if c < 4 and not first:
                            columns(j - 1, c, 1 - odd)
                        if c in (4, 5) and not first:
                            spectra(j - 1, c - 4)
                turn(0, 0)
                turn(0, 1)
                group(0, 0, first=True)
                with pe.Fori(0, JN // 2 - 1) as i:
                    group(i * 2 + 1, 1)
                    group(i * 2 + 2, 0)
                group(JN - 1, 1, last=True)
                for n in range(4):
                    columns(JN - 1, n, 1)
                spectra(JN - 1, 0)
                spectra(JN - 1, 1)

            def mixing(l):
                with pe.Fori(0, KG) as k:
                    for h in range(2):
                        n = k * 2 + h
                        pe.wait_ge(exp_dve, (l * MSTEPS + n) * QG + QG)
                        pe.wait_ge(exp_act, (l * MSTEPS + n) * 3 + 3)
                        pe.wait_ge(a_free, A0 + l * AL + n + 1)
                        for m in reversed(range(MK)):
                            o = PA[h][:, m * 64:m * 64 + 96]
                            pe.matmul(o, wring[:, h, 2 * m, :], xslot[:, h, m * 96 + 32:m * 96 + 128], start=True, stop=False)
                            last = pe.matmul(o, wring[:, h, 2 * m + 1, :], xslot[:, h, m * 96:m * 96 + 96], start=False,
                                             stop=True)
                        last.then_inc(a_full, 1)

            def inverse(l, first):
                dbase = D0 + l * DL

                def spectra(j, n):
                    if n == 0:
                        pe.wait_ge(yp_ready, l * JN + j + 1)
                    pe.wait_ge(d_free, dbase + j * 6 + n + 1)
                    for k in range(3):
                        last = pe.transpose(PD[n][0:96, k * 128:(k + 1) * 128], yp[:, (n * 3 + k) * 96:(n * 3 + k + 1) * 96], ident[:, :])
                    last.then_inc(d_full, 1)

                def columns(j, p):
                    pe.wait_ge(d_free, dbase + j * 6 + p // 3 + 3)
                    pe.wait_ge(c_free, C0 + l * CL + j * 6 + p + 1)
                    pe.matmul(PC[p % 2][:, 0:256], yt[:, p * 128:(p + 1) * 128], tx[:, :], start=True,
                              stop=True).then_inc(c_full, 1)

                def turn(j, s):
                    pe.wait_ge(c_free, C0 + l * CL + j * 6 + 8)
                    pe.wait_ge(d_free, dbase + j * 6 + 2 + s + 1)
                    for k in range(4):
                        g = s * 4 + k
                        last = pe.transpose(PD[s % 2][0:96, k * 128:(k + 1) * 128], z1[:, g * 96:(g + 1) * 96], ident[:, :])
                    last.then_inc(d_full, 1)

                def conv(j, c):
                    free, P, base = ((a_free, PA, A0 + l * AL + AM), (b_free, PB, B0 + l * BL))[c % 2]
                    pe.wait_ge(free, base + j * 4 + c // 2 + 1)
                    if not first:
                        pe.matmul(P[c // 2 % 2][:, :], cur[:, 0:128], big[:, j, c * CW:(c + 1) * CW], start=True, stop=False)

                def rows(j, c, ahead=False):
                    full, P = ((a_full, PA), (b_full, PB))[c % 2]
                    s = c // 2
                    if not ahead:
                        conv(j, c)
                    pe.wait_ge(d_free, dbase + j * 6 + 2 + s + 3)
                    o = P[s % 2]
                    if first and c % 2 == 0:
                        pe.wait_ge(pix_in[s % 2], j * 64 + (s // 2) * 32 + 32)
                    for k in range(2):
                        t = (c % 2) * 2 + k
                        half = o[:, k * 256:(k + 1) * 256]
                        if first:
                            last = pe.matmul(half, z1mix[:, s, t * 128:(t + 1) * 128],
                                             typix[:, s % 2, t * 256:(t + 1) * 256], start=(k == 0), stop=(k == 1))
                        else:
                            last = pe.matmul(half, z1t[:, s, t * 128:(t + 1) * 128], ty[:, :], start=False, stop=(k == 1))
                    last.then_inc(full, 1)

                def group(j, last=False, ahead=False):
                    for c in range(NC):
                        rows(j, c, ahead and c < 4)
                        if c < 2:
                            turn(j, c + 2)
                        if last:
                            continue
                        if c == 2:
                            spectra(j + 1, 0)
                            spectra(j + 1, 1)
                        if c >= 3 and c < 6:
                            columns(j + 1, 2 * (c - 3))
                            columns(j + 1, 2 * (c - 3) + 1)
                        if c == 6:
                            turn(j + 1, 0)
                            turn(j + 1, 1)

                pe.wait_ge(cur_ready, l + 1)
                if first:
                    pe.wait_ge(lmix_ready, 2)
                else:
                    pe.wait_ge(v_copied, l * JN * NC + 4)
                    for c in range(4):
                        conv(0, c)
                spectra(0, 0)
                spectra(0, 1)
                for p in range(6):
                    columns(0, p)
                turn(0, 0)
                turn(0, 1)
                group(0, ahead=not first)
                with pe.Fori(1, JN - 1) as j:
                    group(j)
                group(JN - 1, last=True)

            def norm(l):
                pe.wait_ge(bn_mm, l * 4 + 1)
                pe.matmul(PD[0][:, 0:1], avg[:, :], bn[:, 0:1], start=True, stop=True).then_inc(bn_mm, 1)
                pe.wait_ge(bn_mm, l * 4 + 3)
                pe.matmul(PD[0][:, 1:2], avg[:, :], bn[:, 3:4], start=True, stop=True).then_inc(bn_mm, 1)

            mixing(0)
            inverse(0, True)
            norm(0)
            forward(0)
            with pe.Fori(1, LAYERS - 1) as l:
                mixing(l)
                inverse(l, False)
                norm(l)
                forward(l)
            mixing(LAYERS - 1)
            inverse(LAYERS - 1, False)
            norm(LAYERS - 1)
            pe.wait_ge(q_prep, 2)
            b0 = B0 + LAYERS * BL - BF
            pe.matmul(PD[0][:, 2:3], shift, qcol[:, 0:1], start=True, stop=True).then_inc(q_prep, 1)
            for j in range(JN):
                for c in range(NC):
                    if c % 4 == 0:
                        pe.wait_ge(b_free, j * 2 + b0 + c // 4 + 1)
                    r = (c % 4) * 32
                    pe.matmul(PB[c // 4][r:r + 32, :], qscaled[:, :], big[:, j, c * CW:(c + 1) * CW], start=True,
                              stop=True).then_inc(v_free, 1)

            pe.wait_ge(b_free, B0 + LAYERS * BL - BF + JN * 2 + 2)
            def tokens_to_columns(src, banks_, full):
                for t in range(TT):
                    last = pe.transpose(banks_[t // 4][0:64, (t % 4) * 128:(t % 4 + 1) * 128], src[:, t * 64:(t + 1) * 64],
                                        ident[:, :])
                    if t % 4 == 3:
                        last.then_inc(full, 1)

            pe.wait_ge(xn_ready, 1)
            tokens_to_columns(xn, PB + PC, xt_full)
            pe.wait_ge(tail_in, 15 * 16)
            pe.wait_ge(ones_set, 2)
            pe.wait_ge(xt_ready, 4)
            for t in range(TT):
                last = pe.matmul((PA + PB)[t // 4][:, (t % 4) * 128:(t % 4 + 1) * 128], xt[:, t * 128:(t + 1) * 128],
                                 wqkv[:, 64:192], start=True, stop=True)
                if t % 4 == 3:
                    last.then_inc(kv_full, 1)
            for b in range(4):
                pe.matmul((PC + PD)[b][0:64, :], wqkv[:, 0:64], xt[:, b * 512:(b + 1) * 512], start=True,
                          stop=True).then_inc(q_full, 1)
            for h in range(2):
                pe.wait_ge(kv_ready, h + 1)
                for q in range(QG):
                    r = slice(q * 32, (q + 1) * 32)
                    for j in range(h * 4, h * 4 + 4):
                        for x2 in range(2):
                            o = (j * 2 + x2) * 128
                            last = pe.matmul((PA + PB)[q][0:64, j * 64:(j + 1) * 64], kv[r, o:o + 64],
                                             kv[r, o + 64:o + 128], start=(x2 == 0), stop=(x2 == 1))
                    if h == 1:
                        last.then_inc(kvm_full, 1)
            pe.wait_ge(kvm_ready, 1)
            pe.wait_ge(qt_ready, 4)
            for j in range(JN):
                for q in range(QG):
                    qv = qt[:, j * 256:(j + 1) * 256].rearrange("p (x n) -> p x n", x=2)[:, :, q * 32:(q + 1) * 32]
                    o = (PC + PD)[j // 2][0:64, (j % 2) * 256:(j % 2 + 1) * 256]
                    last = pe.matmul(o.rearrange("p (x n) -> p x n", x=2)[:, :, q * 32:(q + 1) * 32],
                                     kvm[:, q * 512 + j * 64:q * 512 + (j + 1) * 64], qv, start=True, stop=True)
                if j % 2 == 1:
                    last.then_inc(att_full, 1)
            for t in range(TT):
                if t % 4 == 0:
                    pe.wait_ge(rt_ready, t // 4 + 1)
                last = pe.matmul(PA[t // 8][:, (t % 8) * 64:(t % 8 + 1) * 64], rt[:, t * 128:(t + 1) * 128], wproj[:, :],
                                 start=True, stop=True)
                if t % 8 == 7:
                    last.then_inc(proj_full, 1)
            pe.wait_ge(xn_ready, 2)
            tokens_to_columns(xn, PB + PC, xt_full)
            pe.wait_ge(xt_ready, 8)
            for t in range(TT):
                last = pe.matmul(PA[t // 8][:, (t % 8) * 64:(t % 8 + 1) * 64], xt[:, t * 128:(t + 1) * 128], wroute[:, :],
                                 start=True, stop=True)
                if t % 8 == 7:
                    last.then_inc(lg_full, 1)
            pe.wait_ge(chosen_ready, 1)
            pe.wait_ge(ones_set, 8)
            for b in range(2):
                pe.matmul(PC[b][:, :], ones_m[:, :], chosen[:, b * 512:(b + 1) * 512], start=True, stop=True)
            for b in range(2):
                last = pe.matmul(PB[b][:, :], tri16[:, :], chosen[:, b * 512:(b + 1) * 512], start=True, stop=True)
            last.then_inc(tot_full, 1)
            pe.wait_ge(texf_ready, 1)
            pe.matmul(PD[0][0:1, 0:128], texf[:, 0:1], ident[:, :], start=True, stop=True).then_inc(texr_full, 1)

            def turn(i, s):
                pe.wait_ge(xg_in[s], i * 16 + 16)
                pe.sem_inc(pe_past, 1)
                for k in range(4):
                    last = pe.transpose(PA[s % 2][0:64, k * 128:(k + 1) * 128], xg[:, s, k * 64:(k + 1) * 64], ident[:, :])
                last.then_inc(xg_turned, 1)

            def hidden(i, s, further=False):
                if further:
                    pe.wait_ge(wd_in[s], (i - EXPERTS // 16) * 64 + 64)
                else:
                    pe.wait_ge(wt_in[s], i * 16 + 16)
                pe.wait_ge(xgt_ready, i * 4 + s + 1)
                for k in range(4):
                    last = pe.matmul(PB[s % 2][:, k * 128:(k + 1) * 128], wt[:, s, k, 64:192],
                                     xgt[:, s % 2, k * 128:(k + 1) * 128], start=True, stop=True)
                last.then_inc(hid_full, 1)

            def outputs(i, s):
                pe.wait_ge(hid_ready, i * 4 + s + 2)
                pe.wait_ge(yg_ready, i * 4 + s + 1)
                for k in range(4):
                    last = pe.matmul(PC[s % 2][:, k * 64:(k + 1) * 64], hid[:, s % 2, k * 128:(k + 1) * 128],
                                     wt[:, s, k, 0:64], start=True, stop=True)
                last.then_inc(yg_full, 1)

            def group(i, s, further=False, last=False):
                if s < 2 or not last:
                    pe.wait_ge(xgt_ready, i * 4 + s + 1)
                    turn(i + (s + 2) // 4, (s + 2) % 4)
                if s < 3 or not last:
                    pe.wait_ge(hid_ready, i * 4 + s + 1)
                    hidden(i + (s + 1) // 4, (s + 1) % 4, further)
                outputs(i, s)
            turn(0, 0)
            turn(0, 1)
            hidden(0, 0)
            with pe.Fori(0, EXPERTS // 16 - 1) as i:
                for s in range(4):
                    group(i, s)
            for s in range(4):
                group(EXPERTS // 16 - 1, s, s == 3)
            with pe.Fori(EXPERTS // 16, GROUPS // 4 - 1) as i:
                for s in range(4):
                    group(i, s, True)
            for s in range(4):
                group(GROUPS // 4 - 1, s, True, True)
            pe.wait_ge(comb_ready, 1)
            pe.wait_ge(yg_ready, GROUPS + 2)
            tokens_to_columns(comb, PB + PC, ct_full)
            pe.wait_ge(ct_ready, 4)
            for t in range(TT):
                last = pe.matmul(PD[t // 8][:, (t % 8) * 64:(t % 8 + 1) * 64], ct[:, t * 128:(t + 1) * 128], b2all[:, :],
                                 start=True, stop=True)
                if t % 8 == 7:
                    last.then_inc(bias_full, 1)


_INS = ['x', 'L0_tok_p_w', 'L0_tok_p_b', 'L0_tok_fw1', 'L0_tok_fw2', 'L0_tok_w_w', 'L0_tok_w_b', 'L0_tok_bn_g',
        'L0_tok_bn_b', 'L0_tok_q_w', 'L0_tok_q_b', 'L0_attn_W_qkv', 'L0_attn_b_qkv', 'L0_attn_kln_w', 'L0_attn_kln_b',
        'L0_attn_vln_w', 'L0_attn_vln_b', 'L0_attn_W_proj', 'L0_attn_b_proj', 'L0_ffn_Wr', 'L0_ffn_br', 'L0_ffn_W1',
        'L0_ffn_b1', 'L0_ffn_W2', 'L0_ffn_b2']


def kernel(**inputs):
    import concourse.bacc as _bacc
    from concourse import mybir as _mybir
    from concourse.bass_utils import run_bass_kernel_spmd as _run

    nc = _bacc.Bacc("TRN2", target_bir_lowering=False, num_devices=1)
    arrays, args = {}, []

    def give(name, a):
        arrays[name] = a
        args.append(nc.dram_tensor(name, a.shape, _mybir.dt.from_np(a.dtype), kind="ExternalInput").ap())

    for name in _INS:
        a = np.ascontiguousarray(inputs[name])
        if name in ('L0_tok_p_b', 'L0_tok_w_b', 'L0_tok_bn_b'):
            continue
        if name == 'L0_tok_p_w':
            a = np.concatenate([a, np.asarray(inputs['L0_tok_p_b'])[None]])
        if name == 'L0_tok_bn_g':
            a = np.stack([np.asarray(inputs['L0_tok_w_b']), a, np.asarray(inputs['L0_tok_bn_b'])], axis=-1)
        if name in ('L0_tok_fw1', 'L0_tok_fw2'):
            a = a.reshape(LAYERS, CH, CH, 12 * KY * 2)
        if name == 'L0_attn_W_qkv':
            a = np.ascontiguousarray(a.reshape(16, 3, 4, 64).transpose(3, 1, 0, 2).reshape(64, 192))
        if name == 'L0_attn_b_qkv':
            a = np.ascontiguousarray(a.reshape(16, 3, 4).transpose(1, 0, 2).reshape(192))
        if name == 'L0_attn_W_proj':
            a = np.ascontiguousarray(a.T)
        if name in ('L0_ffn_b1', 'L0_ffn_W2'):
            continue
        if name == 'L0_ffn_W1':
            w = np.zeros((EXPERTS, 128, 192), a.dtype)
            w[:, :, 0:64], w[:, 0:64, 64:192] = np.asarray(inputs['L0_ffn_W2']), a
            w[:, 64, 64:192], a = np.asarray(inputs['L0_ffn_b1']), w
        give("in_" + name, a)
    for name, a in constants().items():
        give("const_" + name, a)
    for name in ("slots_x", "slots_y"):
        args.append(nc.dram_tensor(name, (SLOT_TILES * 128, 64), _mybir.dt.float32, kind="Internal").ap())
    args.append(nc.dram_tensor("pixels_out", (B, NPIX), _mybir.dt.float32, kind="Internal").ap())
    args.append(nc.dram_tensor("spectra_x", (JN, QG * CH, QG * GM), _mybir.dt.float32, kind="Internal").ap())
    args.append(nc.dram_tensor("spectra_y", (JN, QG * CH, QG, GM), _mybir.dt.float32, kind="Internal").ap())
    args.append(nc.dram_tensor("out_0", (B, S, S), _mybir.dt.float32, kind="ExternalOutput").ap())
    vit_tower(nc, *args)
    r = _run(nc, [arrays], core_ids=[0])
    return r.results[0]["out_0"]
```
